# Optimizing a Trainium2 kernel written in Bass

```python
import numpy as np
import jax
import jax.numpy as jnp

def _softmax(x, axis=-1):
    return jax.nn.softmax(x, axis=axis)

def _gelu(x):
    return jax.nn.gelu(x, approximate=True)

def _silu(x):
    return jax.nn.silu(x)

def _sigmoid(x):
    return jax.nn.sigmoid(x)

def _layernorm(x, axis=-1, eps=1e-05):
    m = jnp.mean(x, axis=axis, keepdims=True)
    v = jnp.var(x, axis=axis, keepdims=True)
    return (x - m) / jnp.sqrt(v + eps)

def _scatter_add(tgt, idx, src, axis=0):
    return tgt.at[idx].add(src)

def _segment_sum(src, seg, n):
    return jax.ops.segment_sum(src, seg, n)
kernel_name = 'mk_vit_tower_d2_tok_img768_r4_1c9512'

def setup_inputs(seed: int=0):
    np.random.seed(seed)
    _w = jnp.asarray

    def _rec_inputs():
        import jax
        import jax.numpy as jnp
        _rk = jax.random.key(seed)
        x = -0.00016672 + 0.999947 * jax.random.normal(jax.random.fold_in(_rk, 1), (16, 3, 96, 96), jnp.float32)
        return x
    x = _rec_inputs()

    def _L0_tok_setup():
        import jax, jax.numpy as jnp
        import numpy as np
        PATCH = 16
        key = jax.random.key(seed)
        kx, kw, kb = jax.random.split(key, 3)
        B, C, H, W = (64, 3, 96, 96)
        n_embd = 192
        Cpp = C * PATCH * PATCH
        x = jax.random.normal(kx, (B, C, H, W), dtype=jnp.float32)
        bound = 1.0 / np.sqrt(Cpp)
        W_proj = jax.random.uniform(kw, (n_embd, Cpp), dtype=jnp.float32, minval=-bound, maxval=bound)
        b_proj = jax.random.uniform(kb, (n_embd,), dtype=jnp.float32, minval=-bound, maxval=bound)
        return {'x': x, 'W_proj': W_proj, 'b_proj': b_proj}
    _L0_tok_all = _L0_tok_setup()
    _L0_tok_in = {k: v for k, v in _L0_tok_all.items() if k in ('W_proj', 'b_proj')}
    del _L0_tok_all

    def _L0_attn_setup():
        import jax, jax.numpy as jnp
        import numpy as np
        NPATCH = 64
        NWINDOW = 32
        HEADS = 12
        DIM_HEAD = 64
        LN_EPS = 1e-05
        key = jax.random.key(seed)
        k1, k2, k3 = jax.random.split(key, 3)
        b, n, dim = (2, NPATCH * NWINDOW, 192)
        inner = HEADS * DIM_HEAD
        return {'x': jax.random.normal(k1, (b, n, dim), dtype=jnp.float32), 'gamma': jnp.ones((dim,), jnp.float32), 'beta': jnp.zeros((dim,), jnp.float32), 'w_qkv': jax.random.normal(k2, (dim, 3 * inner), dtype=jnp.float32) * dim ** (-0.5), 'w_out': jax.random.normal(k3, (inner, dim), dtype=jnp.float32) * inner ** (-0.5), 'b_out': jnp.zeros((dim,), jnp.float32)}
    _L0_attn_all = _L0_attn_setup()
    _L0_attn_in = {k: v for k, v in _L0_attn_all.items() if k in ('gamma', 'beta', 'w_qkv', 'w_out', 'b_out')}
    del _L0_attn_all

    def _L0_ffn_setup():
        import jax, jax.numpy as jnp
        import numpy as np
        EPS_NORM = 1e-06
        EPS_Q = 1e-05

        def rmsnorm(x, g):
            return x * jax.lax.rsqrt(jnp.mean(x * x, axis=-1, keepdims=True) + EPS_NORM) * g

        def activation_quant(x):
            scale = 127.0 / jnp.maximum(jnp.max(jnp.abs(x), axis=-1, keepdims=True), EPS_Q)
            return jnp.clip(jnp.round(x * scale), -128, 127) / scale

        def weight_quant(w):
            scale = 1.0 / jnp.maximum(jnp.mean(jnp.abs(w)), EPS_Q)
            return jnp.clip(jnp.round(w * scale), -1, 1) / scale

        def bitlinear(x, w, g):
            x_norm = rmsnorm(x, g)
            x_q = x_norm + jax.lax.stop_gradient(activation_quant(x_norm) - x_norm)
            w_q = w + jax.lax.stop_gradient(weight_quant(w) - w)
            return jnp.einsum('bsd,od->bso', x_q, w_q)
        key = jax.random.key(seed)
        k1, k2, k3 = jax.random.split(key, 3)
        B, S, D, H = (8, 1024, 192, 512)
        x = jax.random.normal(k1, (B, S, D), dtype=jnp.float32)
        w_in = jax.random.normal(k2, (2 * H, D), dtype=jnp.float32) * 0.002
        w_out = jax.random.normal(k3, (D, H), dtype=jnp.float32) * 0.002
        g_in = jnp.ones((D,), dtype=jnp.float32)
        g_out = jnp.ones((H,), dtype=jnp.float32)
        return {'x': x, 'w_in': w_in, 'g_in': g_in, 'w_out': w_out, 'g_out': g_out}
    _L0_ffn_all = _L0_ffn_setup()
    _L0_ffn_in = {k: v for k, v in _L0_ffn_all.items() if k in ('w_in', 'g_in', 'w_out', 'g_out')}
    del _L0_ffn_all

    def _L1_attn_setup():
        import jax, jax.numpy as jnp
        import numpy as np
        DIM = 192
        H = 12
        HD = DIM // H
        TTT_BASE_LR = 1.0
        EPS = 1e-06

        def ln_fwd(x, gamma, beta):
            mu = jnp.mean(x, axis=-1, keepdims=True)
            var = jnp.mean((x - mu) ** 2, axis=-1, keepdims=True)
            x_hat = (x - mu) / jnp.sqrt(var + EPS)
            return gamma * x_hat + beta

        def ln_fused_l2_bwd(x, l2_target, gamma, beta):
            D = x.shape[-1]
            mu = jnp.mean(x, axis=-1, keepdims=True)
            var = jnp.mean((x - mu) ** 2, axis=-1, keepdims=True)
            std = jnp.sqrt(var + EPS)
            x_hat = (x - mu) / std
            y = gamma * x_hat + beta
            grad_out = y - l2_target
            g = grad_out * gamma
            z = (D * g - jnp.sum(g, -1, keepdims=True) - x_hat * jnp.sum(g * x_hat, -1, keepdims=True)) / (D * std)
            return z
        key = jax.random.key(seed)
        ks = jax.random.split(key, 10)
        B, N, C = (16, 256, DIM)
        return {'x': jax.random.normal(ks[0], (B, N, C), jnp.float32), 'qkv_weight': jax.random.normal(ks[1], (3 * C, C), jnp.float32) * 0.02, 'q_bias': jnp.zeros((C,), jnp.float32), 'v_bias': jnp.zeros((C,), jnp.float32), 'proj_weight': jax.random.normal(ks[2], (C, C), jnp.float32) * 0.02, 'proj_bias': jnp.zeros((C,), jnp.float32), 'ttt_lr_weight': jax.random.normal(ks[3], (H, 1, C), jnp.float32) * 0.02, 'ttt_lr_bias': jnp.zeros((H, 1), jnp.float32), 'ttt_norm_weight': jnp.ones((H, HD), jnp.float32), 'ttt_norm_bias': jnp.zeros((H, HD), jnp.float32), 'W1': jax.random.normal(ks[4], (H, HD, HD), jnp.float32) * 0.02, 'b1': jnp.zeros((H, 1, HD), jnp.float32)}
    _L1_attn_all = _L1_attn_setup()
    _L1_attn_in = {k: v for k, v in _L1_attn_all.items() if k in ('qkv_weight', 'q_bias', 'v_bias', 'proj_weight', 'proj_bias', 'ttt_lr_weight', 'ttt_lr_bias', 'ttt_norm_weight', 'ttt_norm_bias', 'W1', 'b1')}
    del _L1_attn_all

    def _L1_ffn_setup():
        import jax, jax.numpy as jnp
        import numpy as np
        import math
        B, S, D = (4, 1024, 192)
        E = 8
        TOP_K = 2
        H = 512
        CAP_F = 1.25
        EPS = 1e-06
        ALPHA = 1.0
        key = jax.random.key(seed)
        k0, k1, k2, k3 = jax.random.split(key, 4)
        x = jax.random.normal(k0, (B, S, D), jnp.float32)
        gate_w = jax.random.normal(k1, (E, D), jnp.float32) * 0.02
        w13 = jax.random.normal(k2, (E, 2 * H, D), jnp.float32) * 0.02
        w2 = jax.random.normal(k3, (E, D, H), jnp.float32) * 0.02
        norm_w = jnp.ones((E, D), jnp.float32)
        return {'x': x, 'gate_w': gate_w, 'w13': w13, 'w2': w2, 'norm_w': norm_w}
    _L1_ffn_all = _L1_ffn_setup()
    _L1_ffn_in = {k: v for k, v in _L1_ffn_all.items() if k in ('gate_w', 'w13', 'w2', 'norm_w')}
    del _L1_ffn_all
    return {'x': x, 'L0_tok_W_proj': _L0_tok_in['W_proj'], 'L0_tok_b_proj': _L0_tok_in['b_proj'], 'L0_attn_gamma': _L0_attn_in['gamma'], 'L0_attn_beta': _L0_attn_in['beta'], 'L0_attn_w_qkv': _L0_attn_in['w_qkv'], 'L0_attn_w_out': _L0_attn_in['w_out'], 'L0_attn_b_out': _L0_attn_in['b_out'], 'L0_ffn_w_in': _L0_ffn_in['w_in'], 'L0_ffn_g_in': _L0_ffn_in['g_in'], 'L0_ffn_w_out': _L0_ffn_in['w_out'], 'L0_ffn_g_out': _L0_ffn_in['g_out'], 'L1_attn_qkv_weight': _L1_attn_in['qkv_weight'], 'L1_attn_q_bias': _L1_attn_in['q_bias'], 'L1_attn_v_bias': _L1_attn_in['v_bias'], 'L1_attn_proj_weight': _L1_attn_in['proj_weight'], 'L1_attn_proj_bias': _L1_attn_in['proj_bias'], 'L1_attn_ttt_lr_weight': _L1_attn_in['ttt_lr_weight'], 'L1_attn_ttt_lr_bias': _L1_attn_in['ttt_lr_bias'], 'L1_attn_ttt_norm_weight': _L1_attn_in['ttt_norm_weight'], 'L1_attn_ttt_norm_bias': _L1_attn_in['ttt_norm_bias'], 'L1_attn_W1': _L1_attn_in['W1'], 'L1_attn_b1': _L1_attn_in['b1'], 'L1_ffn_gate_w': _L1_ffn_in['gate_w'], 'L1_ffn_w13': _L1_ffn_in['w13'], 'L1_ffn_w2': _L1_ffn_in['w2'], 'L1_ffn_norm_w': _L1_ffn_in['norm_w']}

def reference(x, L0_tok_W_proj, L0_tok_b_proj, L0_attn_gamma, L0_attn_beta, L0_attn_w_qkv, L0_attn_w_out, L0_attn_b_out, L0_ffn_w_in, L0_ffn_g_in, L0_ffn_w_out, L0_ffn_g_out, L1_attn_qkv_weight, L1_attn_q_bias, L1_attn_v_bias, L1_attn_proj_weight, L1_attn_proj_bias, L1_attn_ttt_lr_weight, L1_attn_ttt_lr_bias, L1_attn_ttt_norm_weight, L1_attn_ttt_norm_bias, L1_attn_W1, L1_attn_b1, L1_ffn_gate_w, L1_ffn_w13, L1_ffn_w2, L1_ffn_norm_w):
    import jax
    import jax.numpy as jnp

    def _L0_tok_ref(x, W_proj, b_proj):
        import jax, jax.numpy as jnp
        import numpy as np
        PATCH = 16
        B, C, H, W = x.shape
        p = PATCH
        x = x.reshape(B, C, H // p, p, W // p, p)
        patches = jnp.transpose(x, (0, 2, 4, 1, 3, 5))
        patches = patches.reshape(B, H // p * (W // p), C * p * p)
        out = jnp.einsum('bnc,ec->bne', patches, W_proj) + b_proj
        return out

    def _L0_attn_ref(x, gamma, beta, w_qkv, w_out, b_out):
        import jax, jax.numpy as jnp
        import numpy as np
        NPATCH = 64
        NWINDOW = 32
        HEADS = 12
        DIM_HEAD = 64
        LN_EPS = 1e-05
        b, n, dim = x.shape
        mu = jnp.mean(x, axis=-1, keepdims=True)
        var = jnp.mean(jnp.square(x - mu), axis=-1, keepdims=True)
        xn = (x - mu) * jax.lax.rsqrt(var + LN_EPS) * gamma + beta
        qkv = xn @ w_qkv
        q, k, v = jnp.split(qkv, 3, axis=-1)

        def to_heads(t):
            return t.reshape(b, n, HEADS, DIM_HEAD).transpose(0, 2, 1, 3)
        q, k, v = (to_heads(q), to_heads(k), to_heads(v))
        scale = DIM_HEAD ** (-0.5)
        dots = jnp.einsum('bhid,bhjd->bhij', q, k) * scale
        blk = jnp.arange(n) // NPATCH
        mask = blk[:, None] >= blk[None, :]
        dots = jnp.where(mask[None, None], dots, -jnp.inf)
        attn = jax.nn.softmax(dots, axis=-1)
        out = jnp.einsum('bhij,bhjd->bhid', attn, v)
        out = out.transpose(0, 2, 1, 3).reshape(b, n, HEADS * DIM_HEAD)
        return out @ w_out + b_out

    def _L0_ffn_ref(x, w_in, g_in, w_out, g_out):
        import jax, jax.numpy as jnp
        import numpy as np
        EPS_NORM = 1e-06
        EPS_Q = 1e-05

        def rmsnorm(x, g):
            return x * jax.lax.rsqrt(jnp.mean(x * x, axis=-1, keepdims=True) + EPS_NORM) * g

        def activation_quant(x):
            scale = 127.0 / jnp.maximum(jnp.max(jnp.abs(x), axis=-1, keepdims=True), EPS_Q)
            return jnp.clip(jnp.round(x * scale), -128, 127) / scale

        def weight_quant(w):
            scale = 1.0 / jnp.maximum(jnp.mean(jnp.abs(w)), EPS_Q)
            return jnp.clip(jnp.round(w * scale), -1, 1) / scale

        def bitlinear(x, w, g):
            x_norm = rmsnorm(x, g)
            x_q = x_norm + jax.lax.stop_gradient(activation_quant(x_norm) - x_norm)
            w_q = w + jax.lax.stop_gradient(weight_quant(w) - w)
            return jnp.einsum('bsd,od->bso', x_q, w_q)
        h = bitlinear(x, w_in, g_in)
        up, gate = jnp.split(h, 2, axis=-1)
        y = jax.nn.silu(gate) * up
        return bitlinear(y, w_out, g_out)

    def _L1_attn_ref(x, qkv_weight, q_bias, v_bias, proj_weight, proj_bias, ttt_lr_weight, ttt_lr_bias, ttt_norm_weight, ttt_norm_bias, W1, b1):
        import jax, jax.numpy as jnp
        import numpy as np
        DIM = 192
        H = 12
        HD = DIM // H
        TTT_BASE_LR = 1.0
        EPS = 1e-06

        def ln_fwd(x, gamma, beta):
            mu = jnp.mean(x, axis=-1, keepdims=True)
            var = jnp.mean((x - mu) ** 2, axis=-1, keepdims=True)
            x_hat = (x - mu) / jnp.sqrt(var + EPS)
            return gamma * x_hat + beta

        def ln_fused_l2_bwd(x, l2_target, gamma, beta):
            D = x.shape[-1]
            mu = jnp.mean(x, axis=-1, keepdims=True)
            var = jnp.mean((x - mu) ** 2, axis=-1, keepdims=True)
            std = jnp.sqrt(var + EPS)
            x_hat = (x - mu) / std
            y = gamma * x_hat + beta
            grad_out = y - l2_target
            g = grad_out * gamma
            z = (D * g - jnp.sum(g, -1, keepdims=True) - x_hat * jnp.sum(g * x_hat, -1, keepdims=True)) / (D * std)
            return z
        B, N, C = x.shape
        num_mini_batch = 1
        m = N // num_mini_batch
        qkv_bias = jnp.concatenate([q_bias, jnp.zeros_like(q_bias), v_bias])
        qkv = x @ qkv_weight.T + qkv_bias
        qkv = qkv.reshape(B, N, 3, H, HD).transpose(2, 0, 3, 1, 4)
        q, k, v = (qkv[0], qkv[1], qkv[2])
        ttt_lr = jnp.einsum('bnc,hdc->bhnd', x, ttt_lr_weight) + ttt_lr_bias.reshape(1, H, 1, 1)
        ttt_lr_eta = TTT_BASE_LR * jax.nn.sigmoid(ttt_lr) / HD
        gamma = ttt_norm_weight.reshape(H, 1, HD)
        beta = ttt_norm_bias.reshape(H, 1, HD)

        def compute_mini_batch(carry, inp):
            W1c, b1c = carry
            XQ, XK, XV, eta = inp
            Z1 = XK @ W1c + b1c
            g = ln_fused_l2_bwd(Z1, XV - XK, gamma, beta)
            g = g * eta / m
            grad_W1 = jnp.einsum('bhmd,bhme->bhde', XK, g)
            grad_b1 = jnp.sum(g, axis=2, keepdims=True)
            W1n = W1c - grad_W1
            b1n = b1c - grad_b1
            Z1_bar = ln_fwd(XQ @ W1n + b1n, gamma, beta)
            return ((W1n, b1n), XQ + Z1_bar)

        def to_scan(t):
            return t.reshape(B, H, num_mini_batch, m, t.shape[-1]).transpose(2, 0, 1, 3, 4)
        xs = (to_scan(q), to_scan(k), to_scan(v), to_scan(ttt_lr_eta))
        init = (jnp.broadcast_to(W1, (B, H, HD, HD)), jnp.broadcast_to(b1, (B, H, 1, HD)))
        _, XQW = jax.lax.scan(compute_mini_batch, init, xs)
        out = XQW.transpose(1, 2, 0, 3, 4).reshape(B, H, N, HD)
        out = out.transpose(0, 2, 1, 3).reshape(B, N, C)
        out = out @ proj_weight.T + proj_bias
        return out

    def _L1_ffn_ref(x, gate_w, w13, w2, norm_w):
        import jax, jax.numpy as jnp
        import numpy as np
        import math
        B, S, D = (4, 1024, 192)
        E = 8
        TOP_K = 2
        H = 512
        CAP_F = 1.25
        EPS = 1e-06
        ALPHA = 1.0
        Bx, Sx, Dx = x.shape
        N = Bx * Sx
        cap = int(math.ceil(CAP_F * TOP_K * N / E))
        xf = x.reshape(N, Dx)
        logits = xf.astype(jnp.float32) @ gate_w.T
        probs = jax.nn.softmax(logits, axis=-1)
        top_p, top_i = jax.lax.top_k(probs, TOP_K)
        w = top_p / jnp.sum(top_p, axis=-1, keepdims=True)
        flat_e = top_i.reshape(-1)
        onehot = jax.nn.one_hot(flat_e, E, dtype=jnp.int32)
        pos = jnp.take_along_axis(jnp.cumsum(onehot, axis=0) - 1, flat_e[:, None], axis=1)[:, 0]
        keep = pos < cap
        didx = flat_e * cap + jnp.minimum(pos, cap - 1)
        safe = jnp.where(keep, didx, E * cap)
        x_rep = jnp.repeat(xf, TOP_K, axis=0)
        buf = jnp.zeros((E * cap + 1, Dx), x.dtype).at[safe].set(x_rep)
        buf = buf[:-1].reshape(E, cap, Dx)
        z = 2.0 * buf
        z = z * jax.lax.rsqrt(jnp.mean(z * z, axis=-1, keepdims=True) + EPS)
        z = z * norm_w[:, None, :]
        gu = jnp.einsum('ecd,ehd->ech', z, w13)
        g, u = jnp.split(gu, 2, axis=-1)
        y = buf + ALPHA * jnp.einsum('ech,edh->ecd', jax.nn.silu(g) * u, w2)
        y_tok = y.reshape(E * cap, Dx)[didx]
        cw = (w.reshape(-1) * keep.astype(w.dtype)).astype(x.dtype)
        out = (cw[:, None] * y_tok).reshape(N, TOP_K, Dx).sum(axis=1)
        return out.reshape(Bx, Sx, Dx)
    h = _L0_tok_ref(x, L0_tok_W_proj, L0_tok_b_proj)
    h = h + _L0_attn_ref(_layernorm(h, axis=-1), L0_attn_gamma, L0_attn_beta, L0_attn_w_qkv, L0_attn_w_out, L0_attn_b_out)
    h = h + _L0_ffn_ref(_layernorm(h, axis=-1), L0_ffn_w_in, L0_ffn_g_in, L0_ffn_w_out, L0_ffn_g_out)
    h = h + _L1_attn_ref(_layernorm(h, axis=-1), L1_attn_qkv_weight, L1_attn_q_bias, L1_attn_v_bias, L1_attn_proj_weight, L1_attn_proj_bias, L1_attn_ttt_lr_weight, L1_attn_ttt_lr_bias, L1_attn_ttt_norm_weight, L1_attn_ttt_norm_bias, L1_attn_W1, L1_attn_b1)
    h = h + _L1_ffn_ref(_layernorm(h, axis=-1), L1_ffn_gate_w, L1_ffn_w13, L1_ffn_w2, L1_ffn_norm_w)
    return h

_drawn_inputs = setup_inputs


def setup_inputs(seed=0):
    import zlib

    import numpy as np

    out = dict(_drawn_inputs(seed))
    spreads = {'L0_attn_gamma': (1.0, 0.2),
     'L0_attn_beta': (0.0, 0.1),
     'L0_attn_b_out': (0.0, 0.1),
     'L0_ffn_g_in': (1.0, 0.6),
     'L0_ffn_g_out': (1.0, 0.6),
     'L1_attn_q_bias': (0.0, 0.1),
     'L1_attn_v_bias': (0.0, 0.1),
     'L1_attn_proj_bias': (0.0, 0.1),
     'L1_attn_ttt_lr_bias': (0.0, 0.529),
     'L1_attn_ttt_norm_weight': (1.0, 0.2),
     'L1_attn_ttt_norm_bias': (0.0, 0.1),
     'L1_attn_b1': (0.0, 0.1),
     'L1_ffn_norm_w': (1.0, 0.6)}
    factors = {'L0_ffn_w_in': 3.498, 'L0_ffn_w_out': 3.165, 'L1_ffn_w13': 7.261, 'L1_ffn_w2': 7.239}
    for name, (base, spread) in spreads.items():
        noise = np.random.default_rng([zlib.crc32(name.encode()), seed]).standard_normal(out[name].shape)
        drawn = base * np.exp(spread * noise) if base else spread * noise
        out[name] = jnp.asarray(drawn.astype(out[name].dtype))
    for name, factor in factors.items():
        out[name] = (out[name] * factor).astype(out[name].dtype)
    return out
```

```python
import math
from contextlib import ExitStack

import numpy as np

import concourse.bass as bass
from concourse import mybir

F32, BF16, F16, U32 = mybir.dt.float32, mybir.dt.bfloat16, mybir.dt.float16, mybir.dt.uint32
ALU, ACT, AX = mybir.AluOpType, mybir.ActivationFunctionType, mybir.AxisListType

B, NP, D = 16, 36, 192
T = B * NP
CPP = 768
KC = CPP // 128
NT = -(-T // 128)
HF = D // 2
AH, AD = 12, 64
HP = AH // 2
PAIRS = B // 2
FH = 512
TH, TD = 12, 16
G3 = 3
TT = -(-B // G3)
TR = G3 * NP
E, CAP = 8, int(math.ceil(1.25 * 2 * T / 8))
SH = CAP // 2
MAGIC = 12582912.0
ROWS = {}
_at = 0
for _name, _n in [("b_proj", D), ("b_out", D), ("g_in", D), ("g_out", FH), ("pb", D), ("qb", D), ("vb", D), ("lrb", TH),
                  ("tg", D), ("tb", D), ("b1", D)]:
    ROWS[_name] = (_at, _n)
    _at += _n
NROW = _at


def rows_of(i):
    return min(128, T - 128 * i)


def tower(nc, d, out, stage=99):
    ctx = ExitStack()
    with ctx:
        def sb(name, shape, dt=F32):
            return ctx.enter_context(nc.sbuf_tensor(name, shape, dt))

        def sem(name):
            return ctx.enter_context(nc.semaphore(name))

        bank = [ctx.enter_context(nc.psum_tensor(f"bank{i}", [128, 512], F32)) for i in range(8)]
        v_scr = nc.dram_tensor("v_scratch", (T, AH * AD), F32).ap()

        V_W, K_W, WQKV_W = B * HP * 128, HP * B * 72, 2 * 3 * AH * AD
        arenaV = sb("arena_v", [128, V_W])
        arenaK = sb("arena_k", [128, K_W + WQKV_W])
        Vbd = arenaV[0:72, :].rearrange("p (b h c) -> p b h c", b=B, h=HP)
        Kbd = arenaK[:, 0:K_W].rearrange("p (h b c) -> p h b c", h=HP, b=B)
        wqkv = arenaK[0:HF, K_W:].rearrange("p (j n) -> p j n", j=2)
        EW13, EW2 = 2 * 2 * 2 * FH // 2, 2 * 4 * D // 2
        w13p, w2p = [], []
        for e in range(E):
            ar, o = (arenaV, e) if e < 4 else (arenaK, e - 4)
            o *= EW13 + EW2
            w13p.append(ar[0:HF, o:o + EW13].bitcast(F16).rearrange("p (x j n) -> p x j n", x=2, j=2))
            w2p.append(ar[:, o + EW13:o + EW13 + EW2].bitcast(F16).rearrange("p (x m n) -> p x m n", x=2, m=4))

        A2W = 16000
        arena = sb("arena_2", [128, A2W])

        def carve(at, *dims, rows=128, dt=F32):
            n = int(np.prod(dims))
            w = n if dt == F32 else (n + 1) // 2
            assert at[0] + w <= A2W, (at, w)
            v = arena[0:rows, at[0]:at[0] + w]
            at[0] += w
            if dt != F32:
                v = v.bitcast(dt)
            if len(dims) == 2:
                v = v.rearrange("p (a b) -> p a b", a=dims[0])
            if len(dims) == 3:
                v = v.rearrange("p (a b c) -> p a b c", a=dims[0], b=dims[1])
            if len(dims) == 4:
                v = v.rearrange("p (a b c e) -> p a b c e", a=dims[0], b=dims[1], c=dims[2])
            return v

        at = [0]
        xpT = carve(at, KC, T)
        aoT = xpT
        v_sb = carve(at, NT, AH * AD)
        qT = carve(at, HP, T + 64 - NP)
        woT = carve(at, HP, D)
        P = carve(at, 3, 432)
        wpT = P[:, :, :].rearrange("p a b -> p (a b)")[:, 0:KC * D].rearrange("p (k n) -> p k n", k=KC)
        PT = carve(at, 2, 768, rows=72)
        at = [KC * T]
        y = carve(at, 2, FH)
        sg = carve(at, 2, FH)
        junk = carve(at, FH)
        yi = carve(at, 2, FH, dt=BF16)
        yiT = carve(at, 2, 4, 128, dt=BF16)
        xi = carve(at, NT, D, dt=BF16)
        xiT = carve(at, 2, T, rows=HF, dt=BF16)
        at = [0]
        QK = carve(at, TT, 2 * D, rows=TR)
        CZ = carve(at, TT, 2 * D + TH, rows=TR)
        XH = carve(at, TT, D, rows=TR)
        GG = carve(at, TT, D, rows=TR)
        SQ = carve(at, TT, D, rows=TR)
        Gm = carve(at, 2, G3, D, rows=TR)
        QTW = G3 * TR
        QTf = carve(at, 2 * TT * QTW + TR, rows=HF)
        W1n = carve(at, 2, 2, G3 * HF, rows=HF)
        b1n = carve(at, 2, D, rows=G3)
        rowa, rowb = carve(at, 2 * D, rows=TR), carve(at, 2 * D + TH, rows=TR)
        gam2, b1c = carve(at, D, rows=TR), carve(at, D, rows=TR)
        at = [0]
        xs = carve(at, NT, D)
        xsp = carve(at, 2, NT, D, dt=F16)
        oh = carve(at, 2, NT, CAP, dt=F16)
        ohT = carve(at, 2, 2, T, rows=SH, dt=F16)
        posb = carve(at, T, rows=SH, dt=F16)
        zf = carve(at, 2, CAP, rows=HF)
        zp = carve(at, 2, 2, CAP, rows=HF, dt=F16)
        sgm = carve(at, 2, 2 * CAP)
        actf = carve(at, 4, CAP)
        actp = carve(at, 2, 4, CAP, dt=F16)
        yp = carve(at, 2, 2, D, rows=SH, dt=F16)
        yf = carve(at, 2, D, rows=SH)
        lg = carve(at, NT, E)
        top, topf = carve(at, NT, 8), carve(at, NT, 8)
        topi = carve(at, NT, 8).bitcast(U32)
        m1, m2, mk = carve(at, NT, E), carve(at, NT, E), carve(at, NT, E)
        mk16, pos16 = carve(at, NT, E, dt=F16), carve(at, NT, E, dt=F16)
        posf, cw, kp = carve(at, NT, E), carve(at, NT, E), carve(at, NT, E)
        cwp = carve(at, 2, NT, E, dt=F16)
        wts = carve(at, NT, 4)

        def q_tile(j, t, b):
            o = (j * TT + t) * QTW + TR * b
            return QTf[:, o:o + TR]

        def q_blocks(j, t):
            o = (j * TT + t) * QTW
            return QTf[:, o:o + G3 * (TR + NP)].rearrange("p (b n) -> p b n", b=G3)[:, :, 0:NP]

        h = sb("h", [128, NT, D])
        xc = sb("xc", [128, NT, D])
        xnT = sb("xnT", [HF, 2, TT * TR])
        rows = sb("rows", [128, NROW])

        def row(name, r=128):
            o, n = ROWS[name]
            return rows[0:r, o:o + n]

        cols = sb("cols", [HF, 4])
        nw = sb("nw", [HF, 2, E])
        idf, idb, idh = sb("idf", [128, 128]), sb("idb", [128, 128], BF16), sb("idh", [128, 128], F16)
        tri, ones16 = sb("tri", [128, 128], F16), sb("ones16", [128, 128], F16)
        iota = sb("iota", [128, CAP], F16)
        iota8 = sb("iota8", [128, E])
        slot = sb("slot", [SH, 2])
        bmask, bmaskT = sb("bmask", [TR, G3]), sb("bmaskT", [G3, TR])
        bd = sb("bd", [HF, HF])
        stage13, stage2 = sb("stage13", [HF, 2, 2 * FH]), sb("stage2", [128, 4, D])
        wiq, w2q = sb("wiq", [HF, 2, 2 * FH], BF16), sb("w2q", [128, 4, D], BF16)
        wa = sb("wa", [HF, 2, 2 * D])
        wb = sb("wb", [HF, 2, 2 * D + TH])
        wkn = sb("wkn", [HF, 2, D])
        w1s = sb("w1s", [HF, 2, TD])
        bdw1 = sb("bdw1", [HF, 2, HF])
        wpj = sb("wpj", [HF, 2, D])
        gateT = sb("gateT", [HF, 2, E])
        st, mv = sb("st", [128, NT, 6]), sb("mv", [128, NT, 2])
        arg, rs, half_ = sb("arg", [128, 2 * NT]), sb("rs", [128, 2 * NT]), sb("mhalf", [128, 2 * NT])
        mx, sm, ri = sb("mx", [128, 2, AH]), sb("sm", [128, 2, AH]), sb("ri", [128, 2, AH])
        am, c1, qs = sb("am", [128, NT]), sb("c1", [128, NT]), sb("qs", [128, NT])
        am2, c2, ssq = sb("am2", [128, NT]), sb("c2", [128, NT]), sb("ssq", [128, NT])
        wsum, mw, sw, mwd = sb("wsum", [128, 2]), sb("mw", [128, 2]), sb("sw", [128, 2]), sb("mwd", [128, 2])
        tail = 4 * (EW13 + EW2)
        hv = [arenaV[0:TR, tail + TT * TH * n:tail + TT * TH * (n + 1)] for n in range(6)]
        sig = arenaV[0:TR, tail + TT * TH * 6:tail + TT * TH * 7].rearrange("p (t h) -> p t h", t=TT)
        wmean = sb("wmean", [HF, 2])
        b1m = sb("b1m", [TR, TH])
        cws = sb("cws", [SH, 2, 2])
        ones = sb("ones", [128, 1])
        kw = sb("kw", [128, NT])

        free = [sem(f"bank{i}_evacuated") for i in range(8)]
        full = [sem(f"bank{i}_filled") for i in range(8)]
        dve_s, act_s, pool_s, pe_s = sem("dve_step"), sem("act_step"), sem("pool_step"), sem("pe_step")
        ln_arg, ln_pow, ln_x = sem("ln_arg"), sem("ln_pow"), sem("ln_x")
        ld = {}

        def loaded(name):
            if name not in ld:
                ld[name] = sem(f"loaded_{name}")
            return ld[name]

        zeroed, idb_made = sem("zeroed"), sem("identity_bf16")
        v_stored, vbd_loaded = sem("v_stored"), sem("vbd_loaded")
        subbed, exped, rinved, normed, hbias = sem("subbed"), sem("exped"), sem("rinved"), sem("normed"), sem("hbias")
        q_ready, silu_done, y_done, sq_done, arg2, pow2, yi_done = (sem(n) for n in (
            "xi_quantised", "silu_done", "y_done", "ysq_done", "y_arg", "y_pow", "yi_quantised"))
        wq_part, wq_sum, wq_done = sem("weight_sums"), sem("weight_mean"), sem("weights_quantised")
        stage_free = sem("stage_free")
        bdw1_done, wz_sum = sem("bdw1_done"), sem("wz_sum")
        split_hi, split_lo = sem("split_hi"), sem("split_lo")
        h_done = sem("h_done")
        tt_z, tt_sq, tt_var, tt_sqrt, tt_sig, tt_g, tt_gm = (sem(n) for n in (
            "ttt_z", "ttt_square", "ttt_var", "ttt_sqrt", "ttt_sigmoid", "ttt_grad", "ttt_masked"))
        tt_w1n, tt_qb, tt_zb, tt_out = sem("ttt_w1n"), sem("ttt_q_plus_beta"), sem("ttt_zb"), sem("ttt_out")
        mk_done, pos_done, lam, ex1, cw_done, xs_done = (sem(n) for n in (
            "mask_done", "pos_done", "logit_gap", "gap_exp", "cw_done", "xs_done"))
        oh_done, oht_done, z_f, z_done, sil, actf_done, act_done, yp_done = (sem(n) for n in (
            "onehot", "onehotT", "z_scaled", "z_split", "moe_silu", "act_f", "act_split", "y_split"))
        acth = sem("act_hi")
        fin, stored = sem("fin"), sem("stored")

        use, count = {}, [0] * 8
        ring = [0, list(range(8))]

        def plan(*key, at=None):
            if at is None:
                at = ring[1][ring[0] % len(ring[1])]
                ring[0] += 1
            use[key] = (at, count[at])
            count[at] += 1

        for i in range(NT):
            plan("embed", i)
        for i in range(NT):
            plan("xnT", i)
        for i in range(NT):
            for c in range(2):
                plan("v", i, c)
        for hp in range(HP):
            if hp == 1:
                plan("wmean")
            for n in range(2):
                plan("k", hp, n)
            for n in range(2):
                plan("q", hp, n)
        for s in range(PAIRS + 2):
            if s < PAIRS:
                plan("S", s)
            if 0 <= s - 1 < PAIRS:
                plan("PT", s - 1, 0)
                plan("PT", s - 1, 1)
            if 0 <= s - 2 < PAIRS:
                plan("PV", s - 2)
        for i in range(NT):
            plan("wo", i)
        for i in range(NT):
            plan("xiT", i)
        for i in range(NT):
            plan("gate", i)
            plan("up", i)
        for i in range(NT):
            plan("yiT", i)
            plan("down", i)
        plan("wz")
        for i in range(NT):
            plan("x1T", i)
        for t in range(TT):
            plan("B", t)
            plan("A", t)
        for t in range(TT):
            plan("QT", t)
        for t in range(TT + 1):
            if t < TT:
                plan("gW", t, 0)
                plan("gW", t, 1)
                plan("gb", t)
            if t >= 1:
                plan("Z", t - 1)
        for t in range(TT):
            plan("oT", t)
        for i in range(NT):
            plan("proj", i)
        for i in range(NT):
            plan("x2T", i)
        plan("logits")
        plan("pos")
        ring = [0, [3, 4, 5, 6, 7]]
        for b in range(3):
            plan("acc", b, at=b)
        for s in range(E + 1):
            if s < E:
                plan("posb", s, 0)
                plan("posb", s, 1)
                plan("z", s)
            if s >= 1:
                plan("y", s - 1)
            if s < E:
                for r in range(2):
                    plan("g", s, r)
                    plan("u", s, r)

        def at_bank(*key):
            return bank[use[key][0]]

        def claim(eng, *key):
            b, n = use[key]
            if n:
                eng.wait_ge(free[b], n)
            return bank[b]

        def wait_full(eng, *key):
            b, n = use[key]
            eng.wait_ge(full[b], n + 1)
            return bank[b]

        def wait_evac(eng, *key):
            b, n = use[key]
            eng.wait_ge(free[b], n + 1)

        def fills(ins, *key):
            ins.then_inc(full[use[key][0]], 1)

        def frees(ins, *key):
            ins.then_inc(free[use[key][0]], 1)

        class Steps:

            def __init__(self, eng, s):
                self.eng, self.s, self.n = eng, s, 0

            def do(self, ins):
                ins.then_inc(self.s, 1)
                self.n += 1

            def settle(self):
                if self.n:
                    self.eng.wait_ge(self.s, self.n)

            def then(self, ins):
                self.do(ins)
                self.settle()

        def split_high(act, e):
            if e == 0:
                wait_full(act, "PV", PAIRS - 1)
            act.wait_ge(loaded("e13"), 16 * (e + 1))
            act.wait_ge(loaded("e2"), 16 * (e + 1))
            nc.scalar.activation(w13p[e][:, 0], stage13[:], ACT.Copy).then_inc(split_hi, 1)
            nc.scalar.activation(w2p[e][:, 0], stage2[:], ACT.Copy).then_inc(split_hi, 1)

        def split_low(pool, e):
            pool.wait_ge(split_hi, 2 * e + 2)
            nc.gpsimd.tensor_tensor(w13p[e][:, 1], stage13[:], w13p[e][:, 0], ALU.subtract).then_inc(split_lo, 1)
            nc.gpsimd.tensor_tensor(w2p[e][:, 1], stage2[:], w2p[e][:, 0], ALU.subtract).then_inc(split_lo, 1)

        block = ctx.enter_context(nc.Block())

        @block.sync
        def _(sp):
            def load(dst, name, src=None):
                sp.dma_start(dst, d[name] if src is None else src).then_inc(loaded(name), 16)

            for k in range(KC):
                sp.dma_start(xpT[:, k, :], d["xT"][:, k, :]).then_inc(loaded(f"x{k}"), 16)
                sp.dma_start(wpT[:, k, :], d["wpT"][:, k, :]).then_inc(loaded(f"x{k}"), 16)
            load(rows[:], "rows", d["rows"].partition_broadcast(128))
            load(idf[:], "idf")
            load(cols[:], "cols")
            sp.dma_start(wqkv[:, :, 2 * AH * AD:], d["wqkv"][:, :, 2 * AH * AD:]).then_inc(loaded("wv"), 16)
            sp.dma_start(wqkv[:, :, 0:2 * AH * AD], d["wqkv"][:, :, 0:2 * AH * AD]).then_inc(loaded("wqk"), 16)
            load(stage13[:], "w_in")
            load(stage2[:], "w_out2")
            load(woT, "woT")
            for name, t in [("idh", idh), ("tri", tri), ("iota", iota), ("iota8", iota8), ("slot", slot),
                            ("bmask", bmask), ("bmaskT", bmaskT), ("bd", bd), ("nw", nw), ("wvT", wb[:, :, D:2 * D]),
                            ("wkn", wkn), ("w1s", w1s), ("wpj", wpj), ("gateT", gateT)]:
                load(t if name == "wvT" else t[:], name)
            load(wa[:], "wa")
            load(wb[:, :, 2 * D:], "lrT")
            for i in range(NT):
                r = rows_of(i)
                wait_evac(sp, "v", i, 0)
                wait_evac(sp, "v", i, 1)
                sp.dma_start(v_scr[128 * i:128 * i + r, :], v_sb[0:r, i, :]).then_inc(v_stored, 16)
            sp.wait_ge(v_stored, 16 * NT)
            sp.wait_ge(zeroed, 2)
            src = v_scr.rearrange("(b k) (h x c) -> x k b h c", k=NP, h=HP, x=2)
            for g in range(B // 2):
                for x in range(2):
                    for b in (2 * g, 2 * g + 1):
                        sp.dma_start(Vbd[NP * x:NP * x + NP, b, :, 64 * x:64 * x + 64], src[x, :, b]).then_inc(vbd_loaded, 16)
            if stage >= 4:
                for e in range(E):
                    sp.wait_ge(wq_done, 2)
                    if e:
                        sp.wait_ge(split_lo, 2 * e)
                        sp.wait_ge(split_hi, 2 * e)
                    sp.dma_start(stage13[:], d["w13"][:, e]).then_inc(loaded("e13"), 16)
                    sp.dma_start(stage2[:], d["w2"][:, e]).then_inc(loaded("e2"), 16)
            for i in range(NT):
                r = rows_of(i)
                sp.wait_ge(fin, i + 1)
                sp.dma_start(out[128 * i:128 * i + r, :], h[0:r, i, :]).then_inc(stored, 16)
            sp.wait_ge(stored, 16 * NT)
            for name in ("rows", "idf", "cols", "wv", "wqk", "w_in", "w_out2", "woT", "idh", "tri", "iota", "iota8", "slot", "bmask", "bmaskT", "bd", "nw", "wvT", "wkn", "w1s", "wpj", "gateT", "wa", "lrT"):
                sp.wait_ge(loaded(name), 16)

        @block.tensor
        def _(pe):
            mm, tr = nc.tensor.matmul, nc.tensor.transpose

            for i in range(NT):
                claim(pe, "embed", i)
            for k in range(KC):
                pe.wait_ge(loaded(f"x{k}"), 32)
                for i in range(NT):
                    r = rows_of(i)
                    ins = mm(at_bank("embed", i)[0:r, 0:D], xpT[:, k, 128 * i:128 * i + r], wpT[:, k, :],
                             start=k == 0, stop=k == KC - 1)
                    if k == KC - 1:
                        fills(ins, "embed", i)

            def x_transposed(key, ln):
                pe.wait_ge(loaded("idf"), 16)
                for i in range(NT):
                    r = rows_of(i)
                    bk = claim(pe, key, i)
                    pe.wait_ge(ln_x, NT * ln + i + 1)
                    for j in range(2):
                        ins = tr(bk[0:HF, 128 * j:128 * j + r], xc[0:r, i, HF * j:HF * j + HF], idf[0:r, 0:r])
                    fills(ins, key, i)

            x_transposed("xnT", 0)
            pe.wait_ge(loaded("wv"), 16)
            for i in range(NT):
                r = rows_of(i)
                wait_evac(pe, "xnT", i)
                for c in range(2):
                    bk = claim(pe, "v", i, c)
                    for j in range(2):
                        ins = mm(bk[0:r, 0:384], xnT[:, j, 128 * i:128 * i + r],
                                 wqkv[:, j, 1536 + 384 * c:1536 + 384 * c + 384], start=j == 0, stop=j == 1)
                    fills(ins, "v", i, c)
            pe.wait_ge(loaded("wqk"), 16)
            for hp in range(HP):
                if hp == 1:
                    bk = claim(pe, "wmean")
                    pe.wait_ge(wq_part, 2)
                    pe.wait_ge(zeroed, 3)
                    mm(bk[:, 0:1], ones[0:HF, :].broadcast_to([HF, 128]), wsum[0:HF, 0:1], start=True, stop=True)
                    ins = mm(bk[:, 1:2], ones[:, :].broadcast_to([128, 128]), wsum[:, 1:2], start=True, stop=True)
                    fills(ins, "wmean")
                for key, o in (("k", AH * AD), ("q", 0)):
                    for n in range(2):
                        bk = claim(pe, key, hp, n)
                        for j in range(2):
                            ins = mm(bk[:, 0:288], wqkv[:, j, o + 128 * hp:o + 128 * hp + 128],
                                     xnT[:, j, 288 * n:288 * n + 288], start=j == 0, stop=j == 1)
                        fills(ins, key, hp, n)
            for hp in range(HP):
                for n in range(2):
                    wait_evac(pe, "k", hp, n)
                    wait_evac(pe, "q", hp, n)
            pe.wait_ge(zeroed, 3)
            for s in range(PAIRS + 2):
                if s < PAIRS:
                    bk = claim(pe, "S", s)
                    for x in range(2):
                        b = 2 * s + x
                        for hp in range(HP):
                            ins = mm(bk[64 * x:64 * x + 64, 72 * hp:72 * hp + 72], qT[:, hp, NP * b:NP * b + 64],
                                     Kbd[:, hp, b, :], start=True, stop=True)
                    fills(ins, "S", s)
                p = s - 1
                if 0 <= p < PAIRS:
                    pe.wait_ge(normed, p + 1)
                    for c in range(2):
                        bk = claim(pe, "PT", p, c)
                        for g in range(3):
                            hp = 3 * c + g
                            ins = tr(bk[0:72, 128 * g:128 * g + 128], P[:, p % 3, 72 * hp:72 * hp + 72], idf[:])
                        fills(ins, "PT", p, c)
                p = s - 2
                if 0 <= p < PAIRS:
                    wait_evac(pe, "PT", p, 0)
                    wait_evac(pe, "PT", p, 1)
                    if p == 0:
                        pe.wait_ge(vbd_loaded, 16 * 2 * B)
                    bk = claim(pe, "PV", p)
                    for hp in range(HP):
                        for x in range(2):
                            ins = mm(bk[:, 72 * hp + NP * x:72 * hp + NP * x + NP], Vbd[:, 2 * p + x, hp, :],
                                     PT[:, p % 2, 128 * hp + 64 * x:128 * hp + 64 * x + NP], start=True, stop=True)
                    fills(ins, "PV", p)
            pe.wait_ge(loaded("woT"), 16)
            for i in range(NT):
                r = rows_of(i)
                wait_evac(pe, "PV", min(PAIRS - 1, (128 * (i + 1) - 1) // 72))
                bk = claim(pe, "wo", i)
                for hp in range(HP):
                    ins = mm(bk[0:r, 0:D], aoT[:, hp, 128 * i:128 * i + r], woT[:, hp, :], start=hp == 0, stop=hp == HP - 1)
                fills(ins, "wo", i)
            if stage < 2:
                return
            pe.wait_ge(idb_made, 1)
            for i in range(NT):
                r = rows_of(i)
                bk = claim(pe, "xiT", i)
                pe.wait_ge(q_ready, i + 1)
                bv = bk[0:HF, :].bitcast(BF16)
                for j in range(2):
                    ins = tr(bv[:, 128 * j:128 * j + r], xi[0:r, i, HF * j:HF * j + HF], idb[0:r, 0:r])
                fills(ins, "xiT", i)
            pe.wait_ge(wq_done, 1)
            for i in range(NT):
                r = rows_of(i)
                wait_evac(pe, "xiT", i)
                for key, o in (("gate", FH), ("up", 0)):
                    bk = claim(pe, key, i)
                    for j in range(2):
                        ins = mm(bk[0:r, :], xiT[:, j, 128 * i:128 * i + r], wiq[:, j, o:o + FH], start=j == 0, stop=j == 1)
                    fills(ins, key, i)
            pe.wait_ge(wq_done, 2)
            for i in range(NT):
                r = rows_of(i)
                bk = claim(pe, "yiT", i)
                pe.wait_ge(yi_done, i + 1)
                bv = bk[:, :].bitcast(BF16)
                for m in range(4):
                    ins = tr(bv[:, 128 * m:128 * m + r], yi[0:r, i % 2, 128 * m:128 * m + 128], idb[0:r, 0:r])
                fills(ins, "yiT", i)
                wait_evac(pe, "yiT", i)
                bk = claim(pe, "down", i)
                for m in range(4):
                    ins = mm(bk[0:r, 0:D], yiT[:, i % 2, m, 0:r], w2q[:, m, :], start=m == 0, stop=m == 3)
                fills(ins, "down", i)
            if stage < 3:
                return
            bk = claim(pe, "wz")
            pe.wait_ge(bdw1_done, 1)
            pe.wait_ge(loaded("wkn"), 16)
            for c in range(2):
                for j in range(2):
                    ins = mm(bk[0:HF, D * c + HF * j:D * c + HF * j + HF], wkn[:, j, HF * c:HF * c + HF], bdw1[:, j, :],
                             start=True, stop=True)
            fills(ins, "wz")
            x_transposed("x1T", 1)
            wait_evac(pe, "wz")
            pe.wait_ge(loaded("wa"), 16)
            pe.wait_ge(loaded("lrT"), 16)
            for i in range(NT):
                wait_evac(pe, "x1T", i)
            for t in range(TT):
                for key, w, n in (("B", wb, 2 * D + TH), ("A", wa, 2 * D)):
                    bk = claim(pe, key, t)
                    for j in range(2):
                        ins = mm(bk[0:TR, 0:n], xnT[:, j, TR * t:TR * t + TR], w[:, j, :], start=j == 0, stop=j == 1)
                    fills(ins, key, t)
            for t in range(TT):
                wait_evac(pe, "A", t)
                bk = claim(pe, "QT", t)
                for j in range(2):
                    ins = tr(bk[0:HF, TR * j:TR * j + TR], QK[:, t, HF * j:HF * j + HF], idf[0:TR, 0:TR])
                fills(ins, "QT", t)
            pe.wait_ge(loaded("bmask"), 16)
            pe.wait_ge(loaded("bmaskT"), 16)
            for t in range(TT + 1):
                if t < TT:
                    pe.wait_ge(tt_gm, t + 1)
                    for j in range(2):
                        bk = claim(pe, "gW", t, j)
                        ins = mm(bk[0:HF, 0:G3 * HF], QK[:, t, D + HF * j:D + HF * j + HF], Gm[:, t % 2, :, HF * j:HF * j + HF],
                                 start=True, stop=True)
                        fills(ins, "gW", t, j)
                    bk = claim(pe, "gb", t)
                    ins = mm(bk[0:G3, 0:D], bmask[:, :], GG[:, t, :], start=True, stop=True)
                    fills(ins, "gb", t)
                u = t - 1
                if u >= 0:
                    wait_evac(pe, "QT", u)
                    wait_evac(pe, "gW", u, 0)
                    wait_evac(pe, "gb", u)
                    pe.wait_ge(tt_w1n, u + 1)
                    bk = claim(pe, "Z", u)
                    for j in range(2):
                        for b in range(G3):
                            mm(bk[0:TR, HF * j:HF * j + HF], q_tile(j, u, b),
                               W1n[:, u % 2, j, HF * b:HF * b + HF], start=b == 0, stop=False)
                        ins = mm(bk[0:TR, HF * j:HF * j + HF], bmaskT[:, :], b1n[:, u % 2, HF * j:HF * j + HF],
                                 start=False, stop=True)
                    fills(ins, "Z", u)
            for t in range(TT):
                pe.wait_ge(tt_out, t // 3 + 1)
                bk = claim(pe, "oT", t)
                for j in range(2):
                    ins = tr(bk[0:HF, TR * j:TR * j + TR], XH[:, t, HF * j:HF * j + HF], idf[0:TR, 0:TR])
                fills(ins, "oT", t)
            pe.wait_ge(loaded("wpj"), 16)
            for i in range(NT):
                r = rows_of(i)
                wait_evac(pe, "oT", min(TT - 1, (128 * (i + 1) - 1) // TR))
                bk = claim(pe, "proj", i)
                for j in range(2):
                    ins = mm(bk[0:r, 0:D], xnT[:, j, 128 * i:128 * i + r], wpj[:, j, :], start=j == 0, stop=j == 1)
                fills(ins, "proj", i)
            if stage < 4:
                return
            x_transposed("x2T", 2)
            pe.wait_ge(loaded("gateT"), 16)
            bk = claim(pe, "logits")
            for i in range(NT):
                r = rows_of(i)
                wait_evac(pe, "x2T", i)
                for j in range(2):
                    ins = mm(bk[0:r, E * i:E * i + E], xnT[:, j, 128 * i:128 * i + r], gateT[:, j, :], start=j == 0, stop=j == 1)
            fills(ins, "logits")
            bk = claim(pe, "pos")
            pe.wait_ge(mk_done, 1)
            pe.wait_ge(loaded("tri"), 16)
            for i in range(NT):
                r = rows_of(i)
                for k in range(i + 1):
                    ins = mm(bk[0:r, E * i:E * i + E], (tri if k == i else ones16)[0:rows_of(k), 0:r],
                             mk16[0:rows_of(k), k, :], start=k == 0, stop=k == i)
            fills(ins, "pos")
            pe.wait_ge(xs_done, 1)
            pe.wait_ge(cw_done, 1)
            pe.wait_ge(pos_done, 1)
            pe.wait_ge(loaded("idh"), 16)
            for b in range(3):
                bk = claim(pe, "acc", b)
                r, n = (128, 2 * D) if b < 2 else (T - 512, D)
                mm(bk[0:r, 0:n], tri[:, 0:1].broadcast_to([128, r]), tri[:, 0:1].broadcast_to([128, n]), start=True, stop=False)

            def dispatch(e):
                for c in range(2):
                    bk = claim(pe, "posb", e, c)
                    for i in ((0, 1, 2), (3, 4))[c]:
                        r = rows_of(i)
                        o = 128 * (i - 3 * c)
                        ins = mm(bk[0:SH, o:o + r], pos16[0:r, i, e:e + 1].broadcast_to([r, SH]), idh[0:r, 0:r],
                                 start=True, stop=True)
                    fills(ins, "posb", e, c)
                bk = claim(pe, "z", e)
                pe.wait_ge(oh_done, e + 1)
                for j in range(2):
                    for i in range(NT):
                        r = rows_of(i)
                        for x in range(2):
                            ins = mm(bk[0:HF, CAP * j:CAP * j + CAP], xsp[0:r, x, i, HF * j:HF * j + HF],
                                     oh[0:r, e % 2, i, :], start=i == 0 and x == 0, stop=i == NT - 1 and x == 1)
                for s in range(2):
                    for i in range(NT):
                        r = rows_of(i)
                        for x in range(2):
                            ins = mm(bk[0:SH, 2 * CAP + s:2 * CAP + s + 1], oh[0:r, e % 2, i, SH * s:SH * s + SH],
                                     cwp[0:r, x, i, e:e + 1], start=i == 0 and x == 0, stop=i == NT - 1 and x == 1)
                fills(ins, "z", e)

            def up_gate(e):
                pe.wait_ge(z_done, e + 1)
                pe.wait_ge(split_hi, 2 * e + 2)
                pe.wait_ge(split_lo, 2 * e + 2)
                for rnd in range(2):
                    for key, o in (("g", 0), ("u", FH)):
                        bk = claim(pe, key, e, rnd)
                        for m in range(2):
                            f = o + 128 * (2 * rnd + m)
                            n = 0
                            for wx, zx in ((0, 0), (0, 1), (1, 0)):
                                for j in range(2):
                                    ins = mm(bk[:, CAP * m:CAP * m + CAP], w13p[e][:, wx, j, f:f + 128], zp[:, zx, j, :],
                                             start=n == 0, stop=n == 5)
                                    n += 1
                        fills(ins, key, e, rnd)

            def down(e):
                pe.wait_ge(act_done, e + 1)
                bk = claim(pe, "y", e)
                for s in range(2):
                    n = 0
                    for m in range(4):
                        for wx, ax in ((0, 0), (0, 1), (1, 0)):
                            ins = mm(bk[0:SH, D * s:D * s + D], actp[:, ax, m, SH * s:SH * s + SH], w2p[e][:, wx, m, :],
                                     start=n == 0, stop=n == 11)
                            n += 1
                fills(ins, "y", e)

            def combine(e):
                pe.wait_ge(yp_done, e + 1)
                pe.wait_ge(oht_done, e + 1)
                for i in range(NT):
                    r = rows_of(i)
                    for s in range(2):
                        for x in range(2):
                            ins = mm(bank[i // 2][0:r, D * (i % 2):D * (i % 2) + D], ohT[:, e % 2, s, 128 * i:128 * i + r],
                                     yp[:, x, s, :], start=False,
                                     stop=e == E - 1 and s == 1 and x == 1 and (i % 2 == 1 or i == NT - 1))
                    if e == E - 1 and (i % 2 == 1 or i == NT - 1):
                        fills(ins, "acc", i // 2)
                if e < E - 1:
                    ins.then_inc(pe_s, 1)

            for s in range(E + 1):
                if s < E:
                    dispatch(s)
                if s >= 1:
                    down(s - 1)
                if s < E:
                    up_gate(s)
                if s >= 1:
                    combine(s - 1)

        @block.vector
        def _(dve):
            st_ = Steps(dve, dve_s)
            v = nc.vector

            def stats(i, A, c, second=None):
                r = rows_of(i)
                st_.then(v.bn_stats(st[0:r, i, :], h[0:r, i, :]))
                st_.then(v.bn_aggr(mv[0:r, i, :], st[0:r, i, :]))
                if second:
                    st_.do(v.tensor_scalar(arg[0:r, NT + i:NT + i + 1], mv[0:r, i, 1:2], *second, ALU.mult, ALU.add))
                v.tensor_scalar(arg[0:r, i:i + 1], mv[0:r, i, 1:2], A, c, ALU.mult, ALU.add).then_inc(ln_arg, 1)

            def normalise(n, i, last=True):
                r = rows_of(i)
                dve.wait_ge(ln_pow, n)
                ins = v.tensor_scalar(xc[0:r, i, :], h[0:r, i, :], mv[0:r, i, 0:1], rs[0:r, i:i + 1], ALU.subtract, ALU.mult)
                if last:
                    ins.then_inc(ln_x, 1)
                return ins

            dve.wait_ge(loaded("rows"), 16)
            for i in range(NT):
                r = rows_of(i)
                bk = wait_full(dve, "embed", i)
                frees(v.tensor_tensor(h[0:r, i, :], bk[0:r, 0:D], row("b_proj", r), ALU.add), "embed", i)
                wait_evac(dve, "embed", i)
                stats(i, 1.0 + 1e-5, 1e-10)
            for i in range(NT):
                normalise(i + 1, i)
            for i in range(NT):
                r = rows_of(i)
                bk = wait_full(dve, "v", i, 0)
                frees(v.tensor_copy(v_sb[0:r, i, 0:384], bk[0:r, 0:384]), "v", i, 0)
            dve.wait_ge(loaded("w_in"), 16)
            dve.wait_ge(loaded("w_out2"), 16)
            v.tensor_reduce(wsum[0:HF, 0:1], stage13[:, :, :], AX.XY, ALU.add, apply_absolute_value=True).then_inc(wq_part, 1)
            v.tensor_reduce(wsum[:, 1:2], stage2[:, :, :], AX.XY, ALU.add, apply_absolute_value=True).then_inc(wq_part, 1)

            dve.wait_ge(loaded("idf"), 16)
            v.tensor_copy(idb[:], idf[:]).then_inc(idb_made, 1)

            def ternary_weights():
                bk = wait_full(dve, "wmean")
                st_.do(v.tensor_scalar(mw[:, 0:1], bk[:, 0:1], 1.0 / (2 * FH * D), 1e-5, ALU.mult, ALU.max))
                frees(v.tensor_scalar(mw[:, 1:2], bk[:, 1:2], 1.0 / (FH * D), 1e-5, ALU.mult, ALU.max), "wmean")
                wait_evac(dve, "wmean")
                st_.do(v.reciprocal(sw[:], mw[:]))
                st_.then(v.tensor_scalar(mwd[:], mw[:], 1.0 / 127.0, None, ALU.mult))
                for n, (w, q, r) in enumerate(((stage13, wiq, HF), (stage2, w2q, 128))):
                    st_.then(v.tensor_scalar(w[:], w[:], sw[0:r, n:n + 1], 1.0, ALU.mult, ALU.min))
                    st_.then(v.tensor_scalar(w[:], w[:], -1.0, MAGIC, ALU.max, ALU.add))
                    v.tensor_scalar(q[:], w[:], MAGIC, None, ALU.subtract).then_inc(wq_done, 1)

            dve.wait_ge(zeroed, 1)
            for hp in range(HP):
                if hp == 3:
                    ternary_weights()
                for n in range(2):
                    bk = wait_full(dve, "k", hp, n)
                    for x in range(2):
                        ins = v.tensor_copy(Kbd[64 * x:64 * x + 64, hp, 8 * n:8 * n + 8, NP * x:NP * x + NP],
                                            bk[64 * x:64 * x + 64, 0:288].rearrange("p (b k) -> p b k", k=NP))
                    frees(ins, "k", hp, n)
            for s in range(PAIRS + 1):
                if s < PAIRS:
                    bk = wait_full(dve, "S", s)
                    sv = bk[:, 0:432].rearrange("p (h k) -> p h k", k=NP)
                    st_.then(v.tensor_reduce(mx[:, s % 2, :], sv, AX.X, ALU.max))
                    if s >= 3:
                        wait_full(dve, "PT", s - 3, 1)
                    v.tensor_tensor(P[:, s % 3, :].rearrange("p (h k) -> p h k", k=NP), sv,
                                    mx[:, s % 2, :].unsqueeze(2).broadcast_to([128, AH, NP]), ALU.subtract).then_inc(
                                        free[use["S", s][0]], 1)
                p = s - 1
                if p >= 0:
                    dve.wait_ge(exped, p + 1)
                    st_.then(v.tensor_reduce(sm[:, p % 2, :], P[:, p % 3, :].rearrange("p (h k) -> p h k", k=NP), AX.X, ALU.add))
                    if p >= 2:
                        dve.wait_ge(normed, p - 1)
                    v.reciprocal(ri[:, p % 2, :], sm[:, p % 2, :]).then_inc(rinved, 1)
            dve.wait_ge(hbias, 1)
            for i in range(NT):
                r = rows_of(i)
                bk = wait_full(dve, "wo", i)
                frees(v.tensor_tensor(h[0:r, i, :], bk[0:r, 0:D], h[0:r, i, :], ALU.add), "wo", i)
                wait_evac(dve, "wo", i)
                if stage < 2:
                    st_.then(v.tensor_copy(xc[0:r, i, :], h[0:r, i, :]))
                    v.tensor_copy(h[0:r, i, :], xc[0:r, i, :]).then_inc(fin, 1)
                else:
                    stats(i, 1.0 + 1e-6, 1e-11)
            if stage < 2:
                return
            for i in range(NT):
                r = rows_of(i)
                st_.then(normalise(NT + i + 1, i, last=False))
                st_.then(v.tensor_tensor(xc[0:r, i, :], xc[0:r, i, :], row("g_in", r), ALU.mult))
                st_.then(v.tensor_reduce(am[0:r, i:i + 1], xc[0:r, i, :], AX.X, ALU.max, apply_absolute_value=True))
                st_.then(v.tensor_scalar(am[0:r, i:i + 1], am[0:r, i:i + 1], 1e-5, None, ALU.max))
                st_.do(v.tensor_scalar(c1[0:r, i:i + 1], am[0:r, i:i + 1], mwd[0:r, 0:1], None, ALU.mult))
                st_.then(v.reciprocal(qs[0:r, i:i + 1], am[0:r, i:i + 1]))
                st_.then(v.tensor_scalar(qs[0:r, i:i + 1], qs[0:r, i:i + 1], 127.0, None, ALU.mult))
                st_.then(v.tensor_scalar(xc[0:r, i, :], xc[0:r, i, :], qs[0:r, i:i + 1], MAGIC, ALU.mult, ALU.add))
                v.tensor_scalar(xi[0:r, i, :], xc[0:r, i, :], MAGIC, None, ALU.subtract).then_inc(q_ready, 1)
            for i in range(NT):
                r = rows_of(i)
                bk = wait_full(dve, "up", i)
                wait_evac(dve, "gate", i)
                if i >= 2:
                    dve.wait_ge(sq_done, i - 1)
                frees(v.scalar_tensor_tensor(out=y[0:r, i % 2, :], in0=bk[0:r, :], scalar=c1[0:r, i:i + 1],
                                             in1=sg[0:r, i % 2, :], op0=ALU.mult, op1=ALU.mult), "up", i)
                wait_evac(dve, "up", i)
                st_.then(v.tensor_tensor(sg[0:r, i % 2, :], y[0:r, i % 2, :], row("g_out", r), ALU.mult))
                st_.then(v.tensor_reduce(am2[0:r, i:i + 1], sg[0:r, i % 2, :], AX.X, ALU.max, apply_absolute_value=True))
                dve.wait_ge(sq_done, i + 1)
                v.tensor_scalar(arg[0:r, NT + i:NT + i + 1], ssq[0:r, i:i + 1], 1.0 / FH, 1e-6, ALU.mult, ALU.add).then_inc(arg2, 1)
                dve.wait_ge(pow2, i + 1)
                rr = rs[0:r, NT + i:NT + i + 1]
                st_.then(v.tensor_scalar(am2[0:r, i:i + 1], am2[0:r, i:i + 1], rr, 1e-5, ALU.mult, ALU.max))
                st_.do(v.tensor_scalar(c2[0:r, i:i + 1], am2[0:r, i:i + 1], mwd[0:r, 1:2], None, ALU.mult))
                st_.then(v.reciprocal(qs[0:r, i:i + 1], am2[0:r, i:i + 1]))
                st_.then(v.tensor_scalar(qs[0:r, i:i + 1], qs[0:r, i:i + 1], 127.0, rr, ALU.mult, ALU.mult))
                st_.then(v.tensor_scalar(sg[0:r, i % 2, :], sg[0:r, i % 2, :], qs[0:r, i:i + 1], MAGIC, ALU.mult, ALU.add))
                if i >= 2:
                    wait_full(dve, "yiT", i - 2)
                v.tensor_scalar(yi[0:r, i % 2, :], sg[0:r, i % 2, :], MAGIC, None, ALU.subtract).then_inc(yi_done, 1)
            for i in range(NT):
                r = rows_of(i)
                bk = wait_full(dve, "down", i)
                frees(v.scalar_tensor_tensor(out=h[0:r, i, :], in0=bk[0:r, 0:D], scalar=c2[0:r, i:i + 1], in1=h[0:r, i, :],
                                             op0=ALU.mult, op1=ALU.add), "down", i)
                wait_evac(dve, "down", i)
                if stage < 3:
                    st_.then(v.tensor_copy(xc[0:r, i, :], h[0:r, i, :]))
                    v.tensor_copy(h[0:r, i, :], xc[0:r, i, :]).then_inc(fin, 1)
                else:
                    stats(i, 1.0, 1e-5)
            if stage < 3:
                return
            for name in ("w1s", "bd", "wvT", "wa", "bmask"):
                dve.wait_ge(loaded(name), 16)
            st_.then(v.tensor_reduce(wmean[:, :], w1s[:, :, :], AX.X, ALU.add))
            st_.then(v.tensor_scalar(wmean[:, :], wmean[:, :], 1.0 / TD, None, ALU.mult))
            st_.then(v.tensor_tensor(w1s[:, :, :], w1s[:, :, :], wmean[:, :].unsqueeze(2).broadcast_to([HF, 2, TD]), ALU.subtract))
            for j in range(2):
                ins = v.tensor_tensor(bdw1[:, j, :].rearrange("p (a b) -> p a b", b=TD),
                                      w1s[:, j, :].unsqueeze(1).broadcast_to([HF, HF // TD, TD]),
                                      bd[:, :].rearrange("p (a b) -> p a b", b=TD), ALU.mult)
                if j == 0:
                    st_.do(ins)
            ins.then_inc(bdw1_done, 1)
            st_.do(v.tensor_tensor(wb[:, :, 0:D], wa[:, :, D:2 * D], wb[:, :, D:2 * D], ALU.subtract))
            st_.do(v.tensor_tensor(gam2[:], row("tg", TR), row("tg", TR), ALU.mult))
            st_.do(v.tensor_copy(rowa[:, 0:D], row("qb", TR)))
            st_.do(v.memset(rowa[:, D:2 * D], 0.0))
            st_.do(v.tensor_tensor(rowb[:, 0:D], row("tb", TR), row("vb", TR), ALU.subtract))
            st_.do(v.tensor_reduce(b1m[:], row("b1", TR).rearrange("p (a b) -> p a b", b=TD), AX.X, ALU.add))
            st_.do(v.tensor_copy(rowb[:, 2 * D:], row("lrb", TR)))
            st_.settle()
            st_.do(v.tensor_scalar(b1m[:], b1m[:], 1.0 / TD, None, ALU.mult))
            st_.do(v.tensor_tensor(rowb[:, 0:D], rowb[:, 0:D], row("tg", TR), ALU.mult))
            for j in range(2):
                st_.do(v.tensor_tensor(wb[:, j, 0:D], wb[:, j, 0:D], row("tg", HF), ALU.mult))
            st_.settle()
            st_.then(v.tensor_tensor(b1c[:].rearrange("p (a b) -> p a b", b=TD), row("b1", TR).rearrange("p (a b) -> p a b", b=TD),
                                     b1m[:].unsqueeze(2).broadcast_to([TR, TH, TD]), ALU.subtract))
            st_.then(v.tensor_copy(rowb[:, D:2 * D], b1c[:]))
            bk = wait_full(dve, "wz")
            frees(v.tensor_copy(wb[:, :, D:2 * D], bk[0:HF, 0:2 * D].rearrange("p (c n) -> p c n", c=2)), "wz")
            for i in range(NT):
                normalise(2 * NT + i + 1, i)
            for t in range(TT):
                bk = wait_full(dve, "B", t)
                frees(v.tensor_tensor(CZ[:, t, :], bk[0:TR, 0:2 * D + TH], rowb[:, :], ALU.add), "B", t)
                bk = wait_full(dve, "A", t)
                frees(v.tensor_tensor(QK[:, t, :], bk[0:TR, 0:2 * D], rowa[:, :], ALU.add), "A", t)
            NH3 = 3 * TH
            def heads(ap, n):
                return ap[:, n * NH3:(n + 1) * NH3]

            def flat(x, n):
                return x[:, 3 * n:3 * n + 3, :].rearrange("p t (h c) -> p (t h) c", c=TD)

            def bc(ap):
                return ap.unsqueeze(2).broadcast_to([TR, NH3, TD])

            def rstd(n, k):
                a, b_, c_ = heads(hv[0], n), heads(hv[1], n), heads(hv[2], n)
                dve.wait_ge(tt_sq, k)
                st_.then(v.tensor_reduce(a, flat(SQ, n), AX.X, ALU.add))
                v.tensor_scalar(a, a, 1.0 / TD, 1e-6, ALU.mult, ALU.add).then_inc(tt_var, 1)
                dve.wait_ge(tt_sqrt, k)
                st_.then(v.reciprocal(b_, b_))
                st_.then(v.tensor_tensor(c_, b_, b_, ALU.mult))
                st_.then(v.tensor_tensor(c_, c_, a, ALU.mult))
                st_.then(v.tensor_scalar(c_, c_, -0.5, 1.5, ALU.mult, ALU.add))
                st_.then(v.tensor_tensor(b_, b_, c_, ALU.mult))
                return b_

            for n in range(2):
                r_ = rstd(n, n + 1)
                z = CZ[:, 3 * n:3 * n + 3, D:2 * D]
                xh, gg, sq = flat(XH, n), flat(GG, n), flat(SQ, n)
                st_.then(v.tensor_tensor(XH[:, 3 * n:3 * n + 3, :].rearrange("p t (h c) -> p t h c", c=TD),
                                         z.rearrange("p t (h c) -> p t h c", c=TD),
                                         r_.rearrange("p (t h) -> p t h", h=TH).unsqueeze(3).broadcast_to([TR, 3, TH, TD]), ALU.mult))
                st_.then(v.tensor_tensor(GG[:, 3 * n:3 * n + 3, :], XH[:, 3 * n:3 * n + 3, :],
                                         gam2[:, :].unsqueeze(1).broadcast_to([TR, 3, D]), ALU.mult))
                st_.then(v.tensor_tensor(GG[:, 3 * n:3 * n + 3, :], GG[:, 3 * n:3 * n + 3, :], CZ[:, 3 * n:3 * n + 3, 0:D], ALU.add))
                st_.do(v.tensor_tensor(sq, gg, xh, ALU.mult))
                st_.do(v.tensor_reduce(heads(hv[3], n), gg, AX.X, ALU.add))
                st_.settle()
                st_.then(v.tensor_reduce(heads(hv[4], n), sq, AX.X, ALU.add))
                st_.do(v.tensor_scalar(heads(hv[4], n), heads(hv[4], n), 1.0 / TD, None, ALU.mult))
                st_.do(v.tensor_scalar(heads(hv[3], n), heads(hv[3], n), 1.0 / TD, None, ALU.mult))
                st_.settle()
                dve.wait_ge(tt_sig, n + 1)
                st_.do(v.scalar_tensor_tensor(out=heads(hv[5], n), in0=r_, scalar=1.0 / (TD * NP),
                                              in1=sig[:, 3 * n:3 * n + 3, :].rearrange("p t h -> p (t h)"), op0=ALU.mult, op1=ALU.mult))
                st_.then(v.tensor_tensor(sq, xh, bc(heads(hv[4], n)), ALU.mult))
                st_.then(v.tensor_tensor(gg, gg, sq, ALU.subtract))
                st_.then(v.tensor_tensor(gg, gg, bc(heads(hv[3], n)), ALU.subtract))
                v.tensor_tensor(gg, gg, bc(heads(hv[5], n)), ALU.mult).then_inc(tt_g, 1)
            for t in range(TT):
                for j in range(2):
                    bk = wait_full(dve, "gW", t, j)
                    if t >= 2 and j == 0:
                        wait_full(dve, "Z", t - 2)
                    w = W1n[:, t % 2, j, :].rearrange("p (g n) -> p g n", g=G3)
                    frees(v.tensor_tensor(w, bk[0:HF, 0:G3 * HF].rearrange("p (g n) -> p g n", g=G3),
                                          bd[:, :].unsqueeze(1).broadcast_to([HF, G3, HF]), ALU.mult), "gW", t, j)
                    wait_evac(dve, "gW", t, j)
                    ins = v.tensor_tensor(w, bdw1[:, j, :].unsqueeze(1).broadcast_to([HF, G3, HF]), w, ALU.subtract)
                    if j == 0:
                        st_.do(ins)
                    else:
                        ins.then_inc(tt_w1n, 1)
                bk = wait_full(dve, "gb", t)
                frees(v.tensor_tensor(b1n[:, t % 2, :], b1c[0:G3, :], bk[0:G3, 0:D], ALU.subtract), "gb", t)
            for n in range(2):
                r_ = rstd(n, 2 + n + 1)
                xh, zb = flat(XH, n), flat(GG, n)
                st_.then(v.tensor_tensor(xh, zb, bc(r_), ALU.mult))
                x3 = XH[:, 3 * n:3 * n + 3, :]
                st_.then(v.tensor_tensor(x3, x3, row("tg", TR).unsqueeze(1).broadcast_to([TR, 3, D]), ALU.mult))
                dve.wait_ge(tt_qb, 1)
                v.tensor_tensor(x3, x3, CZ[:, 3 * n:3 * n + 3, 0:D], ALU.add).then_inc(tt_out, 1)
            dve.wait_ge(hbias, 2)
            for i in range(NT):
                r = rows_of(i)
                bk = wait_full(dve, "proj", i)
                frees(v.tensor_tensor(h[0:r, i, :], bk[0:r, 0:D], h[0:r, i, :], ALU.add), "proj", i)
                wait_evac(dve, "proj", i)
                if stage < 4:
                    st_.then(v.tensor_copy(xc[0:r, i, :], h[0:r, i, :]))
                    v.tensor_copy(h[0:r, i, :], xc[0:r, i, :]).then_inc(fin, 1)
                else:
                    stats(i, 1.0, 1e-5, (1.0 + 0.25e-6, 0.25e-11))
            if stage < 4:
                return
            for i in range(NT):
                normalise(3 * NT + i + 1, i)
            for i in range(NT):
                r = rows_of(i)
                dve.wait_ge(pow2, NT + i + 1)
                st_.then(v.tensor_scalar(xs[0:r, i, :], h[0:r, i, :], mv[0:r, i, 0:1], rs[0:r, NT + i:NT + i + 1],
                                         ALU.subtract, ALU.mult))
                st_.then(v.tensor_copy(xsp[0:r, 0, i, :], xs[0:r, i, :]))
                ins = v.tensor_tensor(xsp[0:r, 1, i, :], xs[0:r, i, :], xsp[0:r, 0, i, :], ALU.subtract)
                if i < NT - 1:
                    st_.then(ins)
            ins.then_inc(xs_done, 1)
            bk = wait_full(dve, "logits")
            dve.wait_ge(zeroed, 5)
            st_.do(v.tensor_copy(lg[:, 0:NT - 1, :], bk[:, 0:E * (NT - 1)].rearrange("p (i e) -> p i e", e=E)))
            frees(v.tensor_copy(lg[0:64, NT - 1, :], bk[0:64, E * (NT - 1):E * NT]), "logits")
            st_.settle()
            wait_evac(dve, "logits")
            for i in range(NT):
                st_.do(v.max(top[:, i, :], lg[:, i, :]))
            st_.settle()
            for i in range(NT):
                st_.do(v.max_index(topi[:, i, :], top[:, i, :], lg[:, i, :]))
            v.tensor_tensor(wts[:, :, 0], top[:, :, 1], top[:, :, 0], ALU.subtract).then_inc(lam, 1)
            st_.settle()
            st_.then(v.tensor_copy(topf[:], topi[:]))
            dve.wait_ge(loaded("iota8"), 16)
            i8 = iota8[:, :].unsqueeze(1).broadcast_to([128, NT, E])
            st_.do(v.tensor_tensor(m1[:], i8, topf[:, :, 0:1].broadcast_to([128, NT, E]), ALU.is_equal))
            st_.do(v.tensor_tensor(m2[:], i8, topf[:, :, 1:2].broadcast_to([128, NT, E]), ALU.is_equal))
            st_.settle()
            st_.do(v.tensor_tensor(mk[:], m1[:], m2[:], ALU.add))
            v.tensor_tensor(mk16[:], m1[:], m2[:], ALU.add).then_inc(mk_done, 1)
            dve.wait_ge(ex1, 1)
            st_.then(v.tensor_scalar(wts[:, :, 2], wts[:, :, 1], 1.0, None, ALU.add))
            st_.then(v.reciprocal(wts[:, :, 2], wts[:, :, 2]))
            st_.then(v.tensor_tensor(wts[:, :, 3], wts[:, :, 1], wts[:, :, 2], ALU.mult))
            st_.do(v.tensor_tensor(m1[:], m1[:], wts[:, :, 2:3].broadcast_to([128, NT, E]), ALU.mult))
            st_.do(v.tensor_tensor(m2[:], m2[:], wts[:, :, 3:4].broadcast_to([128, NT, E]), ALU.mult))
            st_.settle()
            st_.then(v.tensor_tensor(cw[:], m1[:], m2[:], ALU.add))
            st_.then(v.tensor_copy(cwp[:, 0], cw[:]))
            v.tensor_tensor(cwp[:, 1], cw[:], cwp[:, 0], ALU.subtract).then_inc(cw_done, 1)
            bk = wait_full(dve, "pos")
            st_.do(v.tensor_scalar(posf[:, 0:NT - 1, :], bk[:, 0:E * (NT - 1)].rearrange("p (i e) -> p i e", e=E), 1.0, None, ALU.add))
            frees(v.tensor_scalar(posf[0:64, NT - 1, :], bk[0:64, E * (NT - 1):E * NT], 1.0, None, ALU.add), "pos")
            st_.settle()
            wait_evac(dve, "pos")
            st_.then(v.tensor_tensor(posf[:], posf[:], mk[:], ALU.mult))
            st_.do(v.tensor_scalar(kp[:], posf[:], float(CAP), None, ALU.is_le))
            st_.do(v.tensor_scalar(posf[:], posf[:], -1.0, None, ALU.add))
            st_.settle()
            st_.do(v.tensor_tensor(kp[:], kp[:], cw[:], ALU.mult))
            v.tensor_copy(pos16[:], posf[:]).then_inc(pos_done, 1)
            st_.settle()
            st_.then(v.tensor_reduce(kw[:], kp[:], AX.X, ALU.add))
            dve.wait_ge(loaded("iota"), 16)
            dve.wait_ge(loaded("slot"), 16)

            def onehots(e):
                if e >= 2:
                    wait_full(dve, "z", e - 2)
                for i in range(NT):
                    r = rows_of(i)
                    ins = v.tensor_scalar(oh[0:r, e % 2, i, :], iota[0:r, :], posf[0:r, i, e:e + 1], None, ALU.is_equal)
                    if i < NT - 1:
                        st_.do(ins)
                ins.then_inc(oh_done, 1)

            def onehots_t(e):
                wait_evac(dve, "posb", e, 0)
                wait_evac(dve, "posb", e, 1)
                if e >= 2:
                    dve.wait_ge(pe_s, e - 1)
                st_.do(v.tensor_scalar(ohT[:, e % 2, 0, :], posb[:, :], slot[:, 0:1], None, ALU.is_equal))
                v.tensor_scalar(ohT[:, e % 2, 1, :], posb[:, :], slot[:, 1:2], None, ALU.is_equal).then_inc(oht_done, 1)

            def z_split(e):
                wait_evac(dve, "z", e)
                if e >= 1:
                    wait_full(dve, "u", e - 1, 1)
                st_.then(v.tensor_copy(zp[:, 0], zf[:, :, :]))
                v.tensor_tensor(zp[:, 1], zf[:, :, :], zp[:, 0], ALU.subtract).then_inc(z_done, 1)

            onehots(0)
            for s in range(E + 1):
                if s < E:
                    z_split(s)
                if s >= 1:
                    e = s - 1
                    bk = wait_full(dve, "y", e)
                    if e >= 1:
                        dve.wait_ge(pe_s, e)
                    for k in range(2):
                        ins = v.tensor_scalar(yf[:, k, :], bk[0:SH, D * k:D * k + D], cws[:, e % 2, k:k + 1], None, ALU.mult)
                        if k == 0:
                            st_.do(ins)
                    frees(ins, "y", e)
                    wait_evac(dve, "y", e)
                    st_.then(v.tensor_copy(yp[:, 0], yf[:, :, :]))
                    v.tensor_tensor(yp[:, 1], yf[:, :, :], yp[:, 0], ALU.subtract).then_inc(yp_done, 1)
                if s < E:
                    onehots_t(s)
                    if s + 1 < E:
                        onehots(s + 1)
                    for rnd in range(2):
                        bk = wait_full(dve, "u", s, rnd)
                        wait_evac(dve, "g", s, rnd)
                        if s >= 1 and rnd == 0:
                            dve.wait_ge(acth, s)
                            dve.wait_ge(act_done, s)
                        frees(v.tensor_tensor(actf[:, 2 * rnd:2 * rnd + 2, :], bk[:, 0:2 * CAP].rearrange("p (m n) -> p m n", m=2),
                                              sgm[:, rnd, :].rearrange("p (m n) -> p m n", m=2), ALU.mult), "u", s, rnd)
                    wait_evac(dve, "u", s, 1)
                    dve.wait_ge(acth, s + 1)
                    v.tensor_tensor(actp[:, 1], actf[:, :, :], actp[:, 0], ALU.subtract).then_inc(act_done, 1)
            for i in range(NT):
                r = rows_of(i)
                st_.do(v.scalar_tensor_tensor(out=h[0:r, i, :], in0=xc[0:r, i, :], scalar=kw[0:r, i:i + 1], in1=h[0:r, i, :],
                                              op0=ALU.mult, op1=ALU.add))
            st_.settle()
            for i in range(NT):
                r = rows_of(i)
                bk = wait_full(dve, "acc", i // 2)
                v.tensor_tensor(h[0:r, i, :], bk[0:r, D * (i % 2):D * (i % 2) + D], h[0:r, i, :], ALU.add).then_inc(fin, 1)

        @block.scalar
        def _(act):
            st_ = Steps(act, act_s)
            a = nc.scalar.activation
            act.wait_ge(loaded("cols"), 16)
            for i in range(NT):
                r = rows_of(i)
                bk = wait_full(act, "xnT", i)
                for j in range(2):
                    ins = a(xnT[:, j, 128 * i:128 * i + r], bk[0:HF, 128 * j:128 * j + r], ACT.Identity,
                            scale=cols[:, j:j + 1], bias=cols[:, 2 + j:3 + j])
                frees(ins, "xnT", i)
            for i in range(NT):
                r = rows_of(i)
                bk = wait_full(act, "v", i, 1)
                frees(a(v_sb[0:r, i, 384:768], bk[0:r, 0:384], ACT.Copy), "v", i, 1)
            for hp in range(HP):
                for n in range(2):
                    bk = wait_full(act, "q", hp, n)
                    frees(a(qT[:, hp, 288 * n:288 * n + 288], bk[:, 0:288], ACT.Copy, scale=AD ** -0.5), "q", hp, n)
            for s in range(PAIRS + 2):
                if s < PAIRS:
                    wait_evac(act, "S", s)
                    a(P[:, s % 3, :], P[:, s % 3, :], ACT.Exp).then_inc(exped, 1)
                p = s - 1
                if 0 <= p < PAIRS:
                    if p >= 2:
                        wait_full(act, "PV", p - 2)
                    for c in range(2):
                        bk = wait_full(act, "PT", p, c)
                        frees(a(PT[:, p % 2, 384 * c:384 * c + 384], bk[0:72, 0:384], ACT.Copy), "PT", p, c)
                p = s - 2
                if 0 <= p < PAIRS:
                    bk = wait_full(act, "PV", p)
                    frees(a(aoT[:, :, 72 * p:72 * p + 72], bk[:, 0:432].rearrange("p (h q) -> p h q", h=HP), ACT.Copy), "PV", p)
            if stage < 2:
                return
            moe = stage >= 4
            if moe:
                split_high(act, 0)
            for i in range(NT):
                r = rows_of(i)
                bk = wait_full(act, "xiT", i)
                frees(a(xiT[:, :, 128 * i:128 * i + r], bk[0:HF, :].bitcast(BF16)[:, 0:256].rearrange("p (j n) -> p j n", j=2)[:, :, 0:r],
                        ACT.Copy), "xiT", i)

            def yit(i):
                r = rows_of(i)
                bk = wait_full(act, "yiT", i)
                if i >= 2:
                    wait_full(act, "down", i - 2)
                frees(a(yiT[:, i % 2, :, 0:r], bk[:, :].bitcast(BF16)[:, 0:512].rearrange("p (m n) -> p m n", m=4)[:, :, 0:r],
                        ACT.Copy), "yiT", i)

            for i in range(NT):
                r = rows_of(i)
                bk = wait_full(act, "gate", i)
                if i >= 2:
                    act.wait_ge(yi_done, i - 1)
                frees(a(sg[0:r, i % 2, :], bk[0:r, :], ACT.Silu, scale=c1[0:r, i:i + 1]), "gate", i)
                wait_evac(act, "up", i)
                a(junk[0:r, :], y[0:r, i % 2, :], ACT.Square, accum_out=ssq[0:r, i:i + 1]).then_inc(sq_done, 1)
                act.wait_ge(sq_done, i + 1)
                if i >= 1:
                    yit(i - 1)
                if moe and i == 2:
                    split_high(act, 1)
            yit(NT - 1)
            if stage < 3:
                return
            if moe:
                split_high(act, 2)
            for i in range(NT):
                r = rows_of(i)
                bk = wait_full(act, "x1T", i)
                frees(a(xnT[:, :, 128 * i:128 * i + r], bk[0:HF, 0:256].rearrange("p (j n) -> p j n", j=2)[:, :, 0:r],
                        ACT.Copy), "x1T", i)
            for n in range(2):
                for t in range(3 * n, 3 * n + 3):
                    wait_evac(act, "B", t)
                a(SQ[:, 3 * n:3 * n + 3, :], CZ[:, 3 * n:3 * n + 3, D:2 * D], ACT.Square).then_inc(tt_sq, 1)
            for n in range(2):
                a(sig[:, 3 * n:3 * n + 3, :], CZ[:, 3 * n:3 * n + 3, 2 * D:], ACT.Sigmoid).then_inc(tt_sig, 1)

            def roots(k):
                n = k % 2
                act.wait_ge(tt_var, k + 1)
                a(hv[1][:, n * 36:n * 36 + 36], hv[0][:, n * 36:n * 36 + 36], ACT.Sqrt).then_inc(tt_sqrt, 1)

            roots(0)
            roots(1)
            if moe:
                split_high(act, 3)
            act.wait_ge(zeroed, 4)
            for t in range(TT):
                bk = wait_full(act, "QT", t)
                for j in range(2):
                    ins = a(q_blocks(j, t), bk[0:HF, TR * j:TR * j + TR].rearrange("p (b k) -> p b k", k=NP), ACT.Copy)
                frees(ins, "QT", t)
            act.wait_ge(loaded("bmask"), 16)

            def zb(u):
                bk = wait_full(act, "Z", u)
                wait_full(act, "gb", u)
                act.wait_ge(tt_gm, u + 1)
                frees(a(GG[:, u, :], bk[0:TR, 0:D], ACT.Copy), "Z", u)

            for t in range(TT + 1):
                if t < TT:
                    act.wait_ge(tt_g, t // 3 + 1)
                    if t >= 2:
                        wait_full(act, "gb", t - 2)
                    for b in range(G3):
                        ins = a(Gm[:, t % 2, b, :], GG[:, t, :], ACT.Copy, scale=bmask[:, b:b + 1])
                        if b < G3 - 1:
                            st_.do(ins)
                    ins.then_inc(tt_gm, 1)
                if t >= 1:
                    zb(t - 1)
                if moe and t == 3:
                    split_high(act, 4)
            for n in range(2):
                for t in range(3 * n, 3 * n + 3):
                    wait_evac(act, "Z", t)
                a(SQ[:, 3 * n:3 * n + 3, :], GG[:, 3 * n:3 * n + 3, :], ACT.Square).then_inc(tt_sq, 1)
                roots(2 + n)
            if moe:
                split_high(act, 5)
            for t in range(TT):
                bk = wait_full(act, "oT", t)
                frees(a(xnT[:, :, TR * t:TR * t + TR], bk[0:HF, 0:2 * TR].rearrange("p (j n) -> p j n", j=2), ACT.Copy), "oT", t)
            if stage < 4:
                return
            for i in range(NT):
                r = rows_of(i)
                bk = wait_full(act, "x2T", i)
                if i == 0:
                    wait_full(act, "proj", NT - 1)
                frees(a(xnT[:, :, 128 * i:128 * i + r], bk[0:HF, 0:256].rearrange("p (j n) -> p j n", j=2)[:, :, 0:r],
                        ACT.Copy), "x2T", i)
            split_high(act, 6)
            act.wait_ge(lam, 1)
            a(wts[:, :, 1], wts[:, :, 0], ACT.Exp).then_inc(ex1, 1)
            for s in range(E):
                if s >= 1:
                    act.wait_ge(oht_done, s)
                for c in range(2):
                    bk = wait_full(act, "posb", s, c)
                    n = (384, T - 384)[c]
                    frees(a(posb[:, 384 * c:384 * c + n], bk[0:SH, 0:n], ACT.Copy), "posb", s, c)
                bk = wait_full(act, "z", s)
                if s >= 1:
                    act.wait_ge(z_done, s)
                if s >= 2:
                    act.wait_ge(yp_done, s - 1)
                for j in range(2):
                    st_.do(a(zf[:, j, :], bk[0:HF, CAP * j:CAP * j + CAP], ACT.Copy, scale=nw[:, j, s:s + 1]))
                frees(a(cws[:, s % 2, :], bk[0:SH, 2 * CAP:2 * CAP + 2], ACT.Copy), "z", s)
                for rnd in range(2):
                    bk = wait_full(act, "g", s, rnd)
                    if s >= 1:
                        wait_evac(act, "u", s - 1, rnd)
                    frees(a(sgm[:, rnd, :], bk[:, 0:2 * CAP], ACT.Silu), "g", s, rnd)
                wait_evac(act, "u", s, 0)
                wait_evac(act, "u", s, 1)
                if s >= 1:
                    wait_full(act, "y", s - 1)
                a(actp[:, 0], actf[:, :, :], ACT.Copy).then_inc(acth, 1)
                if s == 0:
                    split_high(act, 7)

        @block.gpsimd
        def _(pool):
            st_ = Steps(pool, pool_s)
            g = nc.gpsimd
            g.memset(half_[:], -0.5).then_inc(pool_s, 1)
            st_.n += 1
            st_.do(g.memset(ones16[:], 1.0))
            g.memset(arenaK[:, 0:K_W], 0.0).then_inc(zeroed, 1)
            st_.settle()

            def power(sem_in, n, i, o, sem_out):
                r = rows_of(i)
                pool.wait_ge(sem_in, n)
                g.tensor_tensor(rs[0:r, o + i:o + i + 1], arg[0:r, o + i:o + i + 1], half_[0:r, 0:1], ALU.pow).then_inc(sem_out, 1)

            for i in range(NT):
                power(ln_arg, i + 1, i, 0, ln_pow)
            g.memset(arenaV[0:72, :], 0.0).then_inc(zeroed, 1)
            st_.do(g.memset(ones[:], 1.0))
            st_.do(g.memset(xnT[:, :, T:], 0.0))
            st_.settle()
            g.memset(qT[:, :, T:], 0.0).then_inc(zeroed, 1)
            pool.wait_ge(ln_x, NT)
            pool.wait_ge(loaded("rows"), 16)
            for i in range(NT):
                r = rows_of(i)
                ins = g.tensor_tensor(h[0:r, i, :], h[0:r, i, :], row("b_out", r), ALU.add)
                if i < NT - 1:
                    st_.do(ins)
            ins.then_inc(hbias, 1)
            for p in range(PAIRS):
                pool.wait_ge(rinved, p + 1)
                pv = P[:, p % 3, :].rearrange("p (h k) -> p h k", k=NP)
                g.tensor_tensor(pv, pv, ri[:, p % 2, :].unsqueeze(2).broadcast_to([128, AH, NP]), ALU.mult).then_inc(normed, 1)
            if stage < 2:
                return
            for i in range(NT):
                power(ln_arg, NT + i + 1, i, 0, ln_pow)
            if stage >= 4:
                split_low(pool, 0)
            for i in range(NT):
                power(arg2, i + 1, i, NT, pow2)
                if stage >= 4 and i == 2:
                    split_low(pool, 1)
            if stage < 3:
                return
            for i in range(NT):
                power(ln_arg, 2 * NT + i + 1, i, 0, ln_pow)
            if stage >= 4:
                split_low(pool, 2)
            wait_full(pool, "down", NT - 1)
            g.memset(QTf, 0.0).then_inc(zeroed, 1)
            pool.wait_ge(ln_x, 2 * NT)
            for i in range(NT):
                r = rows_of(i)
                ins = g.tensor_tensor(h[0:r, i, :], h[0:r, i, :], row("pb", r), ALU.add)
                if i < NT - 1:
                    st_.do(ins)
            ins.then_inc(hbias, 1)
            if stage >= 4:
                split_low(pool, 3)
            pool.wait_ge(tt_g, 2)
            for t in range(TT):
                wait_evac(pool, "A", t)
                ins = g.tensor_tensor(CZ[:, t, 0:D], QK[:, t, 0:D], row("tb", TR), ALU.add)
                if t < TT - 1:
                    st_.do(ins)
            ins.then_inc(tt_qb, 1)
            if stage < 4:
                return
            split_low(pool, 4)
            split_low(pool, 5)
            wait_full(pool, "proj", NT - 1)
            st_.then(g.memset(lg[:], 0.0))
            g.memset(posf[:], 0.0).then_inc(zeroed, 1)
            for i in range(NT):
                power(ln_arg, 3 * NT + i + 1, i, 0, ln_pow)
                power(ln_arg, 3 * NT + i + 1, i, NT, pow2)
            split_low(pool, 6)
            split_low(pool, 7)


def laid_out(x):
    c = np.ascontiguousarray

    def tiles(a, p):
        return c(a.reshape(a.shape[0] // p, p, *a.shape[1:]).swapaxes(0, 1))

    patches = x["x"].reshape(B, 3, 6, 16, 6, 16).transpose(1, 3, 5, 0, 2, 4).reshape(CPP, T)
    rows = [x["L0_tok_b_proj"], x["L0_attn_b_out"], x["L0_ffn_g_in"], x["L0_ffn_g_out"], x["L1_attn_proj_bias"],
            x["L1_attn_q_bias"], x["L1_attn_v_bias"], x["L1_attn_ttt_lr_bias"].reshape(-1),
            x["L1_attn_ttt_norm_weight"].reshape(-1), x["L1_attn_ttt_norm_bias"].reshape(-1), x["L1_attn_b1"].reshape(-1)]
    qkv = x["L1_attn_qkv_weight"]
    img = np.arange(TR) // NP
    head = np.arange(HF) // TD
    return {
        "xT": tiles(patches, 128),
        "wpT": tiles(x["L0_tok_W_proj"].T, 128),
        "rows": np.concatenate(rows),
        "cols": c(np.concatenate([x["L0_attn_gamma"].reshape(2, HF), x["L0_attn_beta"].reshape(2, HF)]).T),
        "wqkv": tiles(x["L0_attn_w_qkv"], HF),
        "woT": tiles(x["L0_attn_w_out"], 128),
        "w_in": tiles(x["L0_ffn_w_in"].T, HF),
        "w_out2": tiles(x["L0_ffn_w_out"].T, 128),
        "wa": tiles(qkv[0:2 * D].T, HF),
        "wvT": tiles(qkv[2 * D:].T, HF),
        "wkn": tiles(qkv[D:2 * D], HF),
        "lrT": tiles(x["L1_attn_ttt_lr_weight"].reshape(TH, D).T, HF),
        "w1s": tiles(x["L1_attn_W1"].reshape(D, TD), HF),
        "wpj": tiles(x["L1_attn_proj_weight"].T, HF),
        "gateT": tiles(x["L1_ffn_gate_w"].T, HF),
        "nw": tiles(x["L1_ffn_norm_w"].T, HF),
        "w13": c(x["L1_ffn_w13"].transpose(2, 0, 1).reshape(2, HF, E, 2 * FH).transpose(1, 2, 0, 3)),
        "w2": c(x["L1_ffn_w2"].transpose(2, 0, 1).reshape(4, 128, E, D).transpose(1, 2, 0, 3)),
        "idf": np.eye(128, dtype=np.float32),
        "idh": np.eye(128, dtype=np.float16),
        "tri": np.triu(np.ones((128, 128)), 1).astype(np.float16),
        "iota": c(np.broadcast_to(np.arange(CAP), (128, CAP)).astype(np.float16)),
        "iota8": c(np.broadcast_to(np.arange(E), (128, E)).astype(np.float32)),
        "slot": np.arange(CAP).reshape(2, SH).T.astype(np.float32).copy(),
        "bmask": (img[:, None] == np.arange(G3)).astype(np.float32),
        "bmaskT": c((img[:, None] == np.arange(G3)).astype(np.float32).T),
        "bd": (head[:, None] == head[None, :]).astype(np.float32),
    }


STAGE = 99


def kernel(**inputs):
    import concourse.bacc as _bacc
    from concourse.bass_utils import run_bass_kernel_spmd as _run

    nc = _bacc.Bacc("TRN2", target_bir_lowering=False, num_devices=1)
    arrays = laid_out({k: np.asarray(v) for k, v in inputs.items()})
    d = {}
    for name, a in arrays.items():
        d[name] = nc.dram_tensor(f"in_{name}", a.shape, mybir.dt.from_np(a.dtype), kind="ExternalInput").ap()
    out = nc.dram_tensor("out_0", (T, D), F32, kind="ExternalOutput").ap()
    tower(nc, d, out, STAGE)
    r = _run(nc, [{f"in_{k}": a for k, a in arrays.items()}], core_ids=[0])
    return r.results[0]["out_0"].reshape(B, NP, D)
```

```python
import math
from contextlib import ExitStack

import numpy as np

import concourse.bass as bass
from concourse import mybir

F32, BF16, F16, U32 = mybir.dt.float32, mybir.dt.bfloat16, mybir.dt.float16, mybir.dt.uint32
ALU, ACT, AX = mybir.AluOpType, mybir.ActivationFunctionType, mybir.AxisListType

B, NP, D = 16, 36, 192
T = B * NP
CPP = 768
KC = CPP // 128
NT = -(-T // 128)
HF = D // 2
AH, AD = 12, 64
HP = AH // 2
PAIRS = B // 2
FH = 512
TH, TD = 12, 16
G3 = 3
TT = -(-B // G3)
TR = G3 * NP
E, CAP = 8, int(math.ceil(1.25 * 2 * T / 8))
SH = CAP // 2
PARTS = ((0, 0), (0, 1), (1, 0))
MAGIC = 12582912.0
ROWS = {}
_at = 0
for _name, _n in [("b_proj", D), ("b_out", D), ("g_in", D), ("g_out", FH), ("pb", D), ("qb", D), ("vb", D), ("lrb", TH),
                  ("tg", D), ("tb", D), ("b1", D)]:
    ROWS[_name] = (_at, _n)
    _at += _n
NROW = _at


def rows_of(i):
    return min(128, T - 128 * i)


def tower(nc, d, out, stage=99):
    ctx = ExitStack()
    with ctx:
        def sb(name, shape, dt=F32):
            return ctx.enter_context(nc.sbuf_tensor(name, shape, dt))

        def sem(name):
            return ctx.enter_context(nc.semaphore(name))

        bank = [ctx.enter_context(nc.psum_tensor(f"bank{i}", [128, 512], F32)) for i in range(8)]
        v_scr = nc.dram_tensor("v_scratch", (T, AH * 2 * AD), F16).ap()

        V_W, K_W, WQKV_W = B * HP * 128, HP * B * 72, 2 * 3 * AH * AD
        arenaV = sb("arena_v", [128, V_W])
        arenaK = sb("arena_k", [128, K_W + WQKV_W])
        Vbd = arenaV[0:72, :].bitcast(F16).rearrange("p (b h y c x) -> p b h y c x", b=B, h=HP, y=2, x=2)
        Kbd = arenaK[:, 0:K_W].bitcast(F16).rearrange("p (x h b c) -> p x h b c", x=2, h=HP, b=B)
        wqkv = arenaK[0:HF, K_W:].bitcast(F16).rearrange("p (x j n) -> p x j n", x=2, j=2)
        xraw = arenaV[:, 0:KC * T].rearrange("p (k n) -> p k n", k=KC)
        wpraw = arenaV[:, 3456:3456 + KC * D].rearrange("p (k n) -> p k n", k=KC)
        wp16 = arenaV[:, 4608:4608 + KC * D].bitcast(F16).rearrange("p (x k n) -> p x k n", x=2, k=KC)
        wqkvraw = arenaV[0:HF, 5760:5760 + WQKV_W].rearrange("p (j n) -> p j n", j=2)
        EW13, EW2 = 2 * 2 * 2 * FH // 2, 2 * 4 * D // 2
        w13p, w2p = [], []
        for e in range(E):
            ar, o = (arenaV, e) if e < 4 else (arenaK, e - 4)
            o *= EW13 + EW2
            w13p.append(ar[0:HF, o:o + EW13].bitcast(F16).rearrange("p (x j n) -> p x j n", x=2, j=2))
            w2p.append(ar[:, o + EW13:o + EW13 + EW2].bitcast(F16).rearrange("p (x m n) -> p x m n", x=2, m=4))

        A2W = 16000
        arena = sb("arena_2", [128, A2W])

        def carve(at, *dims, rows=128, dt=F32):
            n = int(np.prod(dims))
            w = n if dt == F32 else (n + 1) // 2
            assert at[0] + w <= A2W, (at, w)
            v = arena[0:rows, at[0]:at[0] + w]
            at[0] += w
            if dt != F32:
                v = v.bitcast(dt)
            if len(dims) == 2:
                v = v.rearrange("p (a b) -> p a b", a=dims[0])
            if len(dims) == 3:
                v = v.rearrange("p (a b c) -> p a b c", a=dims[0], b=dims[1])
            if len(dims) == 4:
                v = v.rearrange("p (a b c e) -> p a b c e", a=dims[0], b=dims[1], c=dims[2])
            return v

        at = [0]
        xpT = carve(at, 2, KC, T, dt=F16)
        aoT = xpT
        x16 = carve([0], 2, 2, T, rows=HF, dt=F16)
        v_sb = carve(at, NT, AH, AD, 2, dt=F16)
        qT = carve(at, 2, HP, T + 64 - NP, dt=F16)
        woT = carve(at, 2, HP, D, dt=F16)
        P = carve(at, 3, 432)
        P16 = carve(at, 2, 2, 432, dt=F16)
        PT = carve(at, 2, 2, 768, rows=72, dt=F16)
        at = [KC * T]
        y = carve(at, 3, FH)
        sg = carve(at, 4, FH)
        junk = carve(at, FH)
        yi = carve(at, 2, FH, dt=BF16)
        yiT = carve(at, 2, 4, 128, dt=BF16)
        xi = carve(at, NT, D, dt=BF16)
        xiT = carve(at, 2, T, rows=HF, dt=BF16)
        at = [0]
        QK = carve(at, TT, 2 * D, rows=TR)
        CZ = carve(at, TT, 2 * D + TH, rows=TR)
        XH = carve(at, TT, D, rows=TR)
        GG = carve(at, TT, D, rows=TR)
        SQ = carve(at, TT, D, rows=TR)
        Gm = carve(at, 2, G3, D, rows=TR)
        QTW = G3 * TR
        QTf = carve(at, 2 * TT * QTW + TR, rows=HF)
        W1n = carve(at, 2, 2, G3 * HF, rows=HF)
        b1n = carve(at, 2, D, rows=G3)
        rowa, rowb = carve(at, 2 * D, rows=TR), carve(at, 2 * D + TH, rows=TR)
        gam2, b1c = carve(at, D, rows=TR), carve(at, D, rows=TR)
        at = [0]
        xs = carve(at, NT, D)
        xsp = carve(at, 2, NT, D, dt=F16)
        oh = carve(at, 2, NT, CAP, dt=F16)
        ohT = carve(at, 2, 2, T, rows=SH, dt=F16)
        posb = carve(at, T, rows=SH, dt=F16)
        zf = carve(at, 2, CAP, rows=HF)
        zp = carve(at, 2, 2, CAP, rows=HF, dt=F16)
        sgm = carve(at, 2, 2 * CAP)
        actf = carve(at, 4, CAP)
        actp = carve(at, 2, 4, CAP, dt=F16)
        yp = carve(at, 2, 2, D, rows=SH, dt=F16)
        yf = carve(at, 2, D, rows=SH)
        lg = carve(at, NT, E)
        top, topf = carve(at, NT, 8), carve(at, NT, 8)
        topi = carve(at, NT, 8).bitcast(U32)
        m1, m2, mk = carve(at, NT, E), carve(at, NT, E), carve(at, NT, E)
        mk16, pos16 = carve(at, NT, E, dt=F16), carve(at, NT, E, dt=F16)
        posf, cw, kp = carve(at, NT, E), carve(at, NT, E), carve(at, NT, E)
        cwp = carve(at, 2, NT, E, dt=F16)
        wts = carve(at, NT, 4)

        def q_tile(j, t, b):
            o = (j * TT + t) * QTW + TR * b
            return QTf[:, o:o + TR]

        def q_blocks(j, t):
            o = (j * TT + t) * QTW
            return QTf[:, o:o + G3 * (TR + NP)].rearrange("p (b n) -> p b n", b=G3)[:, :, 0:NP]

        h = sb("h", [128, NT, D])
        xc = sb("xc", [128, NT, D])
        xnT = sb("xnT", [HF, 2, TT * TR])
        rows = sb("rows", [128, NROW])

        def row(name, r=128):
            o, n = ROWS[name]
            return rows[0:r, o:o + n]

        cols = sb("cols", [HF, 4])
        nw = sb("nw", [HF, 2, E])
        idf, idb, idh = sb("idf", [128, 128]), sb("idb", [128, 128], BF16), sb("idh", [128, 128], F16)
        tri, ones16 = sb("tri", [128, 128], F16), sb("ones16", [128, 128], F16)
        iota = sb("iota", [128, CAP], F16)
        iota8 = sb("iota8", [128, E])
        slot = sb("slot", [SH, 2])
        bmask, bmaskT = sb("bmask", [TR, G3]), sb("bmaskT", [G3, TR])
        bd = sb("bd", [HF, HF])
        stage_a, stage2 = sb("stage_a", [128, 4 * FH]), sb("stage2", [128, 4, D])
        stage13 = stage_a[0:HF, :].rearrange("p (j n) -> p j n", j=2)
        woraw = stage_a[:, 0:HP * D].rearrange("p (k n) -> p k n", k=HP)
        wiq, w2q = sb("wiq", [HF, 2, 2 * FH], BF16), sb("w2q", [128, 4, D], BF16)
        wa = sb("wa", [HF, 2, 2 * D])
        wb = sb("wb", [HF, 2, 2 * D + TH])
        wkn = sb("wkn", [HF, 2, D])
        w1s = sb("w1s", [HF, 2, TD])
        bdw1 = sb("bdw1", [HF, 2, HF])
        wpj = sb("wpj", [HF, 2, D])
        gateT = sb("gateT", [HF, 2, E])
        st, mv = sb("st", [128, NT, 6]), sb("mv", [128, NT, 2])
        arg, rs, half_ = sb("arg", [128, 2 * NT]), sb("rs", [128, 2 * NT]), sb("mhalf", [128, 2 * NT])
        mx, sm, ri = sb("mx", [128, 2, AH]), sb("sm", [128, 2, AH]), sb("ri", [128, 2, AH])
        am, c1, qs = sb("am", [128, NT]), sb("c1", [128, NT]), sb("qs", [128, NT])
        am2, c2, ssq = sb("am2", [128, NT]), sb("c2", [128, NT]), sb("ssq", [128, NT])
        wsum, mw, sw, mwd = sb("wsum", [128, 2]), sb("mw", [128, 2]), sb("sw", [128, 2]), sb("mwd", [128, 2])
        tail = 4 * (EW13 + EW2)
        hv = [arenaV[0:TR, tail + TT * TH * n:tail + TT * TH * (n + 1)] for n in range(6)]
        sig = arenaV[0:TR, tail + TT * TH * 6:tail + TT * TH * 7].rearrange("p (t h) -> p t h", t=TT)
        wmean = sb("wmean", [HF, 2])
        b1m = sb("b1m", [TR, TH])
        cws = sb("cws", [SH, 2, 2])
        ones, nmagic = sb("ones", [128, 1]), sb("nmagic", [128, 1])
        kw = sb("kw", [128, NT])

        free = [sem(f"bank{i}_evacuated") for i in range(8)]
        full = [sem(f"bank{i}_filled") for i in range(8)]
        dve_s, act_s, pool_s, pe_s = sem("dve_step"), sem("act_step"), sem("pool_step"), sem("pe_step")
        ln_arg, ln_pow, ln_x = sem("ln_arg"), sem("ln_pow"), sem("ln_x")
        ld = {}

        def loaded(name):
            if name not in ld:
                ld[name] = sem(f"loaded_{name}")
            return ld[name]

        zeroed, idb_made = sem("zeroed"), sem("identity_bf16")
        v_stored, vbd_loaded = sem("v_stored"), [sem(f"v_of_pair{p}_loaded") for p in range(PAIRS)]
        subbed, exped, rinved, normed, hbias = sem("subbed"), sem("exped"), sem("rinved"), sem("normed"), sem("hbias")
        q_ready, silu_done, y_done, sq_done, arg2, pow2, yi_done = (sem(n) for n in (
            "xi_quantised", "silu_done", "y_done", "ysq_done", "y_arg", "y_pow", "yi_quantised"))
        x_round, y_round, yg_done = sem("xi_rounded"), sem("y_rounded"), sem("y_times_g")
        wq_part, wq_sum, wq_done = sem("weight_sums"), sem("weights_rounded"), sem("weights_quantised")
        stage_free = sem("stage_free")
        bdw1_done, wz_sum = sem("bdw1_done"), sem("wz_sum")
        split_hi, split_lo = sem("split_hi"), sem("split_lo")
        x_hi, x_lo, wv_hi, wv_lo, wqk_hi, wqk_lo, wo_hi, wo_lo = (sem(n) for n in (
            "patch_hi", "patch_lo", "wv_hi", "wv_lo", "wqk_hi", "wqk_lo", "wo_hi", "wo_lo"))
        xn_f, xn_hi, xn_lo, q_hi, k_hi, v_hi, p_hi, p_lo, ao_hi = (sem(n) for n in (
            "xn_scaled", "xn_hi", "xn_lo", "q_hi", "k_hi", "v_hi", "p_hi", "p_lo", "ao_hi"))
        h_done = sem("h_done")
        tt_z, tt_sq, tt_var, tt_sqrt, tt_sig, tt_g, tt_gm = (sem(n) for n in (
            "ttt_z", "ttt_square", "ttt_var", "ttt_sqrt", "ttt_sigmoid", "ttt_grad", "ttt_masked"))
        tt_w1n, tt_qb, tt_zb, tt_out = sem("ttt_w1n"), sem("ttt_q_plus_beta"), sem("ttt_zb"), sem("ttt_out")
        mk_done, pos_done, lam, ex1, cw_done, xs_done = (sem(n) for n in (
            "mask_done", "pos_done", "logit_gap", "gap_exp", "cw_done", "xs_done"))
        oh_done, oht_done, z_f, z_done, sil, actf_done, act_done, yp_done = (sem(n) for n in (
            "onehot", "onehotT", "z_scaled", "z_split", "moe_silu", "act_f", "act_split", "y_split"))
        acth = sem("act_hi")
        fin, stored = sem("fin"), sem("stored")

        use, count = {}, [0] * 8
        ring = [0, list(range(8))]

        def plan(*key, at=None):
            if at is None:
                at = ring[1][ring[0] % len(ring[1])]
                ring[0] += 1
            use[key] = (at, count[at])
            count[at] += 1

        for i in range(NT):
            plan("embed", i)
        for i in range(NT):
            plan("xnT", i)
        for i in range(NT):
            for c in range(2):
                plan("v", i, c)
        for hp in range(HP):
            if hp == 0:
                plan("wmean")
            for n in range(2):
                plan("k", hp, n)
            for n in range(2):
                plan("q", hp, n)
        for s in range(PAIRS + 3):
            if s < PAIRS:
                plan("S", s)
            if 0 <= s - 2 < PAIRS:
                plan("PT", s - 2, 0)
                plan("PT", s - 2, 1)
            if 0 <= s - 3 < PAIRS:
                plan("PV", s - 3)
        for i in range(NT):
            plan("wo", i)
        for i in range(NT):
            plan("xiT", i)
        for i in range(NT):
            plan("gate", i)
            plan("up", i)
        plan("wz")
        for i in range(NT):
            plan("yiT", i)
            plan("down", i)
        for i in range(NT):
            plan("x1T", i)
        for t in range(TT):
            plan("B", t)
            plan("A", t)
        for t in range(TT):
            plan("QT", t)
        for t in range(TT + 1):
            if t < TT:
                plan("gW", t, 0)
                plan("gW", t, 1)
                plan("gb", t)
            if t >= 1:
                plan("Z", t - 1)
        for t in range(TT):
            plan("oT", t)
        for i in range(NT):
            plan("proj", i)
        for i in range(NT):
            plan("x2T", i)
        plan("logits")
        plan("pos")
        ring = [0, [3, 4, 5, 6, 7]]
        for b in range(3):
            plan("acc", b, at=b)
        for s in range(E + 1):
            if s < E:
                plan("posb", s, 0)
                plan("posb", s, 1)
                plan("z", s)
            if s >= 1:
                plan("y", s - 1)
            if s < E:
                for r in range(2):
                    plan("g", s, r)
                    plan("u", s, r)

        def at_bank(*key):
            return bank[use[key][0]]

        def claim(eng, *key):
            b, n = use[key]
            if n:
                eng.wait_ge(free[b], n)
            return bank[b]

        def wait_full(eng, *key):
            b, n = use[key]
            eng.wait_ge(full[b], n + 1)
            return bank[b]

        def wait_evac(eng, *key):
            b, n = use[key]
            eng.wait_ge(free[b], n + 1)

        def fills(ins, *key):
            ins.then_inc(full[use[key][0]], 1)

        def frees(ins, *key):
            ins.then_inc(free[use[key][0]], 1)

        class Steps:

            def __init__(self, eng, s):
                self.eng, self.s, self.n = eng, s, 0

            def do(self, ins):
                ins.then_inc(self.s, 1)
                self.n += 1

            def settle(self):
                if self.n:
                    self.eng.wait_ge(self.s, self.n)

            def then(self, ins):
                self.do(ins)
                self.settle()

        def split_high(act, e):
            if e == 0:
                wait_full(act, "PV", PAIRS - 1)
            act.wait_ge(loaded("e13"), 16 * (e + 1))
            act.wait_ge(loaded("e2"), 16 * (e + 1))
            nc.scalar.activation(w13p[e][:, 0], stage13, ACT.Copy).then_inc(split_hi, 1)
            nc.scalar.activation(w2p[e][:, 0], stage2[:], ACT.Copy).then_inc(split_hi, 1)

        def split_low(pool, e):
            pool.wait_ge(split_hi, 2 * e + 2)
            nc.gpsimd.tensor_tensor(w13p[e][:, 1], stage13, w13p[e][:, 0], ALU.subtract).then_inc(split_lo, 1)
            nc.gpsimd.tensor_tensor(w2p[e][:, 1], stage2[:], w2p[e][:, 0], ALU.subtract).then_inc(split_lo, 1)

        block = ctx.enter_context(nc.Block())

        @block.sync
        def _(sp):
            def load(dst, name, src=None):
                sp.dma_start(dst, d[name] if src is None else src).then_inc(loaded(name), 16)

            for k in range(KC):
                sp.dma_start(xraw[:, k, :], d["xT"][:, k, :]).then_inc(loaded(f"x{k}"), 16)
                sp.dma_start(wpraw[:, k, :], d["wpT"][:, k, :]).then_inc(loaded(f"x{k}"), 16)
            load(rows[:], "rows", d["rows"].partition_broadcast(128))
            load(idf[:], "idf")
            load(cols[:], "cols")
            load(idh[:], "idh")
            for name, o in (("wv", 2 * AH * AD), ("wk", AH * AD), ("wq", 0)):
                load(wqkvraw[:, :, o:o + AH * AD], name, d["wqkv"][:, :, o:o + AH * AD])
            load(stage13, "w_in")
            load(stage2[:], "w_out2")
            for name, t in [("tri", tri), ("iota", iota), ("iota8", iota8), ("slot", slot),
                            ("bmask", bmask), ("bmaskT", bmaskT), ("bd", bd), ("nw", nw), ("wvT", wb[:, :, D:2 * D]),
                            ("wkn", wkn), ("w1s", w1s), ("wpj", wpj), ("gateT", gateT)]:
                load(t if name == "wvT" else t[:], name)
            load(wa[:], "wa")
            load(wb[:, :, 2 * D:], "lrT")
            for i in range(NT):
                r = rows_of(i)
                wait_evac(sp, "v", i, 0)
                wait_evac(sp, "v", i, 1)
                sp.dma_start(v_scr[128 * i:128 * i + r, :], v_sb[0:r, i].rearrange("p h c x -> p (h c x)")).then_inc(v_stored, 16)
            sp.wait_ge(v_stored, 16 * NT)
            sp.wait_ge(zeroed, 2)
            src = v_scr.rearrange("(b k) (h y n) -> y k b h n", k=NP, h=HP, y=2)
            for b in range(B):
                for y_ in range(2):
                    sp.dma_start(Vbd[NP * y_:NP * y_ + NP, b, :, y_].rearrange("p h c x -> p h (c x)"),
                                 src[y_, :, b]).then_inc(vbd_loaded[b // 2], 16)
            sp.wait_ge(wq_done, 2)
            load(woraw, "woT")
            if stage >= 4:
                for e in range(E):
                    if e == 0:
                        sp.wait_ge(wo_lo, 1)
                    if e:
                        sp.wait_ge(split_lo, 2 * e)
                        sp.wait_ge(split_hi, 2 * e)
                    sp.dma_start(stage13, d["w13"][:, e]).then_inc(loaded("e13"), 16)
                    sp.dma_start(stage2[:], d["w2"][:, e]).then_inc(loaded("e2"), 16)
            for i in range(NT):
                r = rows_of(i)
                sp.wait_ge(fin, i + 1)
                sp.dma_start(out[128 * i:128 * i + r, :], h[0:r, i, :]).then_inc(stored, 16)
            sp.wait_ge(stored, 16 * NT)
            for name in ("rows", "idf", "cols", "wv", "wq", "wk", "w_in", "w_out2", "woT", "idh", "tri", "iota", "iota8", "slot", "bmask", "bmaskT", "bd", "nw", "wvT", "wkn", "w1s", "wpj", "gateT", "wa", "lrT"):
                sp.wait_ge(loaded(name), 16)

        @block.tensor
        def _(pe):
            mm, tr = nc.tensor.matmul, nc.tensor.transpose

            for i in range(NT):
                claim(pe, "embed", i)
            for k in range(KC):
                pe.wait_ge(x_lo, 2 * k + 2)
                for i in range(NT):
                    r = rows_of(i)
                    for n, (a_, w_) in enumerate(PARTS):
                        ins = mm(at_bank("embed", i)[0:r, 0:D], xpT[:, a_, k, 128 * i:128 * i + r], wp16[:, w_, k, :],
                                 start=k == 0 and n == 0, stop=k == KC - 1 and n == 2)
                    if k == KC - 1:
                        fills(ins, "embed", i)

            pe.wait_ge(loaded("idh"), 16)

            def x_transposed(key, ln):
                pe.wait_ge(loaded("idf"), 16)
                for i in range(NT):
                    r = rows_of(i)
                    bk = claim(pe, key, i)
                    pe.wait_ge(ln_x, NT * ln + i + 1)
                    for j in range(2):
                        ins = tr(bk[0:HF, 128 * j:128 * j + r], xc[0:r, i, HF * j:HF * j + HF], idf[0:r, 0:r])
                    fills(ins, key, i)

            x_transposed("xnT", 0)
            pe.wait_ge(wv_lo, 1)
            for i in range(NT):
                r = rows_of(i)
                pe.wait_ge(xn_lo, i + 1)
                for c in range(2):
                    bk = claim(pe, "v", i, c)
                    for n, (a_, w_) in enumerate(PARTS):
                        for j in range(2):
                            ins = mm(bk[0:r, 0:384], x16[:, a_, j, 128 * i:128 * i + r],
                                     wqkv[:, w_, j, 1536 + 384 * c:1536 + 384 * c + 384], start=n + j == 0, stop=n == 2 and j == 1)
                    fills(ins, "v", i, c)
            for hp in range(HP):
                if hp == 0:
                    bk = claim(pe, "wmean")
                    pe.wait_ge(wq_part, 2)
                    pe.wait_ge(zeroed, 1)
                    mm(bk[:, 0:1], ones[0:HF, :].broadcast_to([HF, 128]), wsum[0:HF, 0:1], start=True, stop=True)
                    ins = mm(bk[:, 1:2], ones[:, :].broadcast_to([128, 128]), wsum[:, 1:2], start=True, stop=True)
                    fills(ins, "wmean")
                for key, o in (("k", AH * AD), ("q", 0)):
                    for n in range(2):
                        bk = claim(pe, key, hp, n)
                        pe.wait_ge(wqk_lo, 1 if key == "k" else 2)
                        for m, (a_, w_) in enumerate(PARTS):
                            for j in range(2):
                                ins = mm(bk[:, 0:288], wqkv[:, w_, j, o + 128 * hp:o + 128 * hp + 128],
                                         x16[:, a_, j, 288 * n:288 * n + 288], start=m + j == 0, stop=m == 2 and j == 1)
                        fills(ins, key, hp, n)
            for hp in range(HP):
                for n in range(2):
                    wait_evac(pe, "k", hp, n)
                    wait_evac(pe, "q", hp, n)
            for s in range(PAIRS + 3):
                if s < PAIRS:
                    bk = claim(pe, "S", s)
                    for x in range(2):
                        b = 2 * s + x
                        for hp in range(HP):
                            for n, (a_, w_) in enumerate(PARTS):
                                ins = mm(bk[64 * x:64 * x + 64, 72 * hp:72 * hp + 72], qT[:, a_, hp, NP * b:NP * b + 64],
                                         Kbd[:, w_, hp, b, :], start=n == 0, stop=n == 2)
                    fills(ins, "S", s)
                p = s - 2
                if 0 <= p < PAIRS:
                    for c, ready in enumerate((p_hi, p_lo)):
                        bk = claim(pe, "PT", p, c)
                        pe.wait_ge(ready, p + 1)
                        for hp in range(HP):
                            ins = tr(bk[0:72, :].bitcast(F16)[:, 128 * hp:128 * hp + 128], P16[:, p % 2, c, 72 * hp:72 * hp + 72], idh[:])
                        fills(ins, "PT", p, c)
                p = s - 3
                if 0 <= p < PAIRS:
                    wait_evac(pe, "PT", p, 0)
                    wait_evac(pe, "PT", p, 1)
                    pe.wait_ge(vbd_loaded[p], 16 * 4)
                    bk = claim(pe, "PV", p)
                    for hp in range(HP):
                        for x in range(2):
                            for n, (a_, w_) in enumerate(PARTS):
                                ins = mm(bk[:, 72 * hp + NP * x:72 * hp + NP * x + NP], Vbd[:, 2 * p + x, hp].rearrange("p y c x -> p (y c) x")[:, :, w_],
                                         PT[:, p % 2, a_, 128 * hp + 64 * x:128 * hp + 64 * x + NP], start=n == 0, stop=n == 2)
                    fills(ins, "PV", p)
            pe.wait_ge(wo_lo, 1)
            for i in range(NT):
                r = rows_of(i)
                wait_evac(pe, "PV", min(PAIRS - 1, (128 * (i + 1) - 1) // 72))
                bk = claim(pe, "wo", i)
                for hp in range(HP):
                    for n, (a_, w_) in enumerate(PARTS):
                        ins = mm(bk[0:r, 0:D], aoT[:, a_, hp, 128 * i:128 * i + r], woT[:, w_, hp, :],
                                 start=hp + n == 0, stop=hp == HP - 1 and n == 2)
                fills(ins, "wo", i)
            if stage < 2:
                return
            pe.wait_ge(idb_made, 1)
            for i in range(NT):
                r = rows_of(i)
                bk = claim(pe, "xiT", i)
                pe.wait_ge(q_ready, i + 1)
                bv = bk[0:HF, :].bitcast(BF16)
                for j in range(2):
                    ins = tr(bv[:, 128 * j:128 * j + r], xi[0:r, i, HF * j:HF * j + HF], idb[0:r, 0:r])
                fills(ins, "xiT", i)
            pe.wait_ge(wq_done, 2)
            for i in range(NT):
                r = rows_of(i)
                wait_evac(pe, "xiT", i)
                for key, o in (("gate", FH), ("up", 0)):
                    bk = claim(pe, key, i)
                    for j in range(2):
                        ins = mm(bk[0:r, :], xiT[:, j, 128 * i:128 * i + r], wiq[:, j, o:o + FH], start=j == 0, stop=j == 1)
                    fills(ins, key, i)
            bk = claim(pe, "wz")
            pe.wait_ge(bdw1_done, 1)
            pe.wait_ge(loaded("wkn"), 16)
            for c in range(2):
                for j in range(2):
                    ins = mm(bk[0:HF, D * c + HF * j:D * c + HF * j + HF], wkn[:, j, HF * c:HF * c + HF], bdw1[:, j, :],
                             start=True, stop=True)
            fills(ins, "wz")
            for i in range(NT):
                r = rows_of(i)
                bk = claim(pe, "yiT", i)
                pe.wait_ge(yi_done, i + 1)
                bv = bk[:, :].bitcast(BF16)
                for m in range(4):
                    ins = tr(bv[:, 128 * m:128 * m + r], yi[0:r, i % 2, 128 * m:128 * m + 128], idb[0:r, 0:r])
                fills(ins, "yiT", i)
                wait_evac(pe, "yiT", i)
                bk = claim(pe, "down", i)
                for m in range(4):
                    ins = mm(bk[0:r, 0:D], yiT[:, i % 2, m, 0:r], w2q[:, m, :], start=m == 0, stop=m == 3)
                fills(ins, "down", i)
            if stage < 3:
                return
            x_transposed("x1T", 1)
            wait_evac(pe, "wz")
            pe.wait_ge(loaded("wa"), 16)
            pe.wait_ge(loaded("lrT"), 16)
            for i in range(NT):
                wait_evac(pe, "x1T", i)
            for t in range(TT):
                for key, w, n in (("B", wb, 2 * D + TH), ("A", wa, 2 * D)):
                    bk = claim(pe, key, t)
                    for j in range(2):
                        ins = mm(bk[0:TR, 0:n], xnT[:, j, TR * t:TR * t + TR], w[:, j, :], start=j == 0, stop=j == 1)
                    fills(ins, key, t)
            for t in range(TT):
                wait_evac(pe, "A", t)
                bk = claim(pe, "QT", t)
                for j in range(2):
                    ins = tr(bk[0:HF, TR * j:TR * j + TR], QK[:, t, HF * j:HF * j + HF], idf[0:TR, 0:TR])
                fills(ins, "QT", t)
            pe.wait_ge(loaded("bmask"), 16)
            pe.wait_ge(loaded("bmaskT"), 16)
            for t in range(TT + 1):
                if t < TT:
                    pe.wait_ge(tt_gm, t + 1)
                    for j in range(2):
                        bk = claim(pe, "gW", t, j)
                        ins = mm(bk[0:HF, 0:G3 * HF], QK[:, t, D + HF * j:D + HF * j + HF], Gm[:, t % 2, :, HF * j:HF * j + HF],
                                 start=True, stop=True)
                        fills(ins, "gW", t, j)
                    bk = claim(pe, "gb", t)
                    ins = mm(bk[0:G3, 0:D], bmask[:, :], GG[:, t, :], start=True, stop=True)
                    fills(ins, "gb", t)
                u = t - 1
                if u >= 0:
                    wait_evac(pe, "QT", u)
                    wait_evac(pe, "gW", u, 0)
                    wait_evac(pe, "gb", u)
                    pe.wait_ge(tt_w1n, u + 1)
                    bk = claim(pe, "Z", u)
                    for j in range(2):
                        for b in range(G3):
                            mm(bk[0:TR, HF * j:HF * j + HF], q_tile(j, u, b),
                               W1n[:, u % 2, j, HF * b:HF * b + HF], start=b == 0, stop=False)
                        ins = mm(bk[0:TR, HF * j:HF * j + HF], bmaskT[:, :], b1n[:, u % 2, HF * j:HF * j + HF],
                                 start=False, stop=True)
                    fills(ins, "Z", u)
            for t in range(TT):
                pe.wait_ge(tt_out, t // 3 + 1)
                bk = claim(pe, "oT", t)
                for j in range(2):
                    ins = tr(bk[0:HF, TR * j:TR * j + TR], XH[:, t, HF * j:HF * j + HF], idf[0:TR, 0:TR])
                fills(ins, "oT", t)
            pe.wait_ge(loaded("wpj"), 16)
            for i in range(NT):
                r = rows_of(i)
                wait_evac(pe, "oT", min(TT - 1, (128 * (i + 1) - 1) // TR))
                bk = claim(pe, "proj", i)
                for j in range(2):
                    ins = mm(bk[0:r, 0:D], xnT[:, j, 128 * i:128 * i + r], wpj[:, j, :], start=j == 0, stop=j == 1)
                fills(ins, "proj", i)
            if stage < 4:
                return
            x_transposed("x2T", 2)
            pe.wait_ge(loaded("gateT"), 16)
            bk = claim(pe, "logits")
            for i in range(NT):
                r = rows_of(i)
                wait_evac(pe, "x2T", i)
                for j in range(2):
                    ins = mm(bk[0:r, E * i:E * i + E], xnT[:, j, 128 * i:128 * i + r], gateT[:, j, :], start=j == 0, stop=j == 1)
            fills(ins, "logits")
            bk = claim(pe, "pos")
            pe.wait_ge(mk_done, 1)
            pe.wait_ge(loaded("tri"), 16)
            for i in range(NT):
                r = rows_of(i)
                for k in range(i + 1):
                    ins = mm(bk[0:r, E * i:E * i + E], (tri if k == i else ones16)[0:rows_of(k), 0:r],
                             mk16[0:rows_of(k), k, :], start=k == 0, stop=k == i)
            fills(ins, "pos")
            pe.wait_ge(xs_done, 1)
            pe.wait_ge(cw_done, 1)
            pe.wait_ge(pos_done, 1)
            for b in range(3):
                bk = claim(pe, "acc", b)
                r, n = (128, 2 * D) if b < 2 else (T - 512, D)
                mm(bk[0:r, 0:n], tri[:, 0:1].broadcast_to([128, r]), tri[:, 0:1].broadcast_to([128, n]), start=True, stop=False)

            def dispatch(e):
                for c in range(2):
                    bk = claim(pe, "posb", e, c)
                    for i in ((0, 1, 2), (3, 4))[c]:
                        r = rows_of(i)
                        o = 128 * (i - 3 * c)
                        ins = mm(bk[0:SH, o:o + r], pos16[0:r, i, e:e + 1].broadcast_to([r, SH]), idh[0:r, 0:r],
                                 start=True, stop=True)
                    fills(ins, "posb", e, c)
                bk = claim(pe, "z", e)
                pe.wait_ge(oh_done, e + 1)
                for j in range(2):
                    for i in range(NT):
                        r = rows_of(i)
                        for x in range(2):
                            ins = mm(bk[0:HF, CAP * j:CAP * j + CAP], xsp[0:r, x, i, HF * j:HF * j + HF],
                                     oh[0:r, e % 2, i, :], start=i == 0 and x == 0, stop=i == NT - 1 and x == 1)
                for s in range(2):
                    for i in range(NT):
                        r = rows_of(i)
                        for x in range(2):
                            ins = mm(bk[0:SH, 2 * CAP + s:2 * CAP + s + 1], oh[0:r, e % 2, i, SH * s:SH * s + SH],
                                     cwp[0:r, x, i, e:e + 1], start=i == 0 and x == 0, stop=i == NT - 1 and x == 1)
                fills(ins, "z", e)

            def up_gate(e):
                pe.wait_ge(z_done, e + 1)
                pe.wait_ge(split_hi, 2 * e + 2)
                pe.wait_ge(split_lo, 2 * e + 2)
                for rnd in range(2):
                    for key, o in (("g", 0), ("u", FH)):
                        bk = claim(pe, key, e, rnd)
                        for m in range(2):
                            f = o + 128 * (2 * rnd + m)
                            n = 0
                            for wx, zx in ((0, 0), (0, 1), (1, 0)):
                                for j in range(2):
                                    ins = mm(bk[:, CAP * m:CAP * m + CAP], w13p[e][:, wx, j, f:f + 128], zp[:, zx, j, :],
                                             start=n == 0, stop=n == 5)
                                    n += 1
                        fills(ins, key, e, rnd)

            def down(e):
                pe.wait_ge(act_done, e + 1)
                bk = claim(pe, "y", e)
                for s in range(2):
                    n = 0
                    for m in range(4):
                        for wx, ax in ((0, 0), (0, 1), (1, 0)):
                            ins = mm(bk[0:SH, D * s:D * s + D], actp[:, ax, m, SH * s:SH * s + SH], w2p[e][:, wx, m, :],
                                     start=n == 0, stop=n == 11)
                            n += 1
                fills(ins, "y", e)

            def combine(e):
                pe.wait_ge(yp_done, e + 1)
                pe.wait_ge(oht_done, e + 1)
                for i in range(NT):
                    r = rows_of(i)
                    for s in range(2):
                        for x in range(2):
                            ins = mm(bank[i // 2][0:r, D * (i % 2):D * (i % 2) + D], ohT[:, e % 2, s, 128 * i:128 * i + r],
                                     yp[:, x, s, :], start=False,
                                     stop=e == E - 1 and s == 1 and x == 1 and (i % 2 == 1 or i == NT - 1))
                    if e == E - 1 and (i % 2 == 1 or i == NT - 1):
                        fills(ins, "acc", i // 2)
                if e < E - 1:
                    ins.then_inc(pe_s, 1)

            for s in range(E + 1):
                if s < E:
                    dispatch(s)
                if s >= 1:
                    down(s - 1)
                if s < E:
                    up_gate(s)
                if s >= 1:
                    combine(s - 1)

        @block.vector
        def _(dve):
            st_ = Steps(dve, dve_s)
            v = nc.vector

            def stats(i, A, c, second=None):
                r = rows_of(i)
                st_.then(v.bn_stats(st[0:r, i, :], h[0:r, i, :]))
                st_.then(v.bn_aggr(mv[0:r, i, :], st[0:r, i, :]))
                if second:
                    st_.do(v.tensor_scalar(arg[0:r, NT + i:NT + i + 1], mv[0:r, i, 1:2], *second, ALU.mult, ALU.add))
                v.tensor_scalar(arg[0:r, i:i + 1], mv[0:r, i, 1:2], A, c, ALU.mult, ALU.add).then_inc(ln_arg, 1)

            def normalise(n, i, last=True):
                r = rows_of(i)
                dve.wait_ge(ln_pow, n)
                ins = v.tensor_scalar(xc[0:r, i, :], h[0:r, i, :], mv[0:r, i, 0:1], rs[0:r, i:i + 1], ALU.subtract, ALU.mult)
                if last:
                    ins.then_inc(ln_x, 1)
                return ins

            for k in range(KC):
                dve.wait_ge(x_hi, 2 * k + 2)
                v.tensor_tensor(xpT[:, 1, k, :], xraw[:, k, :], xpT[:, 0, k, :], ALU.subtract).then_inc(x_lo, 1)
                v.tensor_tensor(wp16[:, 1, k, :], wpraw[:, k, :], wp16[:, 0, k, :], ALU.subtract).then_inc(x_lo, 1)
            dve.wait_ge(loaded("rows"), 16)
            for i in range(NT):
                r = rows_of(i)
                bk = wait_full(dve, "embed", i)
                frees(v.tensor_tensor(h[0:r, i, :], bk[0:r, 0:D], row("b_proj", r), ALU.add), "embed", i)
                wait_evac(dve, "embed", i)
                stats(i, 1.0 + 1e-5, 1e-10)
                if i >= 1:
                    normalise(i, i - 1)
            normalise(NT, NT - 1)
            dve.wait_ge(wv_hi, 1)
            v.tensor_tensor(wqkv[:, 1, :, 1536:], wqkvraw[:, :, 1536:], wqkv[:, 0, :, 1536:], ALU.subtract).then_inc(wv_lo, 1)
            for i in range(NT):
                r = rows_of(i)
                dve.wait_ge(xn_hi, i + 1)
                v.tensor_tensor(x16[:, 1, :, 128 * i:128 * i + r], xnT[:, :, 128 * i:128 * i + r],
                                x16[:, 0, :, 128 * i:128 * i + r], ALU.subtract).then_inc(xn_lo, 1)
            dve.wait_ge(loaded("w_in"), 16)
            dve.wait_ge(loaded("w_out2"), 16)
            v.tensor_reduce(wsum[0:HF, 0:1], stage13[:, :, :], AX.XY, ALU.add, apply_absolute_value=True).then_inc(wq_part, 1)
            v.tensor_reduce(wsum[:, 1:2], stage2[:, :, :], AX.XY, ALU.add, apply_absolute_value=True).then_inc(wq_part, 1)
            for i in range(NT):
                r = rows_of(i)
                for c in range(2):
                    bk = wait_full(dve, "v", i, c)
                    dve.wait_ge(v_hi, 2 * i + c + 1)
                    frees(v.tensor_tensor(v_sb[0:r, i, 6 * c:6 * c + 6, :, 1], bk[0:r, 0:384].rearrange("p (h c) -> p h c", h=6),
                                          v_sb[0:r, i, 6 * c:6 * c + 6, :, 0], ALU.subtract), "v", i, c)

            dve.wait_ge(loaded("idf"), 16)
            v.tensor_copy(idb[:], idf[:]).then_inc(idb_made, 1)

            bk = wait_full(dve, "wmean")
            st_.do(v.tensor_scalar(mw[:, 0:1], bk[:, 0:1], 1.0 / (2 * FH * D), 1e-5, ALU.mult, ALU.max))
            frees(v.tensor_scalar(mw[:, 1:2], bk[:, 1:2], 1.0 / (FH * D), 1e-5, ALU.mult, ALU.max), "wmean")
            st_.settle()
            wait_evac(dve, "wmean")
            st_.do(v.reciprocal(sw[:], mw[:]))
            st_.then(v.tensor_scalar(mwd[:], mw[:], 1.0 / 127.0, None, ALU.mult))
            for hp in range(HP):
                if hp == 2:
                    st_.then(v.tensor_scalar(stage2[:], stage2[:], sw[:, 1:2], 1.0, ALU.mult, ALU.min))
                    v.tensor_scalar(stage2[:], stage2[:], -1.0, MAGIC, ALU.max, ALU.add).then_inc(wq_sum, 1)
                if hp == 3:
                    st_.then(v.tensor_scalar(stage13[:], stage13[:], sw[0:HF, 0:1], 1.0, ALU.mult, ALU.min))
                if hp == 4:
                    v.tensor_scalar(stage13[:], stage13[:], -1.0, MAGIC, ALU.max, ALU.add).then_inc(wq_sum, 1)
                for n in range(2):
                    bk = wait_full(dve, "k", hp, n)
                    if n == 0:
                        dve.wait_ge(zeroed, 1)
                    dve.wait_ge(k_hi, 2 * hp + n + 1)
                    for x in range(2):
                        o = slice(64 * x, 64 * x + 64)
                        ins = v.tensor_tensor(Kbd[o, 1, hp, 8 * n:8 * n + 8, NP * x:NP * x + NP],
                                              bk[o, 0:288].rearrange("p (b k) -> p b k", k=NP),
                                              Kbd[o, 0, hp, 8 * n:8 * n + 8, NP * x:NP * x + NP], ALU.subtract)
                    frees(ins, "k", hp, n)
                for n in range(2):
                    bk = wait_full(dve, "q", hp, n)
                    dve.wait_ge(q_hi, 2 * hp + n + 1)
                    o = slice(288 * n, 288 * n + 288)
                    frees(v.scalar_tensor_tensor(out=qT[:, 1, hp, o], in0=bk[:, 0:288], scalar=AD ** -0.5,
                                                 in1=qT[:, 0, hp, o], op0=ALU.mult, op1=ALU.subtract), "q", hp, n)
            for s in range(PAIRS + 3):
                p = s - 2
                if 0 <= p < PAIRS:
                    if p >= 2:
                        wait_full(dve, "PT", p - 2, 1)
                    dve.wait_ge(p_hi, p + 1)
                    v.tensor_tensor(P16[:, p % 2, 1, :], P[:, p % 3, :], P16[:, p % 2, 0, :], ALU.subtract).then_inc(p_lo, 1)
                if s < PAIRS:
                    bk = wait_full(dve, "S", s)
                    sv = bk[:, 0:432].rearrange("p (h k) -> p h k", k=NP)
                    st_.then(v.tensor_reduce(mx[:, s % 2, :], sv, AX.X, ALU.max))
                    if s >= 3:
                        dve.wait_ge(p_lo, s - 2)
                    frees(v.tensor_tensor(P[:, s % 3, :].rearrange("p (h k) -> p h k", k=NP), sv,
                                          mx[:, s % 2, :].unsqueeze(2).broadcast_to([128, AH, NP]), ALU.subtract), "S", s)
                p = s - 1
                if 0 <= p < PAIRS:
                    dve.wait_ge(exped, p + 1)
                    st_.then(v.tensor_reduce(sm[:, p % 2, :], P[:, p % 3, :].rearrange("p (h k) -> p h k", k=NP), AX.X, ALU.add))
                    if p >= 2:
                        dve.wait_ge(normed, p - 1)
                    v.reciprocal(ri[:, p % 2, :], sm[:, p % 2, :]).then_inc(rinved, 1)
                p = s - 2
                if 0 <= p < PAIRS:
                    bk = wait_full(dve, "PT", p, 1)
                    if p >= 2:
                        wait_full(dve, "PV", p - 2)
                    frees(v.tensor_copy(PT[:, p % 2, 1, :], bk[0:72, :].bitcast(F16)[:, 0:768]), "PT", p, 1)
                p = s - 3
                if 0 <= p < PAIRS:
                    bk = wait_full(dve, "PV", p)
                    dve.wait_ge(ao_hi, p + 1)
                    o = slice(72 * p, 72 * p + 72)
                    frees(v.tensor_tensor(aoT[:, 1, :, o], bk[:, 0:432].rearrange("p (h q) -> p h q", h=HP), aoT[:, 0, :, o],
                                          ALU.subtract), "PV", p)
            dve.wait_ge(hbias, 1)
            for i in range(NT):
                r = rows_of(i)
                bk = wait_full(dve, "wo", i)
                frees(v.tensor_tensor(h[0:r, i, :], bk[0:r, 0:D], h[0:r, i, :], ALU.add), "wo", i)
                wait_evac(dve, "wo", i)
                stats(i, 1.0 + 1e-6, 1e-11)
                if i >= 1:
                    st_.do(normalise(NT + i, i - 1, last=False))
            st_.do(normalise(2 * NT, NT - 1, last=False))
            for g0, g1 in ((0, 3), (3, NT)):
                c = slice(g0, g1)
                st_.settle()
                for i in range(g0, g1):
                    r = rows_of(i)
                    st_.do(v.tensor_tensor(xc[0:r, i, :], xc[0:r, i, :], row("g_in", r), ALU.mult))
                st_.settle()
                for i in range(g0, g1):
                    r = rows_of(i)
                    st_.do(v.tensor_reduce(am[0:r, i:i + 1], xc[0:r, i, :], AX.X, ALU.max, apply_absolute_value=True))
                st_.settle()
                st_.then(v.tensor_scalar(am[:, c], am[:, c], 1e-5, None, ALU.max))
                st_.do(v.tensor_scalar(c1[:, c], am[:, c], mwd[:, 0:1], None, ALU.mult))
                st_.then(v.reciprocal(qs[:, c], am[:, c]))
                st_.then(v.tensor_scalar(qs[:, c], qs[:, c], 127.0, None, ALU.mult))
                for i in range(g0, g1):
                    r = rows_of(i)
                    v.tensor_scalar(xc[0:r, i, :], xc[0:r, i, :], qs[0:r, i:i + 1], MAGIC, ALU.mult, ALU.add).then_inc(x_round, 1)
            for name in ("w1s", "bd", "wvT", "wa", "bmask"):
                dve.wait_ge(loaded(name), 16)
            st_.then(v.tensor_reduce(wmean[:, :], w1s[:, :, :], AX.X, ALU.add))
            st_.then(v.tensor_scalar(wmean[:, :], wmean[:, :], 1.0 / TD, None, ALU.mult))
            st_.then(v.tensor_tensor(w1s[:, :, :], w1s[:, :, :], wmean[:, :].unsqueeze(2).broadcast_to([HF, 2, TD]), ALU.subtract))
            for j in range(2):
                ins = v.tensor_tensor(bdw1[:, j, :].rearrange("p (a b) -> p a b", b=TD),
                                      w1s[:, j, :].unsqueeze(1).broadcast_to([HF, HF // TD, TD]),
                                      bd[:, :].rearrange("p (a b) -> p a b", b=TD), ALU.mult)
                if j == 0:
                    st_.do(ins)
            ins.then_inc(bdw1_done, 1)
            st_.do(v.tensor_tensor(wb[:, :, 0:D], wa[:, :, D:2 * D], wb[:, :, D:2 * D], ALU.subtract))
            st_.do(v.tensor_tensor(gam2[:], row("tg", TR), row("tg", TR), ALU.mult))
            st_.do(v.tensor_copy(rowa[:, 0:D], row("qb", TR)))
            st_.do(v.memset(rowa[:, D:2 * D], 0.0))
            st_.do(v.tensor_tensor(rowb[:, 0:D], row("tb", TR), row("vb", TR), ALU.subtract))
            st_.do(v.tensor_reduce(b1m[:], row("b1", TR).rearrange("p (a b) -> p a b", b=TD), AX.X, ALU.add))
            st_.do(v.tensor_copy(rowb[:, 2 * D:], row("lrb", TR)))
            st_.settle()
            st_.do(v.tensor_scalar(b1m[:], b1m[:], 1.0 / TD, None, ALU.mult))
            st_.do(v.tensor_tensor(rowb[:, 0:D], rowb[:, 0:D], row("tg", TR), ALU.mult))
            for j in range(2):
                st_.do(v.tensor_tensor(wb[:, j, 0:D], wb[:, j, 0:D], row("tg", HF), ALU.mult))
            st_.settle()
            st_.then(v.tensor_tensor(b1c[:].rearrange("p (a b) -> p a b", b=TD), row("b1", TR).rearrange("p (a b) -> p a b", b=TD),
                                     b1m[:].unsqueeze(2).broadcast_to([TR, TH, TD]), ALU.subtract))
            st_.then(v.tensor_copy(rowb[:, D:2 * D], b1c[:]))
            for s in range(NT + 4):
                if s < NT:
                    i, r = s, rows_of(s)
                    bk = wait_full(dve, "up", i)
                    wait_evac(dve, "gate", i)
                    if i >= 3:
                        dve.wait_ge(sq_done, i - 2)
                        dve.wait_ge(yg_done, i - 2)
                    frees(v.scalar_tensor_tensor(out=y[0:r, i % 3, :], in0=bk[0:r, :], scalar=c1[0:r, i:i + 1],
                                                 in1=sg[0:r, i % 4, :], op0=ALU.mult, op1=ALU.mult), "up", i)
                if 0 <= s - 2 < NT:
                    i, r = s - 2, rows_of(s - 2)
                    dve.wait_ge(pow2, i + 1)
                    st_.settle()
                    rr = rs[0:r, NT + i:NT + i + 1]
                    st_.then(v.tensor_scalar(am2[0:r, i:i + 1], am2[0:r, i:i + 1], rr, 1e-5, ALU.mult, ALU.max))
                    st_.do(v.tensor_scalar(c2[0:r, i:i + 1], am2[0:r, i:i + 1], mwd[0:r, 1:2], None, ALU.mult))
                    st_.then(v.reciprocal(qs[0:r, i:i + 1], am2[0:r, i:i + 1]))
                    st_.then(v.tensor_scalar(qs[0:r, i:i + 1], qs[0:r, i:i + 1], 127.0, rr, ALU.mult, ALU.mult))
                    v.tensor_scalar(sg[0:r, i % 4, :], sg[0:r, i % 4, :], qs[0:r, i:i + 1], MAGIC, ALU.mult, ALU.add).then_inc(y_round, 1)
                if 0 <= s - 1 < NT:
                    i, r = s - 1, rows_of(s - 1)
                    dve.wait_ge(sq_done, i + 1)
                    v.tensor_scalar(arg[0:r, NT + i:NT + i + 1], ssq[0:r, i:i + 1], 1.0 / FH, 1e-6, ALU.mult, ALU.add).then_inc(arg2, 1)
                    dve.wait_ge(yg_done, i + 1)
                    st_.do(v.tensor_reduce(am2[0:r, i:i + 1], sg[0:r, i % 4, :], AX.X, ALU.max, apply_absolute_value=True))
                if s == 3:
                    bk = wait_full(dve, "wz")
                    frees(v.tensor_copy(wb[:, :, D:2 * D], bk[0:HF, 0:2 * D].rearrange("p (c n) -> p c n", c=2)), "wz")
                if 0 <= s - 4:
                    i, r = s - 4, rows_of(s - 4)
                    bk = wait_full(dve, "down", i)
                    frees(v.scalar_tensor_tensor(out=h[0:r, i, :], in0=bk[0:r, 0:D], scalar=c2[0:r, i:i + 1], in1=h[0:r, i, :],
                                                 op0=ALU.mult, op1=ALU.add), "down", i)
                    wait_evac(dve, "down", i)
                    stats(i, 1.0, 1e-5)
                    if i >= 1:
                        normalise(2 * NT + i, i - 1)
            normalise(3 * NT, NT - 1)
            for t in range(TT):
                bk = wait_full(dve, "B", t)
                frees(v.tensor_tensor(CZ[:, t, :], bk[0:TR, 0:2 * D + TH], rowb[:, :], ALU.add), "B", t)
                bk = wait_full(dve, "A", t)
                frees(v.tensor_tensor(QK[:, t, :], bk[0:TR, 0:2 * D], rowa[:, :], ALU.add), "A", t)
            NH3 = 3 * TH
            def heads(ap, n):
                return ap[:, n * NH3:(n + 1) * NH3]

            def flat(x, n):
                return x[:, 3 * n:3 * n + 3, :].rearrange("p t (h c) -> p (t h) c", c=TD)

            def bc(ap):
                return ap.unsqueeze(2).broadcast_to([TR, NH3, TD])

            def rstd(n, k):
                a, b_, c_ = heads(hv[0], n), heads(hv[1], n), heads(hv[2], n)
                dve.wait_ge(tt_sq, k)
                st_.then(v.tensor_reduce(a, flat(SQ, n), AX.X, ALU.add))
                v.tensor_scalar(a, a, 1.0 / TD, 1e-6, ALU.mult, ALU.add).then_inc(tt_var, 1)
                dve.wait_ge(tt_sqrt, k)
                st_.then(v.reciprocal(b_, b_))
                st_.then(v.tensor_tensor(c_, b_, b_, ALU.mult))
                st_.then(v.tensor_tensor(c_, c_, a, ALU.mult))
                st_.then(v.tensor_scalar(c_, c_, -0.5, 1.5, ALU.mult, ALU.add))
                st_.then(v.tensor_tensor(b_, b_, c_, ALU.mult))
                return b_

            for n in range(2):
                r_ = rstd(n, n + 1)
                z = CZ[:, 3 * n:3 * n + 3, D:2 * D]
                xh, gg, sq = flat(XH, n), flat(GG, n), flat(SQ, n)
                st_.then(v.tensor_tensor(XH[:, 3 * n:3 * n + 3, :].rearrange("p t (h c) -> p t h c", c=TD),
                                         z.rearrange("p t (h c) -> p t h c", c=TD),
                                         r_.rearrange("p (t h) -> p t h", h=TH).unsqueeze(3).broadcast_to([TR, 3, TH, TD]), ALU.mult))
                st_.then(v.tensor_tensor(GG[:, 3 * n:3 * n + 3, :], XH[:, 3 * n:3 * n + 3, :],
                                         gam2[:, :].unsqueeze(1).broadcast_to([TR, 3, D]), ALU.mult))
                st_.then(v.tensor_tensor(GG[:, 3 * n:3 * n + 3, :], GG[:, 3 * n:3 * n + 3, :], CZ[:, 3 * n:3 * n + 3, 0:D], ALU.add))
                st_.do(v.tensor_tensor(sq, gg, xh, ALU.mult))
                st_.do(v.tensor_reduce(heads(hv[3], n), gg, AX.X, ALU.add))
                st_.settle()
                st_.then(v.tensor_reduce(heads(hv[4], n), sq, AX.X, ALU.add))
                st_.do(v.tensor_scalar(heads(hv[4], n), heads(hv[4], n), 1.0 / TD, None, ALU.mult))
                st_.do(v.tensor_scalar(heads(hv[3], n), heads(hv[3], n), 1.0 / TD, None, ALU.mult))
                st_.settle()
                dve.wait_ge(tt_sig, n + 1)
                st_.do(v.scalar_tensor_tensor(out=heads(hv[5], n), in0=r_, scalar=1.0 / (TD * NP),
                                              in1=sig[:, 3 * n:3 * n + 3, :].rearrange("p t h -> p (t h)"), op0=ALU.mult, op1=ALU.mult))
                st_.then(v.tensor_tensor(sq, xh, bc(heads(hv[4], n)), ALU.mult))
                st_.then(v.tensor_tensor(gg, gg, sq, ALU.subtract))
                st_.then(v.tensor_tensor(gg, gg, bc(heads(hv[3], n)), ALU.subtract))
                v.tensor_tensor(gg, gg, bc(heads(hv[5], n)), ALU.mult).then_inc(tt_g, 1)
            for t in range(TT):
                for j in range(2):
                    bk = wait_full(dve, "gW", t, j)
                    if t >= 2 and j == 0:
                        wait_full(dve, "Z", t - 2)
                    w = W1n[:, t % 2, j, :].rearrange("p (g n) -> p g n", g=G3)
                    frees(v.tensor_tensor(w, bk[0:HF, 0:G3 * HF].rearrange("p (g n) -> p g n", g=G3),
                                          bd[:, :].unsqueeze(1).broadcast_to([HF, G3, HF]), ALU.mult), "gW", t, j)
                    wait_evac(dve, "gW", t, j)
                    ins = v.tensor_tensor(w, bdw1[:, j, :].unsqueeze(1).broadcast_to([HF, G3, HF]), w, ALU.subtract)
                    if j == 0:
                        st_.do(ins)
                    else:
                        ins.then_inc(tt_w1n, 1)
                bk = wait_full(dve, "gb", t)
                frees(v.tensor_tensor(b1n[:, t % 2, :], b1c[0:G3, :], bk[0:G3, 0:D], ALU.subtract), "gb", t)
            for n in range(2):
                r_ = rstd(n, 2 + n + 1)
                xh, zb = flat(XH, n), flat(GG, n)
                st_.then(v.tensor_tensor(xh, zb, bc(r_), ALU.mult))
                x3 = XH[:, 3 * n:3 * n + 3, :]
                st_.then(v.tensor_tensor(x3, x3, row("tg", TR).unsqueeze(1).broadcast_to([TR, 3, D]), ALU.mult))
                dve.wait_ge(tt_qb, 1)
                v.tensor_tensor(x3, x3, CZ[:, 3 * n:3 * n + 3, 0:D], ALU.add).then_inc(tt_out, 1)
            dve.wait_ge(hbias, 2)
            for i in range(NT):
                r = rows_of(i)
                bk = wait_full(dve, "proj", i)
                frees(v.tensor_tensor(h[0:r, i, :], bk[0:r, 0:D], h[0:r, i, :], ALU.add), "proj", i)
                wait_evac(dve, "proj", i)
                if stage < 4:
                    st_.then(v.tensor_copy(xc[0:r, i, :], h[0:r, i, :]))
                    v.tensor_copy(h[0:r, i, :], xc[0:r, i, :]).then_inc(fin, 1)
                else:
                    stats(i, 1.0, 1e-5, (1.0 + 0.25e-6, 0.25e-11))
            if stage < 4:
                return
            for i in range(NT):
                normalise(3 * NT + i + 1, i)
            for i in range(NT):
                r = rows_of(i)
                dve.wait_ge(pow2, NT + i + 1)
                st_.then(v.tensor_scalar(xs[0:r, i, :], h[0:r, i, :], mv[0:r, i, 0:1], rs[0:r, NT + i:NT + i + 1],
                                         ALU.subtract, ALU.mult))
                st_.then(v.tensor_copy(xsp[0:r, 0, i, :], xs[0:r, i, :]))
                ins = v.tensor_tensor(xsp[0:r, 1, i, :], xs[0:r, i, :], xsp[0:r, 0, i, :], ALU.subtract)
                if i < NT - 1:
                    st_.then(ins)
            ins.then_inc(xs_done, 1)
            bk = wait_full(dve, "logits")
            dve.wait_ge(zeroed, 4)
            st_.do(v.tensor_copy(lg[:, 0:NT - 1, :], bk[:, 0:E * (NT - 1)].rearrange("p (i e) -> p i e", e=E)))
            frees(v.tensor_copy(lg[0:64, NT - 1, :], bk[0:64, E * (NT - 1):E * NT]), "logits")
            st_.settle()
            wait_evac(dve, "logits")
            for i in range(NT):
                st_.do(v.max(top[:, i, :], lg[:, i, :]))
            st_.settle()
            for i in range(NT):
                st_.do(v.max_index(topi[:, i, :], top[:, i, :], lg[:, i, :]))
            v.tensor_tensor(wts[:, :, 0], top[:, :, 1], top[:, :, 0], ALU.subtract).then_inc(lam, 1)
            st_.settle()
            st_.then(v.tensor_copy(topf[:], topi[:]))
            dve.wait_ge(loaded("iota8"), 16)
            i8 = iota8[:, :].unsqueeze(1).broadcast_to([128, NT, E])
            st_.do(v.tensor_tensor(m1[:], i8, topf[:, :, 0:1].broadcast_to([128, NT, E]), ALU.is_equal))
            st_.do(v.tensor_tensor(m2[:], i8, topf[:, :, 1:2].broadcast_to([128, NT, E]), ALU.is_equal))
            st_.settle()
            st_.do(v.tensor_tensor(mk[:], m1[:], m2[:], ALU.add))
            v.tensor_tensor(mk16[:], m1[:], m2[:], ALU.add).then_inc(mk_done, 1)
            dve.wait_ge(ex1, 1)
            st_.then(v.tensor_scalar(wts[:, :, 2], wts[:, :, 1], 1.0, None, ALU.add))
            st_.then(v.reciprocal(wts[:, :, 2], wts[:, :, 2]))
            st_.then(v.tensor_tensor(wts[:, :, 3], wts[:, :, 1], wts[:, :, 2], ALU.mult))
            st_.do(v.tensor_tensor(m1[:], m1[:], wts[:, :, 2:3].broadcast_to([128, NT, E]), ALU.mult))
            st_.do(v.tensor_tensor(m2[:], m2[:], wts[:, :, 3:4].broadcast_to([128, NT, E]), ALU.mult))
            st_.settle()
            st_.then(v.tensor_tensor(cw[:], m1[:], m2[:], ALU.add))
            st_.then(v.tensor_copy(cwp[:, 0], cw[:]))
            v.tensor_tensor(cwp[:, 1], cw[:], cwp[:, 0], ALU.subtract).then_inc(cw_done, 1)
            bk = wait_full(dve, "pos")
            st_.do(v.tensor_scalar(posf[:, 0:NT - 1, :], bk[:, 0:E * (NT - 1)].rearrange("p (i e) -> p i e", e=E), 1.0, None, ALU.add))
            frees(v.tensor_scalar(posf[0:64, NT - 1, :], bk[0:64, E * (NT - 1):E * NT], 1.0, None, ALU.add), "pos")
            st_.settle()
            wait_evac(dve, "pos")
            st_.then(v.tensor_tensor(posf[:], posf[:], mk[:], ALU.mult))
            st_.do(v.tensor_scalar(kp[:], posf[:], float(CAP), None, ALU.is_le))
            st_.do(v.tensor_scalar(posf[:], posf[:], -1.0, None, ALU.add))
            st_.settle()
            st_.do(v.tensor_tensor(kp[:], kp[:], cw[:], ALU.mult))
            v.tensor_copy(pos16[:], posf[:]).then_inc(pos_done, 1)
            st_.settle()
            st_.then(v.tensor_reduce(kw[:], kp[:], AX.X, ALU.add))
            dve.wait_ge(loaded("iota"), 16)
            dve.wait_ge(loaded("slot"), 16)

            def onehots(e):
                if e >= 2:
                    wait_full(dve, "z", e - 2)
                for i in range(NT):
                    r = rows_of(i)
                    ins = v.tensor_scalar(oh[0:r, e % 2, i, :], iota[0:r, :], posf[0:r, i, e:e + 1], None, ALU.is_equal)
                    if i < NT - 1:
                        st_.do(ins)
                ins.then_inc(oh_done, 1)

            def onehots_t(e):
                wait_evac(dve, "posb", e, 0)
                wait_evac(dve, "posb", e, 1)
                if e >= 2:
                    dve.wait_ge(pe_s, e - 1)
                st_.do(v.tensor_scalar(ohT[:, e % 2, 0, :], posb[:, :], slot[:, 0:1], None, ALU.is_equal))
                v.tensor_scalar(ohT[:, e % 2, 1, :], posb[:, :], slot[:, 1:2], None, ALU.is_equal).then_inc(oht_done, 1)

            def z_split(e):
                wait_evac(dve, "z", e)
                if e >= 1:
                    wait_full(dve, "u", e - 1, 1)
                st_.then(v.tensor_copy(zp[:, 0], zf[:, :, :]))
                v.tensor_tensor(zp[:, 1], zf[:, :, :], zp[:, 0], ALU.subtract).then_inc(z_done, 1)

            onehots(0)
            for s in range(E + 1):
                if s < E:
                    z_split(s)
                if s >= 1:
                    e = s - 1
                    bk = wait_full(dve, "y", e)
                    if e >= 1:
                        dve.wait_ge(pe_s, e)
                    for k in range(2):
                        ins = v.tensor_scalar(yf[:, k, :], bk[0:SH, D * k:D * k + D], cws[:, e % 2, k:k + 1], None, ALU.mult)
                        if k == 0:
                            st_.do(ins)
                    frees(ins, "y", e)
                    wait_evac(dve, "y", e)
                    st_.then(v.tensor_copy(yp[:, 0], yf[:, :, :]))
                    v.tensor_tensor(yp[:, 1], yf[:, :, :], yp[:, 0], ALU.subtract).then_inc(yp_done, 1)
                if s < E:
                    onehots_t(s)
                    if s + 1 < E:
                        onehots(s + 1)
                    for rnd in range(2):
                        bk = wait_full(dve, "u", s, rnd)
                        wait_evac(dve, "g", s, rnd)
                        if s >= 1 and rnd == 0:
                            dve.wait_ge(acth, s)
                            dve.wait_ge(act_done, s)
                        frees(v.tensor_tensor(actf[:, 2 * rnd:2 * rnd + 2, :], bk[:, 0:2 * CAP].rearrange("p (m n) -> p m n", m=2),
                                              sgm[:, rnd, :].rearrange("p (m n) -> p m n", m=2), ALU.mult), "u", s, rnd)
                    wait_evac(dve, "u", s, 1)
                    dve.wait_ge(acth, s + 1)
                    v.tensor_tensor(actp[:, 1], actf[:, :, :], actp[:, 0], ALU.subtract).then_inc(act_done, 1)
            for i in range(NT):
                r = rows_of(i)
                st_.do(v.scalar_tensor_tensor(out=h[0:r, i, :], in0=xc[0:r, i, :], scalar=kw[0:r, i:i + 1], in1=h[0:r, i, :],
                                              op0=ALU.mult, op1=ALU.add))
            st_.settle()
            for i in range(NT):
                r = rows_of(i)
                bk = wait_full(dve, "acc", i // 2)
                v.tensor_tensor(h[0:r, i, :], bk[0:r, D * (i % 2):D * (i % 2) + D], h[0:r, i, :], ALU.add).then_inc(fin, 1)

        @block.scalar
        def _(act):
            st_ = Steps(act, act_s)
            a = nc.scalar.activation
            for k in range(KC):
                act.wait_ge(loaded(f"x{k}"), 32)
                a(xpT[:, 0, k, :], xraw[:, k, :], ACT.Copy).then_inc(x_hi, 1)
                a(wp16[:, 0, k, :], wpraw[:, k, :], ACT.Copy).then_inc(x_hi, 1)
            act.wait_ge(loaded("cols"), 16)
            act.wait_ge(loaded("wv"), 16)
            a(wqkv[:, 0, :, 1536:], wqkvraw[:, :, 1536:], ACT.Copy).then_inc(wv_hi, 1)
            act.wait_ge(loaded("wk"), 16)
            a(wqkv[:, 0, :, 768:1536], wqkvraw[:, :, 768:1536], ACT.Copy).then_inc(wqk_hi, 1)
            for i in range(NT):
                r = rows_of(i)
                bk = wait_full(act, "xnT", i)
                for j in range(2):
                    ins = a(xnT[:, j, 128 * i:128 * i + r], bk[0:HF, 128 * j:128 * j + r], ACT.Identity,
                            scale=cols[:, j:j + 1], bias=cols[:, 2 + j:3 + j])
                frees(ins, "xnT", i)
                wait_evac(act, "xnT", i)
                a(x16[:, 0, :, 128 * i:128 * i + r], xnT[:, :, 128 * i:128 * i + r], ACT.Copy).then_inc(xn_hi, 1)
            act.wait_ge(loaded("wq"), 16)
            a(wqkv[:, 0, :, 0:768], wqkvraw[:, :, 0:768], ACT.Copy).then_inc(wqk_hi, 1)
            for i in range(NT):
                r = rows_of(i)
                for c in range(2):
                    bk = wait_full(act, "v", i, c)
                    a(v_sb[0:r, i, 6 * c:6 * c + 6, :, 0], bk[0:r, 0:384].rearrange("p (h c) -> p h c", h=6),
                      ACT.Copy).then_inc(v_hi, 1)
            act.wait_ge(zeroed, 1)
            for hp in range(HP):
                if hp == 4:
                    act.wait_ge(wq_sum, 1)
                    a(w2q[:], stage2[:], ACT.Identity, bias=nmagic[:, 0:1]).then_inc(wq_done, 1)
                for n in range(2):
                    bk = wait_full(act, "k", hp, n)
                    for x in range(2):
                        o = slice(64 * x, 64 * x + 64)
                        ins = a(Kbd[o, 0, hp, 8 * n:8 * n + 8, NP * x:NP * x + NP],
                                bk[o, 0:288].rearrange("p (b k) -> p b k", k=NP), ACT.Copy)
                    ins.then_inc(k_hi, 1)
                for n in range(2):
                    bk = wait_full(act, "q", hp, n)
                    a(qT[:, 0, hp, 288 * n:288 * n + 288], bk[:, 0:288], ACT.Copy, scale=AD ** -0.5).then_inc(q_hi, 1)
            act.wait_ge(wq_sum, 2)
            a(wiq[:], stage13[:], ACT.Identity, bias=nmagic[0:HF, 0:1]).then_inc(wq_done, 1)
            for s in range(PAIRS + 3):
                if s < PAIRS:
                    wait_evac(act, "S", s)
                    a(P[:, s % 3, :], P[:, s % 3, :], ACT.Exp).then_inc(exped, 1)
                p = s - 2
                if 0 <= p < PAIRS:
                    if p >= 2:
                        wait_full(act, "PV", p - 2)
                    bk = wait_full(act, "PT", p, 0)
                    frees(a(PT[:, p % 2, 0, :], bk[0:72, :].bitcast(F16)[:, 0:768], ACT.Copy), "PT", p, 0)
                p = s - 1
                if 0 <= p < PAIRS:
                    act.wait_ge(normed, p + 1)
                    if p >= 2:
                        wait_full(act, "PT", p - 2, 0)
                    a(P16[:, p % 2, 0, :], P[:, p % 3, :], ACT.Copy).then_inc(p_hi, 1)
                p = s - 3
                if 0 <= p < PAIRS:
                    bk = wait_full(act, "PV", p)
                    a(aoT[:, 0, :, 72 * p:72 * p + 72], bk[:, 0:432].rearrange("p (h q) -> p h q", h=HP),
                      ACT.Copy).then_inc(ao_hi, 1)
                if s == 4:
                    act.wait_ge(loaded("woT"), 16)
                    a(woT[:, 0], woraw, ACT.Copy).then_inc(wo_hi, 1)
            if stage < 2:
                return
            moe = stage >= 4
            if moe:
                split_high(act, 0)
            for i in range(NT):
                r = rows_of(i)
                act.wait_ge(x_round, i + 1)
                a(xi[0:r, i, :], xc[0:r, i, :], ACT.Identity, bias=nmagic[0:r, 0:1]).then_inc(q_ready, 1)
            for i in range(NT):
                r = rows_of(i)
                bk = wait_full(act, "xiT", i)
                frees(a(xiT[:, :, 128 * i:128 * i + r], bk[0:HF, :].bitcast(BF16)[:, 0:256].rearrange("p (j n) -> p j n", j=2)[:, :, 0:r],
                        ACT.Copy), "xiT", i)
            for s in range(NT + 3):
                if s < NT:
                    i, r = s, rows_of(s)
                    bk = wait_full(act, "gate", i)
                    frees(a(sg[0:r, i % 4, :], bk[0:r, :], ACT.Silu, scale=c1[0:r, i:i + 1]), "gate", i)
                if 0 <= s - 1 < NT:
                    i, r = s - 1, rows_of(s - 1)
                    wait_evac(act, "up", i)
                    if i >= 1:
                        act.wait_ge(sq_done, i)
                    a(junk[0:r, :], y[0:r, i % 3, :], ACT.Square, accum_out=ssq[0:r, i:i + 1]).then_inc(sq_done, 1)
                if 0 <= s - 3:
                    i, r = s - 3, rows_of(s - 3)
                    bk = wait_full(act, "yiT", i)
                    if i >= 2:
                        wait_full(act, "down", i - 2)
                    frees(a(yiT[:, i % 2, :, 0:r], bk[:, :].bitcast(BF16)[:, 0:512].rearrange("p (m n) -> p m n", m=4)[:, :, 0:r],
                            ACT.Copy), "yiT", i)
                if 0 <= s - 2 < NT:
                    i, r = s - 2, rows_of(s - 2)
                    act.wait_ge(y_round, i + 1)
                    if i >= 2:
                        wait_full(act, "yiT", i - 2)
                    a(yi[0:r, i % 2, :], sg[0:r, i % 4, :], ACT.Identity, bias=nmagic[0:r, 0:1]).then_inc(yi_done, 1)
            if moe:
                split_high(act, 1)
            for i in range(NT):
                r = rows_of(i)
                bk = wait_full(act, "x1T", i)
                frees(a(xnT[:, :, 128 * i:128 * i + r], bk[0:HF, 0:256].rearrange("p (j n) -> p j n", j=2)[:, :, 0:r],
                        ACT.Copy), "x1T", i)
            for n in range(2):
                for t in range(3 * n, 3 * n + 3):
                    wait_evac(act, "B", t)
                a(SQ[:, 3 * n:3 * n + 3, :], CZ[:, 3 * n:3 * n + 3, D:2 * D], ACT.Square).then_inc(tt_sq, 1)
            for n in range(2):
                a(sig[:, 3 * n:3 * n + 3, :], CZ[:, 3 * n:3 * n + 3, 2 * D:], ACT.Sigmoid).then_inc(tt_sig, 1)

            def roots(k):
                n = k % 2
                act.wait_ge(tt_var, k + 1)
                a(hv[1][:, n * 36:n * 36 + 36], hv[0][:, n * 36:n * 36 + 36], ACT.Sqrt).then_inc(tt_sqrt, 1)

            roots(0)
            roots(1)
            if moe:
                split_high(act, 2)
            act.wait_ge(zeroed, 3)
            for t in range(TT):
                bk = wait_full(act, "QT", t)
                for j in range(2):
                    ins = a(q_blocks(j, t), bk[0:HF, TR * j:TR * j + TR].rearrange("p (b k) -> p b k", k=NP), ACT.Copy)
                frees(ins, "QT", t)
            act.wait_ge(loaded("bmask"), 16)

            def zb(u):
                bk = wait_full(act, "Z", u)
                wait_full(act, "gb", u)
                act.wait_ge(tt_gm, u + 1)
                frees(a(GG[:, u, :], bk[0:TR, 0:D], ACT.Copy), "Z", u)

            for t in range(TT + 1):
                if t < TT:
                    act.wait_ge(tt_g, t // 3 + 1)
                    if t >= 2:
                        wait_full(act, "gb", t - 2)
                    for b in range(G3):
                        ins = a(Gm[:, t % 2, b, :], GG[:, t, :], ACT.Copy, scale=bmask[:, b:b + 1])
                        if b < G3 - 1:
                            st_.do(ins)
                    ins.then_inc(tt_gm, 1)
                if t >= 1:
                    zb(t - 1)
                if moe and t == 3:
                    split_high(act, 3)
            for n in range(2):
                for t in range(3 * n, 3 * n + 3):
                    wait_evac(act, "Z", t)
                a(SQ[:, 3 * n:3 * n + 3, :], GG[:, 3 * n:3 * n + 3, :], ACT.Square).then_inc(tt_sq, 1)
                roots(2 + n)
            if moe:
                split_high(act, 4)
            for t in range(TT):
                bk = wait_full(act, "oT", t)
                frees(a(xnT[:, :, TR * t:TR * t + TR], bk[0:HF, 0:2 * TR].rearrange("p (j n) -> p j n", j=2), ACT.Copy), "oT", t)
            if stage < 4:
                return
            for i in range(NT):
                r = rows_of(i)
                bk = wait_full(act, "x2T", i)
                if i == 0:
                    wait_full(act, "proj", NT - 1)
                frees(a(xnT[:, :, 128 * i:128 * i + r], bk[0:HF, 0:256].rearrange("p (j n) -> p j n", j=2)[:, :, 0:r],
                        ACT.Copy), "x2T", i)
            split_high(act, 5)
            act.wait_ge(lam, 1)
            a(wts[:, :, 1], wts[:, :, 0], ACT.Exp).then_inc(ex1, 1)
            for s in range(E):
                if s >= 1:
                    act.wait_ge(oht_done, s)
                for c in range(2):
                    bk = wait_full(act, "posb", s, c)
                    n = (384, T - 384)[c]
                    frees(a(posb[:, 384 * c:384 * c + n], bk[0:SH, 0:n], ACT.Copy), "posb", s, c)
                bk = wait_full(act, "z", s)
                if s >= 1:
                    act.wait_ge(z_done, s)
                if s >= 2:
                    act.wait_ge(yp_done, s - 1)
                for j in range(2):
                    st_.do(a(zf[:, j, :], bk[0:HF, CAP * j:CAP * j + CAP], ACT.Copy, scale=nw[:, j, s:s + 1]))
                frees(a(cws[:, s % 2, :], bk[0:SH, 2 * CAP:2 * CAP + 2], ACT.Copy), "z", s)
                for rnd in range(2):
                    bk = wait_full(act, "g", s, rnd)
                    if s >= 1:
                        wait_evac(act, "u", s - 1, rnd)
                    frees(a(sgm[:, rnd, :], bk[:, 0:2 * CAP], ACT.Silu), "g", s, rnd)
                wait_evac(act, "u", s, 0)
                wait_evac(act, "u", s, 1)
                if s >= 1:
                    wait_full(act, "y", s - 1)
                a(actp[:, 0], actf[:, :, :], ACT.Copy).then_inc(acth, 1)
                if s < 2:
                    split_high(act, 6 + s)

        @block.gpsimd
        def _(pool):
            st_ = Steps(pool, pool_s)
            g = nc.gpsimd
            g.memset(half_[:], -0.5).then_inc(pool_s, 1)
            st_.n += 1
            st_.do(g.memset(ones16[:], 1.0))
            st_.do(g.memset(ones[:], 1.0))
            st_.do(g.memset(nmagic[:], -MAGIC))
            st_.do(g.memset(am[:], 0.0))
            st_.do(g.memset(xnT[:, :, T:], 0.0))
            st_.do(g.memset(qT[:, :, :, T:], 0.0))
            st_.settle()
            g.memset(arenaK[:, 0:K_W], 0.0).then_inc(zeroed, 1)

            def power(sem_in, n, i, o, sem_out):
                r = rows_of(i)
                pool.wait_ge(sem_in, n)
                g.tensor_tensor(rs[0:r, o + i:o + i + 1], arg[0:r, o + i:o + i + 1], half_[0:r, 0:1], ALU.pow).then_inc(sem_out, 1)

            for i in range(NT):
                power(ln_arg, i + 1, i, 0, ln_pow)
            for n in range(2):
                pool.wait_ge(wqk_hi, n + 1)
                o = slice(768 - 768 * n, 1536 - 768 * n)
                g.tensor_tensor(wqkv[:, 1, :, o], wqkvraw[:, :, o], wqkv[:, 0, :, o], ALU.subtract).then_inc(wqk_lo, 1)
            pool.wait_ge(wqk_lo, 2)
            pool.wait_ge(wv_lo, 1)
            wait_full(pool, "embed", NT - 1)
            g.memset(arenaV[0:72, :], 0.0).then_inc(zeroed, 1)
            pool.wait_ge(ln_x, NT)
            pool.wait_ge(loaded("rows"), 16)
            for i in range(NT):
                r = rows_of(i)
                ins = g.tensor_tensor(h[0:r, i, :], h[0:r, i, :], row("b_out", r), ALU.add)
                if i < NT - 1:
                    st_.do(ins)
            ins.then_inc(hbias, 1)
            for p in range(PAIRS):
                pool.wait_ge(rinved, p + 1)
                pv = P[:, p % 3, :].rearrange("p (h k) -> p h k", k=NP)
                g.tensor_tensor(pv, pv, ri[:, p % 2, :].unsqueeze(2).broadcast_to([128, AH, NP]), ALU.mult).then_inc(normed, 1)
                if p == 4:
                    pool.wait_ge(wo_hi, 1)
                    g.tensor_tensor(woT[:, 1], woraw, woT[:, 0], ALU.subtract).then_inc(wo_lo, 1)
            if stage < 2:
                return
            for i in range(NT):
                power(ln_arg, NT + i + 1, i, 0, ln_pow)
            if stage >= 4:
                split_low(pool, 0)
            for s in range(NT + 1):
                if s < NT:
                    i, r = s, rows_of(s)
                    wait_evac(pool, "up", i)
                    g.tensor_tensor(sg[0:r, i % 4, :], y[0:r, i % 3, :], row("g_out", r), ALU.mult).then_inc(yg_done, 1)
                if s >= 1:
                    power(arg2, s, s - 1, NT, pow2)
            for i in range(NT):
                power(ln_arg, 2 * NT + i + 1, i, 0, ln_pow)
            wait_full(pool, "down", NT - 1)
            g.memset(QTf, 0.0).then_inc(zeroed, 1)
            pool.wait_ge(ln_x, 2 * NT)
            for i in range(NT):
                r = rows_of(i)
                ins = g.tensor_tensor(h[0:r, i, :], h[0:r, i, :], row("pb", r), ALU.add)
                if i < NT - 1:
                    st_.do(ins)
            ins.then_inc(hbias, 1)
            split_low(pool, 1)
            split_low(pool, 2)
            pool.wait_ge(tt_g, 2)
            for t in range(TT):
                wait_evac(pool, "A", t)
                ins = g.tensor_tensor(CZ[:, t, 0:D], QK[:, t, 0:D], row("tb", TR), ALU.add)
                if t < TT - 1:
                    st_.do(ins)
            ins.then_inc(tt_qb, 1)
            if stage < 4:
                return
            split_low(pool, 3)
            split_low(pool, 4)
            wait_full(pool, "proj", NT - 1)
            st_.then(g.memset(lg[:], 0.0))
            g.memset(posf[:], 0.0).then_inc(zeroed, 1)
            for i in range(NT):
                power(ln_arg, 3 * NT + i + 1, i, 0, ln_pow)
                power(ln_arg, 3 * NT + i + 1, i, NT, pow2)
            split_low(pool, 5)
            split_low(pool, 6)
            split_low(pool, 7)


def laid_out(x):
    c = np.ascontiguousarray

    def tiles(a, p):
        return c(a.reshape(a.shape[0] // p, p, *a.shape[1:]).swapaxes(0, 1))

    patches = x["x"].reshape(B, 3, 6, 16, 6, 16).transpose(1, 3, 5, 0, 2, 4).reshape(CPP, T)
    rows = [x["L0_tok_b_proj"], x["L0_attn_b_out"], x["L0_ffn_g_in"], x["L0_ffn_g_out"], x["L1_attn_proj_bias"],
            x["L1_attn_q_bias"], x["L1_attn_v_bias"], x["L1_attn_ttt_lr_bias"].reshape(-1),
            x["L1_attn_ttt_norm_weight"].reshape(-1), x["L1_attn_ttt_norm_bias"].reshape(-1), x["L1_attn_b1"].reshape(-1)]
    qkv = x["L1_attn_qkv_weight"]
    img = np.arange(TR) // NP
    head = np.arange(HF) // TD
    return {
        "xT": tiles(patches, 128),
        "wpT": tiles(x["L0_tok_W_proj"].T, 128),
        "rows": np.concatenate(rows),
        "cols": c(np.concatenate([x["L0_attn_gamma"].reshape(2, HF), x["L0_attn_beta"].reshape(2, HF)]).T),
        "wqkv": tiles(x["L0_attn_w_qkv"], HF),
        "woT": tiles(x["L0_attn_w_out"], 128),
        "w_in": tiles(x["L0_ffn_w_in"].T, HF),
        "w_out2": tiles(x["L0_ffn_w_out"].T, 128),
        "wa": tiles(qkv[0:2 * D].T, HF),
        "wvT": tiles(qkv[2 * D:].T, HF),
        "wkn": tiles(qkv[D:2 * D], HF),
        "lrT": tiles(x["L1_attn_ttt_lr_weight"].reshape(TH, D).T, HF),
        "w1s": tiles(x["L1_attn_W1"].reshape(D, TD), HF),
        "wpj": tiles(x["L1_attn_proj_weight"].T, HF),
        "gateT": tiles(x["L1_ffn_gate_w"].T, HF),
        "nw": tiles(x["L1_ffn_norm_w"].T, HF),
        "w13": c(x["L1_ffn_w13"].transpose(2, 0, 1).reshape(2, HF, E, 2 * FH).transpose(1, 2, 0, 3)),
        "w2": c(x["L1_ffn_w2"].transpose(2, 0, 1).reshape(4, 128, E, D).transpose(1, 2, 0, 3)),
        "idf": np.eye(128, dtype=np.float32),
        "idh": np.eye(128, dtype=np.float16),
        "tri": np.triu(np.ones((128, 128)), 1).astype(np.float16),
        "iota": c(np.broadcast_to(np.arange(CAP), (128, CAP)).astype(np.float16)),
        "iota8": c(np.broadcast_to(np.arange(E), (128, E)).astype(np.float32)),
        "slot": np.arange(CAP).reshape(2, SH).T.astype(np.float32).copy(),
        "bmask": (img[:, None] == np.arange(G3)).astype(np.float32),
        "bmaskT": c((img[:, None] == np.arange(G3)).astype(np.float32).T),
        "bd": (head[:, None] == head[None, :]).astype(np.float32),
    }


STAGE = 99


def kernel(**inputs):
    import concourse.bacc as _bacc
    from concourse.bass_utils import run_bass_kernel_spmd as _run

    nc = _bacc.Bacc("TRN2", target_bir_lowering=False, num_devices=1)
    arrays = laid_out({k: np.asarray(v) for k, v in inputs.items()})
    d = {}
    for name, a in arrays.items():
        d[name] = nc.dram_tensor(f"in_{name}", a.shape, mybir.dt.from_np(a.dtype), kind="ExternalInput").ap()
    out = nc.dram_tensor("out_0", (T, D), F32, kind="ExternalOutput").ap()
    tower(nc, d, out, STAGE)
    r = _run(nc, [{f"in_{k}": a for k, a in arrays.items()}], core_ids=[0])
    return r.results[0]["out_0"].reshape(B, NP, D)
```

```python
import math
from contextlib import ExitStack

import numpy as np

import concourse.bass as bass
from concourse import mybir

F32, BF16, F16, U32 = mybir.dt.float32, mybir.dt.bfloat16, mybir.dt.float16, mybir.dt.uint32
ALU, ACT, AX = mybir.AluOpType, mybir.ActivationFunctionType, mybir.AxisListType

B, NP, D = 16, 36, 192
T = B * NP
CPP = 768
KC = CPP // 128
NT = -(-T // 128)
HF = D // 2
AH, AD = 12, 64
HP = AH // 2
PAIRS = B // 2
FH = 512
TH, TD = 12, 16
G3 = 3
TT = -(-B // G3)
TR = G3 * NP
E, CAP = 8, int(math.ceil(1.25 * 2 * T / 8))
SH = CAP // 2
PARTS = ((0, 0), (0, 1), (1, 0))
MAGIC = 12582912.0
ROWS = {}
_at = 0
for _name, _n in [("vb", D), ("b_proj", D), ("lrb", TH), ("b_out", D), ("g_in", D), ("g_out", FH), ("pb", D),
                  ("tg", D), ("tb", D), ("b1", D)]:
    ROWS[_name] = (_at, _n)
    _at += _n
NROW = _at


def rows_of(i):
    return min(128, T - 128 * i)


def tower(nc, d, out):
    ctx = ExitStack()
    with ctx:
        def sb(name, shape, dt=F32):
            return ctx.enter_context(nc.sbuf_tensor(name, shape, dt))

        def sem(name):
            return ctx.enter_context(nc.semaphore(name))

        bank = [ctx.enter_context(nc.psum_tensor(f"bank{i}", [128, 512], F32)) for i in range(8)]
        v_scr = nc.dram_tensor("v_scratch", (T, AH * 2 * AD), F16).ap()

        V_W, K_W, WQKV_W = B * HP * 128, HP * B * 72, 2 * 3 * AH * AD
        arenaV = sb("arena_v", [128, V_W])
        arenaK = sb("arena_k", [128, K_W + WQKV_W])
        Vbd = arenaV[0:72, :].bitcast(F16).rearrange("p (b h y c x) -> p b h y c x", b=B, h=HP, y=2, x=2)
        Kbd = arenaK[:, 0:K_W].bitcast(F16).rearrange("p (x h b c) -> p x h b c", x=2, h=HP, b=B)
        wqkv = arenaK[0:HF, K_W:].bitcast(F16).rearrange("p (x j n) -> p x j n", x=2, j=2)
        xraw = arenaV[:, 0:KC * T].rearrange("p (k n) -> p k n", k=KC)
        wpraw = arenaV[:, 3456:3456 + KC * D].rearrange("p (k n) -> p k n", k=KC)
        wp16 = arenaV[:, 4608:4608 + KC * D].bitcast(F16).rearrange("p (x k n) -> p x k n", x=2, k=KC)
        wqkvraw = arenaV[0:HF, 5760:5760 + WQKV_W].rearrange("p (j n) -> p j n", j=2)
        EW13, EW2 = 2 * 2 * 2 * FH // 2, 2 * 4 * D // 2
        w13p, w2p = [], []
        for e in range(E):
            ar, o = (arenaV, e) if e < 4 else (arenaK, e - 4)
            o *= EW13 + EW2
            w13p.append(ar[0:HF, o:o + EW13].bitcast(F16).rearrange("p (x j n) -> p x j n", x=2, j=2))
            w2p.append(ar[:, o + EW13:o + EW13 + EW2].bitcast(F16).rearrange("p (x m n) -> p x m n", x=2, m=4))

        A2W = 16000
        arena = sb("arena_2", [128, A2W])

        def carve(at, *dims, rows=128, dt=F32):
            n = int(np.prod(dims))
            w = n if dt == F32 else (n + 1) // 2
            assert at[0] + w <= A2W, (at, w)
            v = arena[0:rows, at[0]:at[0] + w]
            at[0] += w
            if dt != F32:
                v = v.bitcast(dt)
            if len(dims) == 2:
                v = v.rearrange("p (a b) -> p a b", a=dims[0])
            if len(dims) == 3:
                v = v.rearrange("p (a b c) -> p a b c", a=dims[0], b=dims[1])
            if len(dims) == 4:
                v = v.rearrange("p (a b c e) -> p a b c e", a=dims[0], b=dims[1], c=dims[2])
            return v

        at = [0]
        xpT = carve(at, 2, KC, T, dt=F16)
        aoT = xpT
        x16 = carve([0], 2, 2, T, rows=HF, dt=F16)
        v_sb = carve(at, NT, AH, AD, 2, dt=F16)
        qT = carve(at, 2, HP, T + 64 - NP, dt=F16)
        woT = carve(at, 2, HP, D, dt=F16)
        P = carve(at, 3, 432)
        P16 = carve(at, 2, 2, 432, dt=F16)
        PT = carve(at, 2, 2, 768, rows=72, dt=F16)
        at = [KC * T]
        y = carve(at, 3, FH)
        sg = carve(at, 4, FH)
        junk = carve(at, FH)
        yi = carve(at, 2, FH, dt=BF16)
        yiT = carve(at, 2, 4, 128, dt=BF16)
        xi = carve(at, NT, D, dt=BF16)
        xiT = carve(at, 2, T, rows=HF, dt=BF16)
        at = [0]
        CZ = carve(at, TT, 2 * D + TH, rows=TR)
        XH = carve(at, TT, D, rows=TR)
        GG = carve(at, TT, D, rows=TR)
        o_sq = at[0]
        SQ = carve(at, TT, D, rows=TR)
        G16 = carve([o_sq], TT, 2, D, rows=TR, dt=F16)
        E16 = carve([TT * (2 * D + TH)], TT, 2, D, rows=TR, dt=F16)
        zT = CZ[0:HF, :, 0:2 * TR].rearrange("p t (j n) -> p t j n", j=2)
        K16 = carve(at, 3, 2, D, rows=TR, dt=F16)
        KM_N, PAD = 2 * G3 * 2 * (HF + 1), 32
        KM_W = (KM_N + PAD) // 2
        o_km = at[0]
        at[0] += TT * KM_W
        Kmf = [arena[0:TR, o_km + t * KM_W:o_km + (t + 1) * KM_W].bitcast(F16) for t in range(TT)]
        Km = [f[:, 0:KM_N].rearrange("p (x b j n) -> p x b j n", x=2, b=G3, j=2) for f in Kmf]
        q16 = carve(at, 2, 2, TT * TR, rows=HF + 1, dt=F16)
        qtb = carve(at, 2, TT * TR, rows=HF)
        Wt = carve(at, 2, 2, G3 * HF, rows=HF + 1)
        W_N = 2 * 2 * G3 * HF
        W16f = carve(at, 2, W_N + PAD, rows=HF + 1, dt=F16)
        W16 = [W16f[:, u, 0:W_N].rearrange("p (x j n) -> p x j n", x=2, j=2) for u in range(2)]
        sqf, sq16 = carve(at, 2, 2 * TR, rows=HF), carve(at, 2, 2, 2 * TR, rows=HF, dt=F16)
        o_w7 = 3 * (EW13 + EW2)

        def weight_parts(n, rows=HF):
            nonlocal o_w7
            v = arenaK[0:rows, o_w7:o_w7 + 2 * n].bitcast(F16).rearrange("p (x j n) -> p x j n", x=2, j=2)
            o_w7 += 2 * n
            return v

        wa16, wb16 = weight_parts(2 * D), weight_parts(2 * D + TH)
        wpj16, base16 = weight_parts(D), weight_parts(HF, HF + 1)
        base16f = arenaK[0:HF + 1, o_w7 - 2 * HF:o_w7 + PAD // 2].bitcast(F16)
        at = [0]
        xs = carve(at, NT, D)
        xsp = carve(at, 2, NT, D, dt=F16)
        oh = carve(at, 2, NT, CAP, dt=F16)
        ohT = carve(at, 2, 2, T, rows=SH, dt=F16)
        posb = carve(at, T, rows=SH, dt=F16)
        zf = carve(at, 2, CAP, rows=HF)
        zp = carve(at, 2, 2, CAP, rows=HF, dt=F16)
        sgm = carve(at, 2, 2 * CAP)
        actf = carve(at, 4, CAP)
        actp = carve(at, 2, 4, CAP, dt=F16)
        yp = carve(at, 2, 2, D, rows=SH, dt=F16)
        yf = carve(at, 2, D, rows=SH)
        lg = carve(at, NT, E)
        top, topf = carve(at, NT, 8), carve(at, NT, 8)
        topi = carve(at, NT, 8).bitcast(U32)
        m1, m2, mk = carve(at, NT, E), carve(at, NT, E), carve(at, NT, E)
        mk16, pos16 = carve(at, NT, E, dt=F16), carve(at, NT, E, dt=F16)
        posf, cw, kp = carve(at, NT, E), carve(at, NT, E), carve(at, NT, E)
        cwp = carve(at, NT, E, 2, dt=F16)
        wts = carve(at, NT, 4)

        h = sb("h", [128, NT, D])
        xc = sb("xc", [128, NT, D])
        xnT = sb("xnT", [HF, 2, TT * TR])
        xnp = xnT[:, :, :].rearrange("p j n -> p (j n)").bitcast(F16).rearrange("p (x j n) -> p x j n", x=2, j=2)
        rows = sb("rows", [128, NROW])

        def row(name, r=128):
            o, n = ROWS[name]
            return rows[0:r, o:o + n]

        cols = sb("cols", [HF, 10])
        qbt = sb("qbt", [HF, 2])
        nw = sb("nw", [HF, 2, E])
        idf, idb, idh = sb("idf", [128, 128]), sb("idb", [128, 128], BF16), sb("idh", [128, 128], F16)
        tri, ones16 = sb("tri", [128, 128], F16), sb("ones16", [128, 128], F16)
        iota = sb("iota", [128, CAP], F16)
        iota8 = sb("iota8", [128, E])
        slot = sb("slot", [SH, 2])
        bmask = sb("bmask", [TR, G3])
        hsel = sb("hsel", [HF, 2, TH], F16)
        bd = sb("bd", [HF + 1, HF])
        stage_a, stage2 = sb("stage_a", [128, 4 * FH]), sb("stage2", [128, 4, D])
        stage13 = stage_a[0:HF, :].rearrange("p (j n) -> p j n", j=2)
        woraw = stage_a[:, 0:HP * D].rearrange("p (k n) -> p k n", k=HP)
        wiq, w2q = sb("wiq", [HF, 2, 2 * FH], BF16), sb("w2q", [128, 4, D], BF16)
        wa = sb("wa", [HF, 2, 2 * D])
        wb = sb("wb", [HF, 2, 2 * D + TH])
        wkn = sb("wkn", [HF, 2, D])
        w1s = sb("w1s", [HF, 2, TD])
        bdw1 = sb("bdw1", [HF + 1, 2, HF])
        wpj = sb("wpj", [HF, 2, D])
        gateT = sb("gateT", [HF, 2, E])
        st, mv = sb("st", [128, NT, 6]), sb("mv", [128, NT, 2])
        arg, rs, half_ = sb("arg", [128, 2 * NT]), sb("rs", [128, 2 * NT]), sb("mhalf", [128, 2 * NT])
        mx, sm, ri = sb("mx", [128, 2, AH]), sb("sm", [128, 2, AH]), sb("ri", [128, 2, AH])
        am, c1, qs = sb("am", [128, NT]), sb("c1", [128, NT]), sb("qs", [128, NT])
        am2, c2, ssq = sb("am2", [128, NT]), sb("c2", [128, NT]), sb("ssq", [128, NT])
        wsum, mw, sw, mwd = sb("wsum", [128, 2]), sb("mw", [128, 2]), sb("sw", [128, 2]), sb("mwd", [128, 2])
        tail = 4 * (EW13 + EW2)
        hv = [arenaV[0:TR, tail + TT * TH * n:tail + TT * TH * (n + 1)] for n in range(6)]
        sig = arenaV[0:TR, tail + TT * TH * 6:tail + TT * TH * 7].rearrange("p (t h) -> p t h", t=TT)
        rowb = rows[0:TR, 0:2 * D + TH]
        gam2, b1c = row("b_out", TR), row("b1", TR)
        wmean = sb("wmean", [HF, 2])
        b1m = sb("b1m", [TR, TH])
        cws, cwx = sb("cws", [SH, 2, 2]), sb("cwx", [SH, 2, 2, 2])
        warm = sb("warm", [128, 1])
        ones, nmagic = sb("ones", [128, 1]), sb("nmagic", [128, 1])
        kw = sb("kw", [128, NT])

        free = [sem(f"bank{i}_evacuated") for i in range(8)]
        full = [sem(f"bank{i}_filled") for i in range(8)]
        dve_s, act_s, pool_s = sem("dve_step"), sem("act_step"), sem("pool_step")
        ln_arg, ln_pow, ln_x = sem("ln_arg"), sem("ln_pow"), sem("ln_x")
        ld = {}

        def loaded(name):
            if name not in ld:
                ld[name] = sem(f"loaded_{name}")
            return ld[name]

        zeroed, idb_made = sem("zeroed"), sem("identity_bf16")
        v_stored, vbd_loaded = sem("v_stored"), [sem(f"v_of_pair{p}_loaded") for p in range(PAIRS)]
        exped, rinved, normed, hbias = sem("exped"), sem("rinved"), sem("normed"), sem("hbias")
        x_round, q_ready, yg_done, sq_done, arg2, pow2, y_round, yi_done = (sem(n) for n in (
            "xi_rounded", "xi_quantised", "y_times_g", "ysq_done", "y_arg", "y_pow", "y_rounded", "yi_quantised"))
        wq_part, wq_sum, wq_done = sem("weight_sums"), sem("weights_rounded"), sem("weights_quantised")
        bdw1_done = sem("bdw1_done")
        split_hi, split_lo = sem("expert_hi"), sem("expert_lo")
        x_hi, x_lo, wv_hi, wv_lo, wqk_hi, wqk_lo, wo_hi, wo_lo = (sem(n) for n in (
            "patch_hi", "patch_lo", "wv_hi", "wv_lo", "wqk_hi", "wqk_lo", "wo_hi", "wo_lo"))
        xn_hi, xn_lo, q_hi, k_hi, v_hi, p_hi, p_lo, ao_hi = (sem(n) for n in (
            "xn_hi", "xn_lo", "q_hi", "k_hi", "v_hi", "p_hi", "p_lo", "ao_hi"))
        tt_sq, tt_var, tt_sqrt, tt_sig, tt_g, tt_ghi, tt_glo = (sem(n) for n in (
            "ttt_square", "ttt_var", "ttt_sqrt", "ttt_sigmoid", "ttt_grad", "ttt_grad_hi", "ttt_grad_lo"))
        tw_hi, tw_lo, x1_hi, k1_hi, km_hi, km_lo, q1_hi = (sem(n) for n in (
            "ttt_weight_hi", "ttt_weight_lo", "ttt_x_hi", "ttt_k_hi", "ttt_k_masked_hi", "ttt_k_masked_lo", "ttt_q_hi"))
        w_hi, w_lo, z_copied, sq_lo, e_done, o_done, o_hi, o_lo = (sem(n) for n in (
            "ttt_w_hi", "ttt_w_lo", "ttt_z_copied", "ttt_zsq_lo", "ttt_rstd_spread",
            "ttt_out", "ttt_out_hi", "ttt_out_lo"))
        mk_done, pos_done, lam, ex1, cw_done, xs_f, xs_hi, xs_done = (sem(n) for n in (
            "mask_done", "pos_done", "logit_gap", "gap_exp", "cw_done", "xs_scaled", "xs_hi", "xs_lo"))
        oh_done, oht_done, z_done, acth, act_done, yp_done, moe_combined = (sem(n) for n in (
            "onehot", "onehotT", "z_split", "act_hi", "act_lo", "y_split", "moe_combined"))
        fin, stored = sem("output_ready"), sem("output_stored")

        use, count = {}, [0] * 8
        ring = [0, list(range(8))]

        def plan(*key, at=None):
            if at is None:
                at = ring[1][ring[0] % len(ring[1])]
                ring[0] += 1
            use[key] = (at, count[at])
            count[at] += 1

        for i in range(NT):
            plan("embed", i)
        for i in range(NT):
            plan("xnT", i)
        for i in range(NT):
            for c in range(2):
                plan("v", i, c)
        for hp in range(HP):
            if hp == 0:
                plan("wmean")
            for n in range(2):
                plan("k", hp, n)
            for n in range(2):
                plan("q", hp, n)
        for s in range(PAIRS + 3):
            if s < PAIRS:
                plan("S", s)
            if 0 <= s - 2 < PAIRS:
                plan("PT", s - 2, 0)
                plan("PT", s - 2, 1)
            if 0 <= s - 3 < PAIRS:
                plan("PV", s - 3)
            if s >= PAIRS:
                plan("wo", s - PAIRS)
        for i in range(3, NT):
            plan("wo", i)
        FFN_ORDER = [("xiT", 0), ("xiT", 1), ("xiT", 2), ("gate", 0), ("gate", 1), ("xiT", 3), ("xiT", 4)] + [
            ("gate", i) for i in range(2, NT)]
        for key, i in FFN_ORDER:
            plan(key, i)
            if key == "gate":
                plan("up", i)
        plan("wz")
        for i in range(NT):
            plan("yiT", i)
            plan("down", i)
        for i in range(NT):
            plan("x1T", i)
        for n in range(2):
            for key in ("B", "A"):
                for t in range(3 * n, 3 * n + 3):
                    plan(key, t)
        for j in range(2):
            for n in range(2):
                plan("Q", j, n)
        for t in range(TT + 3):
            if t < TT:
                plan("gW", t, 0)
                plan("gW", t, 1)
            if 0 <= t - 2 < TT:
                plan("Z", t - 2)
            if 0 <= t - 3:
                plan("var", t - 3)
        for t in range(TT):
            plan("R", t)
        for i in range(NT):
            plan("proj", i)
        plan("logits")
        for i in range(NT):
            plan("x2T", i)
        plan("pos")
        ring = [0, [3, 4, 5, 6, 7]]
        for b in range(3):
            plan("acc", b, at=b)
        for s in range(E + 1):
            if s < E:
                plan("posb", s, 0)
                plan("posb", s, 1)
                plan("z", s)
            if s >= 1:
                plan("y", s - 1)
            if s < E:
                for r in range(2):
                    plan("g", s, r)
                    plan("u", s, r)

        def at_bank(*key):
            return bank[use[key][0]]

        def claim(eng, *key):
            b, n = use[key]
            if n:
                eng.wait_ge(free[b], n)
            return bank[b]

        def wait_full(eng, *key):
            b, n = use[key]
            eng.wait_ge(full[b], n + 1)
            return bank[b]

        def wait_evac(eng, *key):
            b, n = use[key]
            eng.wait_ge(free[b], n + 1)

        def fills(ins, *key):
            ins.then_inc(full[use[key][0]], 1)

        def frees(ins, *key):
            ins.then_inc(free[use[key][0]], 1)

        class Steps:

            def __init__(self, eng, s):
                self.eng, self.s, self.n = eng, s, 0

            def do(self, ins):
                ins.then_inc(self.s, 1)
                self.n += 1

            def settle(self):
                if self.n:
                    self.eng.wait_ge(self.s, self.n)

            def then(self, ins):
                self.do(ins)
                self.settle()

        def split_high(act, e):
            if e == 0:
                wait_full(act, "PV", PAIRS - 1)
            act.wait_ge(loaded("e13"), 16 * (e + 1))
            act.wait_ge(loaded("e2"), 16 * (e + 1))
            nc.scalar.activation(w13p[e][:, 0], stage13, ACT.Copy).then_inc(split_hi, 1)
            nc.scalar.activation(w2p[e][:, 0], stage2[:], ACT.Copy).then_inc(split_hi, 1)

        def split_low(pool, e):
            pool.wait_ge(split_hi, 2 * e + 2)
            nc.gpsimd.tensor_tensor(w13p[e][:, 1], stage13, w13p[e][:, 0], ALU.subtract).then_inc(split_lo, 1)
            nc.gpsimd.tensor_tensor(w2p[e][:, 1], stage2[:], w2p[e][:, 0], ALU.subtract).then_inc(split_lo, 1)

        block = ctx.enter_context(nc.Block())

        @block.sync
        def _(sp):
            def load(dst, name, src=None):
                sp.dma_start(dst, d[name] if src is None else src).then_inc(loaded(name), 16)

            for k in range(KC):
                sp.dma_start(xraw[:, k, :], d["xT"][:, k, :]).then_inc(loaded(f"x{k}"), 16)
                sp.dma_start(wpraw[:, k, :], d["wpT"][:, k, :]).then_inc(loaded(f"x{k}"), 16)
            load(rows[:], "rows", d["rows"].partition_broadcast(128))
            load(idf[:], "idf")
            load(cols[:], "cols")
            load(idh[:], "idh")
            for name, o in (("wv", 2 * AH * AD), ("wk", AH * AD), ("wq", 0)):
                load(wqkvraw[:, :, o:o + AH * AD], name, d["wqkv"][:, :, o:o + AH * AD])
            load(stage13, "w_in")
            load(stage2[:], "w_out2")
            for name, t in [("tri", tri), ("iota", iota), ("iota8", iota8), ("slot", slot),
                            ("bmask", bmask), ("hsel", hsel), ("bd", bd), ("nw", nw), ("wvT", wb[:, :, D:2 * D]),
                            ("wkn", wkn), ("w1s", w1s), ("wpj", wpj), ("gateT", gateT)]:
                load(t if name == "wvT" else t[:], name)
            load(wa[:], "wa")
            load(wb[:, :, 2 * D:], "lrT")
            for i in range(NT):
                r = rows_of(i)
                wait_evac(sp, "v", i, 0)
                wait_evac(sp, "v", i, 1)
                sp.dma_start(v_scr[128 * i:128 * i + r, :], v_sb[0:r, i].rearrange("p h c x -> p (h c x)")).then_inc(v_stored, 16)
            sp.wait_ge(v_stored, 16 * NT)
            sp.wait_ge(zeroed, 2)
            src = v_scr.rearrange("(b k) (h y n) -> y k b h n", k=NP, h=HP, y=2)
            for b in range(B):
                for y_ in range(2):
                    sp.dma_start(Vbd[NP * y_:NP * y_ + NP, b, :, y_].rearrange("p h c x -> p h (c x)"),
                                 src[y_, :, b]).then_inc(vbd_loaded[b // 2], 16)
            sp.wait_ge(wq_done, 2)
            load(woraw, "woT")
            for e in range(E):
                if e == 0:
                    sp.wait_ge(wo_lo, 1)
                if e:
                    sp.wait_ge(split_lo, 2 * e)
                    sp.wait_ge(split_hi, 2 * e)
                sp.dma_start(stage13, d["w13"][:, e]).then_inc(loaded("e13"), 16)
                sp.dma_start(stage2[:], d["w2"][:, e]).then_inc(loaded("e2"), 16)
            for i in range(NT):
                r = rows_of(i)
                sp.wait_ge(fin, i + 1)
                sp.dma_start(out[128 * i:128 * i + r, :], h[0:r, i, :]).then_inc(stored, 16)
            sp.wait_ge(stored, 16 * NT)

        @block.tensor
        def _(pe):
            mm, tr = nc.tensor.matmul, nc.tensor.transpose

            for i in range(NT):
                claim(pe, "embed", i)
            for k in range(KC):
                pe.wait_ge(x_lo, 2 * k + 2)
                for i in range(NT):
                    r = rows_of(i)
                    for n, (a_, w_) in enumerate(PARTS):
                        ins = mm(at_bank("embed", i)[0:r, 0:D], xpT[:, a_, k, 128 * i:128 * i + r], wp16[:, w_, k, :],
                                 start=k == 0 and n == 0, stop=k == KC - 1 and n == 2)
                    if k == KC - 1:
                        fills(ins, "embed", i)

            pe.wait_ge(loaded("idh"), 16)

            def x_transposed(key, ln, tiles=range(NT)):
                pe.wait_ge(loaded("idf"), 16)
                for i in tiles:
                    r = rows_of(i)
                    bk = claim(pe, key, i)
                    pe.wait_ge(ln_x, NT * ln + i + 1)
                    for j in range(2):
                        ins = tr(bk[0:HF, 128 * j:128 * j + r], xc[0:r, i, HF * j:HF * j + HF], idf[0:r, 0:r])
                    fills(ins, key, i)

            x_transposed("xnT", 0)
            pe.wait_ge(wv_lo, 1)
            for i in range(NT):
                r = rows_of(i)
                pe.wait_ge(xn_lo, i + 1)
                for c in range(2):
                    bk = claim(pe, "v", i, c)
                    for n, (a_, w_) in enumerate(PARTS):
                        for j in range(2):
                            ins = mm(bk[0:r, 0:384], x16[:, a_, j, 128 * i:128 * i + r],
                                     wqkv[:, w_, j, 1536 + 384 * c:1536 + 384 * c + 384], start=n + j == 0, stop=n == 2 and j == 1)
                    fills(ins, "v", i, c)
            for hp in range(HP):
                if hp == 0:
                    bk = claim(pe, "wmean")
                    pe.wait_ge(wq_part, 2)
                    pe.wait_ge(zeroed, 1)
                    mm(bk[:, 0:1], ones[0:HF, :].broadcast_to([HF, 128]), wsum[0:HF, 0:1], start=True, stop=True)
                    ins = mm(bk[:, 1:2], ones[:, :].broadcast_to([128, 128]), wsum[:, 1:2], start=True, stop=True)
                    fills(ins, "wmean")
                for key, o in (("k", AH * AD), ("q", 0)):
                    for n in range(2):
                        bk = claim(pe, key, hp, n)
                        pe.wait_ge(wqk_lo, 1 if key == "k" else 2)
                        for m, (a_, w_) in enumerate(PARTS):
                            for j in range(2):
                                ins = mm(bk[:, 0:288], wqkv[:, w_, j, o + 128 * hp:o + 128 * hp + 128],
                                         x16[:, a_, j, 288 * n:288 * n + 288], start=m + j == 0, stop=m == 2 and j == 1)
                        fills(ins, key, hp, n)
            for hp in range(HP):
                for n in range(2):
                    wait_evac(pe, "k", hp, n)
                    wait_evac(pe, "q", hp, n)
            def output_projection(i):
                pe.wait_ge(wo_lo, 1)
                r = rows_of(i)
                wait_evac(pe, "PV", min(PAIRS - 1, (128 * (i + 1) - 1) // 72))
                bk = claim(pe, "wo", i)
                for hp in range(HP):
                    for n, (a_, w_) in enumerate(PARTS):
                        ins = mm(bk[0:r, 0:D], aoT[:, a_, hp, 128 * i:128 * i + r], woT[:, w_, hp, :],
                                 start=hp + n == 0, stop=hp == HP - 1 and n == 2)
                fills(ins, "wo", i)

            for s in range(PAIRS + 3):
                if s < PAIRS:
                    bk = claim(pe, "S", s)
                    for x in range(2):
                        b = 2 * s + x
                        for hp in range(HP):
                            for n, (a_, w_) in enumerate(PARTS):
                                ins = mm(bk[64 * x:64 * x + 64, 72 * hp:72 * hp + 72], qT[:, a_, hp, NP * b:NP * b + 64],
                                         Kbd[:, w_, hp, b, :], start=n == 0, stop=n == 2)
                    fills(ins, "S", s)
                p = s - 2
                if 0 <= p < PAIRS:
                    for c, ready in enumerate((p_hi, p_lo)):
                        bk = claim(pe, "PT", p, c)
                        pe.wait_ge(ready, p + 1)
                        for hp in range(HP):
                            ins = tr(bk[0:72, :].bitcast(F16)[:, 128 * hp:128 * hp + 128], P16[:, p % 2, c, 72 * hp:72 * hp + 72], idh[:])
                        fills(ins, "PT", p, c)
                p = s - 3
                if 0 <= p < PAIRS:
                    wait_evac(pe, "PT", p, 0)
                    wait_evac(pe, "PT", p, 1)
                    pe.wait_ge(vbd_loaded[p], 16 * 4)
                    bk = claim(pe, "PV", p)
                    for hp in range(HP):
                        for x in range(2):
                            for n, (a_, w_) in enumerate(PARTS):
                                ins = mm(bk[:, 72 * hp + NP * x:72 * hp + NP * x + NP], Vbd[:, 2 * p + x, hp].rearrange("p y c x -> p (y c) x")[:, :, w_],
                                         PT[:, p % 2, a_, 128 * hp + 64 * x:128 * hp + 64 * x + NP], start=n == 0, stop=n == 2)
                    fills(ins, "PV", p)
                if s >= PAIRS:
                    output_projection(s - PAIRS)
            for i in range(3, NT):
                output_projection(i)
            pe.wait_ge(idb_made, 1)
            def xi_transposed(i):
                r = rows_of(i)
                bk = claim(pe, "xiT", i)
                pe.wait_ge(q_ready, i + 1)
                bv = bk[0:HF, :].bitcast(BF16)
                for j in range(2):
                    ins = tr(bv[:, 128 * j:128 * j + r], xi[0:r, i, HF * j:HF * j + HF], idb[0:r, 0:r])
                fills(ins, "xiT", i)

            def gate_up(i):
                r = rows_of(i)
                pe.wait_ge(wq_done, 2)
                wait_evac(pe, "xiT", i)
                for key, o in (("gate", FH), ("up", 0)):
                    bk = claim(pe, key, i)
                    for j in range(2):
                        ins = mm(bk[0:r, :], xiT[:, j, 128 * i:128 * i + r], wiq[:, j, o:o + FH], start=j == 0, stop=j == 1)
                    fills(ins, key, i)

            for key, i in FFN_ORDER:
                (xi_transposed if key == "xiT" else gate_up)(i)
            bk = claim(pe, "wz")
            pe.wait_ge(bdw1_done, 1)
            pe.wait_ge(loaded("wkn"), 16)
            for c in range(2):
                for j in range(2):
                    ins = mm(bk[0:HF, D * c + HF * j:D * c + HF * j + HF], wkn[:, j, HF * c:HF * c + HF], bdw1[0:HF, j, :],
                             start=True, stop=True)
            fills(ins, "wz")
            for i in range(NT):
                r = rows_of(i)
                bk = claim(pe, "yiT", i)
                pe.wait_ge(yi_done, i + 1)
                bv = bk[:, :].bitcast(BF16)
                for m in range(4):
                    ins = tr(bv[:, 128 * m:128 * m + r], yi[0:r, i % 2, 128 * m:128 * m + 128], idb[0:r, 0:r])
                fills(ins, "yiT", i)
                wait_evac(pe, "yiT", i)
                bk = claim(pe, "down", i)
                for m in range(4):
                    ins = mm(bk[0:r, 0:D], yiT[:, i % 2, m, 0:r], w2q[:, m, :], start=m == 0, stop=m == 3)
                fills(ins, "down", i)
            x_transposed("x1T", 1)
            pe.wait_ge(tw_lo, 4)
            pe.wait_ge(zeroed, 3)
            for i in range(NT):
                wait_evac(pe, "x1T", i)
            for grp in range(2):
                for key, w, o, n in (("B", wb16, 0, 2 * D + TH), ("A", wa16, D, D)):
                    for t in range(3 * grp, 3 * grp + 3):
                        bk = claim(pe, key, t)
                        for m, (a_, w_) in enumerate(PARTS):
                            for j in range(2):
                                ins = mm(bk[0:TR, 0:n], xnp[:, a_, j, TR * t:TR * t + TR], w[:, w_, j, o:o + n],
                                         start=m + j == 0, stop=m == 2 and j == 1)
                        fills(ins, key, t)
            for jo in range(2):
                for n in range(2):
                    bk = claim(pe, "Q", jo, n)
                    for m, (a_, w_) in enumerate(PARTS):
                        for j in range(2):
                            ins = mm(bk[0:HF, 0:288], wa16[:, w_, j, HF * jo:HF * jo + HF], xnp[:, a_, j, 288 * n:288 * n + 288],
                                     start=m + j == 0, stop=m == 2 and j == 1)
                    fills(ins, "Q", jo, n)
            pe.wait_ge(loaded("hsel"), 16)
            for t in range(TT + 3):
                if t < TT:
                    pe.wait_ge(tt_glo, t // 3 + 1)
                    pe.wait_ge(km_hi, t + 1)
                    pe.wait_ge(km_lo, t + 1)
                    for j in range(2):
                        bk = claim(pe, "gW", t, j)
                        for b in range(G3):
                            for n, (k_, g_) in enumerate(PARTS):
                                o = ((k_ * G3 + b) * 2 + j) * (HF + 1)
                                ins = mm(bk[:, HF * b:HF * b + HF], Kmf[t][:, o:o + 128], G16[:, t, g_, HF * j:HF * j + HF],
                                         start=n == 0, stop=n == 2)
                        fills(ins, "gW", t, j)
                u = t - 2
                if 0 <= u < TT:
                    if u == 0:
                        for j in range(2):
                            for n in range(2):
                                wait_evac(pe, "Q", j, n)
                    pe.wait_ge(w_lo, u + 1)
                    bk = claim(pe, "Z", u)
                    for j in range(2):
                        for n, (w_, q_) in enumerate(PARTS):
                            o = (w_ * 2 + j) * HF
                            mm(bk[:, TR * j:TR * j + TR], base16f[:, o:o + 128], q16[:, q_, j, TR * u:TR * u + TR],
                               start=n == 0, stop=False)
                        images = min(G3, B - G3 * u)
                        for b in range(images):
                            for n, (w_, q_) in enumerate(PARTS):
                                c = TR * u + NP * b
                                o = ((w_ * 2 + j) * G3 + b) * HF
                                ins = mm(bk[:, TR * j + NP * b:TR * j + NP * b + NP], W16f[:, u % 2, o:o + 128],
                                         q16[:, q_, j, c:c + NP], start=False, stop=b == images - 1 and n == 2)
                    fills(ins, "Z", u)
                u = t - 3
                if u >= 0:
                    bk = claim(pe, "var", u)
                    wait_evac(pe, "Z", u)
                    pe.wait_ge(sq_lo, u + 1)
                    for x in range(2):
                        for j in range(2):
                            ins = mm(bk[0:TR, 0:TH], sq16[:, u % 2, x, TR * j:TR * j + TR], hsel[:, j, :],
                                     start=x + j == 0, stop=x + j == 2)
                    fills(ins, "var", u)
            for t in range(TT):
                pe.wait_ge(e_done, t // 3 + 1)
                bk = claim(pe, "R", t)
                for j in range(2):
                    for x in range(2):
                        m = HF if j else 128
                        ins = mm(bk[0:m, TR * j:TR * j + TR], E16[:, t].rearrange("p x n -> p (x n)")[:, D * x + HF * j:D * x + HF * j + m],
                                 idh[0:TR, 0:TR],
                                 start=x == 0, stop=x == 1)
                fills(ins, "R", t)
            for i in range(NT):
                r = rows_of(i)
                pe.wait_ge(o_lo, 1 if 128 * i + r <= 3 * TR else 2)
                bk = claim(pe, "proj", i)
                for m, (a_, w_) in enumerate(PARTS):
                    for j in range(2):
                        ins = mm(bk[0:r, 0:D], xnp[:, a_, j, 128 * i:128 * i + r], wpj16[:, w_, j, :],
                                 start=m + j == 0, stop=m == 2 and j == 1)
                fills(ins, "proj", i)
            def logits(i):
                r = rows_of(i)
                wait_evac(pe, "x2T", i)
                bk = at_bank("logits")
                for j in range(2):
                    ins = mm(bk[0:r, E * i:E * i + E], xnT[:, j, 128 * i:128 * i + r], gateT[:, j, :], start=j == 0, stop=j == 1)
                if i == NT - 1:
                    fills(ins, "logits")

            pe.wait_ge(loaded("gateT"), 16)
            claim(pe, "logits")
            for i in range(NT):
                x_transposed("x2T", 2, (i,))
                if i >= 1:
                    logits(i - 1)
            logits(NT - 1)
            bk = claim(pe, "pos")
            pe.wait_ge(mk_done, 1)
            pe.wait_ge(loaded("tri"), 16)
            for i in range(NT):
                r = rows_of(i)
                for k in range(i + 1):
                    ins = mm(bk[0:r, E * i:E * i + E], (tri if k == i else ones16)[0:rows_of(k), 0:r],
                             mk16[0:rows_of(k), k, :], start=k == 0, stop=k == i)
            fills(ins, "pos")
            for b in range(3):
                bk = claim(pe, "acc", b)
                r, n = (128, 2 * D) if b < 2 else (T - 512, D)
                mm(bk[0:r, 0:n], tri[:, 0:1].broadcast_to([128, r]), tri[:, 0:1].broadcast_to([128, n]), start=True, stop=False)

            pe.wait_ge(xs_done, 1)
            pe.wait_ge(cw_done, 1)
            pe.wait_ge(pos_done, 1)

            def dispatch(e):
                for c in range(2):
                    bk = claim(pe, "posb", e, c)
                    for i in ((0, 1, 2), (3, 4))[c]:
                        r = rows_of(i)
                        o = 128 * (i - 3 * c)
                        ins = mm(bk[0:SH, o:o + r], pos16[0:r, i, e:e + 1].broadcast_to([r, SH]), idh[0:r, 0:r],
                                 start=True, stop=True)
                    fills(ins, "posb", e, c)
                bk = claim(pe, "z", e)
                pe.wait_ge(oh_done, e + 1)
                for j in range(2):
                    for i in range(NT):
                        r = rows_of(i)
                        for x in range(2):
                            ins = mm(bk[0:HF, CAP * j:CAP * j + CAP], xsp[0:r, x, i, HF * j:HF * j + HF],
                                     oh[0:r, e % 2, i, :], start=i == 0 and x == 0, stop=i == NT - 1 and x == 1)
                for s in range(2):
                    for i in range(NT):
                        r = rows_of(i)
                        ins = mm(bk[0:SH, 2 * CAP + 2 * s:2 * CAP + 2 * s + 2], oh[0:r, e % 2, i, SH * s:SH * s + SH],
                                 cwp[0:r, i, e, :], start=i == 0, stop=i == NT - 1)
                fills(ins, "z", e)

            def up_gate(e):
                pe.wait_ge(z_done, e + 1)
                pe.wait_ge(split_hi, 2 * e + 2)
                pe.wait_ge(split_lo, 2 * e + 2)
                for rnd in range(2):
                    for key, o in (("g", 0), ("u", FH)):
                        bk = claim(pe, key, e, rnd)
                        for m in range(2):
                            f = o + 128 * (2 * rnd + m)
                            n = 0
                            for wx, zx in ((0, 0), (0, 1), (1, 0)):
                                for j in range(2):
                                    ins = mm(bk[:, CAP * m:CAP * m + CAP], w13p[e][:, wx, j, f:f + 128], zp[:, zx, j, :],
                                             start=n == 0, stop=n == 5)
                                    n += 1
                        fills(ins, key, e, rnd)

            def down(e):
                pe.wait_ge(act_done, e + 1)
                bk = claim(pe, "y", e)
                for s in range(2):
                    n = 0
                    for m in range(4):
                        for wx, ax in ((0, 0), (0, 1), (1, 0)):
                            ins = mm(bk[0:SH, D * s:D * s + D], actp[:, ax, m, SH * s:SH * s + SH], w2p[e][:, wx, m, :],
                                     start=n == 0, stop=n == 11)
                            n += 1
                fills(ins, "y", e)

            def combine(e):
                pe.wait_ge(yp_done, e + 1)
                pe.wait_ge(oht_done, e + 1)
                for i in range(NT):
                    r = rows_of(i)
                    for s in range(2):
                        for x in range(2):
                            ins = mm(bank[i // 2][0:r, D * (i % 2):D * (i % 2) + D], ohT[:, e % 2, s, 128 * i:128 * i + r],
                                     yp[:, x, s, :], start=False,
                                     stop=e == E - 1 and s == 1 and x == 1 and (i % 2 == 1 or i == NT - 1))
                    if e == E - 1 and (i % 2 == 1 or i == NT - 1):
                        fills(ins, "acc", i // 2)
                if e < E - 1:
                    ins.then_inc(moe_combined, 1)

            for s in range(E + 1):
                if s < E:
                    dispatch(s)
                if s >= 1:
                    down(s - 1)
                if s < E:
                    up_gate(s)
                if s >= 1:
                    combine(s - 1)

        @block.vector
        def _(dve):
            st_ = Steps(dve, dve_s)
            v = nc.vector

            def stats(i, A, c, second=None):
                r = rows_of(i)
                st_.then(v.bn_stats(st[0:r, i, :], h[0:r, i, :]))
                st_.then(v.bn_aggr(mv[0:r, i, :], st[0:r, i, :]))
                if second:
                    st_.do(v.tensor_scalar(arg[0:r, NT + i:NT + i + 1], mv[0:r, i, 1:2], *second, ALU.mult, ALU.add))
                v.tensor_scalar(arg[0:r, i:i + 1], mv[0:r, i, 1:2], A, c, ALU.mult, ALU.add).then_inc(ln_arg, 1)

            def normalise(n, i, last=True):
                r = rows_of(i)
                dve.wait_ge(ln_pow, n)
                ins = v.tensor_scalar(xc[0:r, i, :], h[0:r, i, :], mv[0:r, i, 0:1], rs[0:r, i:i + 1], ALU.subtract, ALU.mult)
                if last:
                    ins.then_inc(ln_x, 1)
                return ins

            for k in range(KC):
                dve.wait_ge(x_hi, 2 * k + 2)
                v.tensor_tensor(xpT[:, 1, k, :], xraw[:, k, :], xpT[:, 0, k, :], ALU.subtract).then_inc(x_lo, 1)
                v.tensor_tensor(wp16[:, 1, k, :], wpraw[:, k, :], wp16[:, 0, k, :], ALU.subtract).then_inc(x_lo, 1)
            dve.wait_ge(loaded("rows"), 16)
            for i in range(NT):
                r = rows_of(i)
                bk = wait_full(dve, "embed", i)
                frees(v.tensor_tensor(h[0:r, i, :], bk[0:r, 0:D], row("b_proj", r), ALU.add), "embed", i)
                wait_evac(dve, "embed", i)
                stats(i, 1.0 + 1e-5, 1e-10)
                if i >= 1:
                    normalise(i, i - 1)
            normalise(NT, NT - 1)
            dve.wait_ge(wv_hi, 1)
            v.tensor_tensor(wqkv[:, 1, :, 1536:], wqkvraw[:, :, 1536:], wqkv[:, 0, :, 1536:], ALU.subtract).then_inc(wv_lo, 1)
            for i in range(NT):
                r = rows_of(i)
                dve.wait_ge(xn_hi, i + 1)
                v.tensor_tensor(x16[:, 1, :, 128 * i:128 * i + r], xnT[:, :, 128 * i:128 * i + r],
                                x16[:, 0, :, 128 * i:128 * i + r], ALU.subtract).then_inc(xn_lo, 1)
            dve.wait_ge(loaded("w_in"), 16)
            dve.wait_ge(loaded("w_out2"), 16)
            v.tensor_reduce(wsum[0:HF, 0:1], stage13[:, :, :], AX.XY, ALU.add, apply_absolute_value=True).then_inc(wq_part, 1)
            v.tensor_reduce(wsum[:, 1:2], stage2[:, :, :], AX.XY, ALU.add, apply_absolute_value=True).then_inc(wq_part, 1)
            for i in range(NT):
                r = rows_of(i)
                for c in range(2):
                    bk = wait_full(dve, "v", i, c)
                    dve.wait_ge(v_hi, 2 * i + c + 1)
                    frees(v.tensor_tensor(v_sb[0:r, i, 6 * c:6 * c + 6, :, 1], bk[0:r, 0:384].rearrange("p (h c) -> p h c", h=6),
                                          v_sb[0:r, i, 6 * c:6 * c + 6, :, 0], ALU.subtract), "v", i, c)

            dve.wait_ge(loaded("idf"), 16)
            v.tensor_copy(idb[:], idf[:]).then_inc(idb_made, 1)

            bk = wait_full(dve, "wmean")
            st_.do(v.tensor_scalar(mw[:, 0:1], bk[:, 0:1], 1.0 / (2 * FH * D), 1e-5, ALU.mult, ALU.max))
            frees(v.tensor_scalar(mw[:, 1:2], bk[:, 1:2], 1.0 / (FH * D), 1e-5, ALU.mult, ALU.max), "wmean")
            st_.settle()
            wait_evac(dve, "wmean")
            st_.do(v.reciprocal(sw[:], mw[:]))
            st_.then(v.tensor_scalar(mwd[:], mw[:], 1.0 / 127.0, None, ALU.mult))
            for hp in range(HP):
                if hp == 2:
                    st_.then(v.tensor_scalar(stage2[:], stage2[:], sw[:, 1:2], 1.0, ALU.mult, ALU.min))
                    v.tensor_scalar(stage2[:], stage2[:], -1.0, MAGIC, ALU.max, ALU.add).then_inc(wq_sum, 1)
                if hp == 3:
                    st_.then(v.tensor_scalar(stage13[:], stage13[:], sw[0:HF, 0:1], 1.0, ALU.mult, ALU.min))
                if hp == 4:
                    v.tensor_scalar(stage13[:], stage13[:], -1.0, MAGIC, ALU.max, ALU.add).then_inc(wq_sum, 1)
                for n in range(2):
                    bk = wait_full(dve, "k", hp, n)
                    if n == 0:
                        dve.wait_ge(zeroed, 1)
                    dve.wait_ge(k_hi, 2 * hp + n + 1)
                    for x in range(2):
                        o = slice(64 * x, 64 * x + 64)
                        ins = v.tensor_tensor(Kbd[o, 1, hp, 8 * n:8 * n + 8, NP * x:NP * x + NP],
                                              bk[o, 0:288].rearrange("p (b k) -> p b k", k=NP),
                                              Kbd[o, 0, hp, 8 * n:8 * n + 8, NP * x:NP * x + NP], ALU.subtract)
                    frees(ins, "k", hp, n)
                for n in range(2):
                    bk = wait_full(dve, "q", hp, n)
                    dve.wait_ge(q_hi, 2 * hp + n + 1)
                    o = slice(288 * n, 288 * n + 288)
                    frees(v.scalar_tensor_tensor(out=qT[:, 1, hp, o], in0=bk[:, 0:288], scalar=AD ** -0.5,
                                                 in1=qT[:, 0, hp, o], op0=ALU.mult, op1=ALU.subtract), "q", hp, n)
            def ttt_weights():
                for name in ("w1s", "bd", "wvT", "wa", "bmask"):
                    dve.wait_ge(loaded(name), 16)
                st_.then(v.tensor_reduce(wmean[:, :], w1s[:, :, :], AX.X, ALU.add))
                st_.then(v.tensor_scalar(wmean[:, :], wmean[:, :], 1.0 / TD, None, ALU.mult))
                st_.then(v.tensor_tensor(w1s[:, :, :], w1s[:, :, :], wmean[:, :].unsqueeze(2).broadcast_to([HF, 2, TD]), ALU.subtract))
                for j in range(2):
                    ins = v.tensor_tensor(bdw1[0:HF, j, :].rearrange("p (a b) -> p a b", b=TD),
                                          w1s[:, j, :].unsqueeze(1).broadcast_to([HF, HF // TD, TD]),
                                          bd[0:HF, :].rearrange("p (a b) -> p a b", b=TD), ALU.mult)
                    if j == 0:
                        st_.do(ins)
                ins.then_inc(bdw1_done, 1)
                st_.do(v.tensor_tensor(wb[:, :, 0:D], wa[:, :, D:2 * D], wb[:, :, D:2 * D], ALU.subtract))
                st_.do(v.tensor_tensor(gam2[:], row("tg", TR), row("tg", TR), ALU.mult))
                st_.do(v.tensor_tensor(qbt[:], cols[:, 6:8], cols[:, 8:10], ALU.add))
                st_.do(v.tensor_tensor(rowb[:, 0:D], row("tb", TR), row("vb", TR), ALU.subtract))
                st_.do(v.tensor_reduce(b1m[:], row("b1", TR).rearrange("p (a b) -> p a b", b=TD), AX.X, ALU.add))
                st_.settle()
                st_.do(v.tensor_scalar(b1m[:], b1m[:], 1.0 / TD, None, ALU.mult))
                st_.do(v.tensor_tensor(rowb[:, 0:D], rowb[:, 0:D], row("tg", TR), ALU.mult))
                for j in range(2):
                    st_.do(v.tensor_tensor(wb[:, j, 0:D], wb[:, j, 0:D], row("tg", HF), ALU.mult))
                st_.settle()
                st_.then(v.tensor_tensor(b1c[:].rearrange("p (a b) -> p a b", b=TD), row("b1", TR).rearrange("p (a b) -> p a b", b=TD),
                                         b1m[:].unsqueeze(2).broadcast_to([TR, TH, TD]), ALU.subtract))
                st_.do(v.tensor_copy(rowb[:, D:2 * D], b1c[:]))
                v.tensor_copy(bdw1[HF:HF + 1, :, :].rearrange("p j n -> p (j n)"), b1c[HF:HF + 1, :]).then_inc(bdw1_done, 1)

            def residual(i):
                r = rows_of(i)
                bk = wait_full(dve, "wo", i)
                frees(v.tensor_tensor(h[0:r, i, :], bk[0:r, 0:D], h[0:r, i, :], ALU.add), "wo", i)
                wait_evac(dve, "wo", i)
                stats(i, 1.0 + 1e-6, 1e-11)

            dve.wait_ge(hbias, 1)
            for s in range(PAIRS + 3):
                p = s - 2
                if 0 <= p < PAIRS:
                    if p >= 2:
                        wait_full(dve, "PT", p - 2, 1)
                    dve.wait_ge(p_hi, p + 1)
                    v.tensor_tensor(P16[:, p % 2, 1, :], P[:, p % 3, :], P16[:, p % 2, 0, :], ALU.subtract).then_inc(p_lo, 1)
                if s < PAIRS:
                    bk = wait_full(dve, "S", s)
                    sv = bk[:, 0:432].rearrange("p (h k) -> p h k", k=NP)
                    st_.then(v.tensor_reduce(mx[:, s % 2, :], sv, AX.X, ALU.max))
                    if s >= 3:
                        dve.wait_ge(p_lo, s - 2)
                    frees(v.tensor_tensor(P[:, s % 3, :].rearrange("p (h k) -> p h k", k=NP), sv,
                                          mx[:, s % 2, :].unsqueeze(2).broadcast_to([128, AH, NP]), ALU.subtract), "S", s)
                p = s - 1
                if 0 <= p < PAIRS:
                    dve.wait_ge(exped, p + 1)
                    st_.then(v.tensor_reduce(sm[:, p % 2, :], P[:, p % 3, :].rearrange("p (h k) -> p h k", k=NP), AX.X, ALU.add))
                    if p >= 2:
                        dve.wait_ge(normed, p - 1)
                    v.reciprocal(ri[:, p % 2, :], sm[:, p % 2, :]).then_inc(rinved, 1)
                p = s - 2
                if 0 <= p < PAIRS:
                    bk = wait_full(dve, "PT", p, 1)
                    if p >= 2:
                        wait_full(dve, "PV", p - 2)
                    frees(v.tensor_copy(PT[:, p % 2, 1, :], bk[0:72, :].bitcast(F16)[:, 0:768]), "PT", p, 1)
                p = s - 3
                if 0 <= p < PAIRS:
                    bk = wait_full(dve, "PV", p)
                    dve.wait_ge(ao_hi, p + 1)
                    o = slice(72 * p, 72 * p + 72)
                    frees(v.tensor_tensor(aoT[:, 1, :, o], bk[:, 0:432].rearrange("p (h q) -> p h q", h=HP), aoT[:, 0, :, o],
                                          ALU.subtract), "PV", p)
                if s == 9:
                    ttt_weights()
                if s >= PAIRS + 1:
                    residual(s - PAIRS - 1)
            residual(2)
            residual(3)
            for i in range(3):
                st_.do(normalise(NT + i + 1, i, last=False))
            residual(4)
            for g0, g1 in ((0, 3), (3, NT)):
                c = slice(g0, g1)
                if g0:
                    for i in range(g0, g1):
                        st_.do(normalise(NT + i + 1, i, last=False))
                st_.settle()
                for i in range(g0, g1):
                    r = rows_of(i)
                    st_.do(v.tensor_tensor(xc[0:r, i, :], xc[0:r, i, :], row("g_in", r), ALU.mult))
                st_.settle()
                for i in range(g0, g1):
                    r = rows_of(i)
                    st_.do(v.tensor_reduce(am[0:r, i:i + 1], xc[0:r, i, :], AX.X, ALU.max, apply_absolute_value=True))
                st_.settle()
                st_.then(v.tensor_scalar(am[:, c], am[:, c], 1e-5, None, ALU.max))
                st_.do(v.tensor_scalar(c1[:, c], am[:, c], mwd[:, 0:1], None, ALU.mult))
                st_.then(v.reciprocal(qs[:, c], am[:, c]))
                st_.then(v.tensor_scalar(qs[:, c], qs[:, c], 127.0, None, ALU.mult))
                for i in range(g0, g1):
                    r = rows_of(i)
                    v.tensor_scalar(xc[0:r, i, :], xc[0:r, i, :], qs[0:r, i:i + 1], MAGIC, ALU.mult, ALU.add).then_inc(x_round, 1)
            for s in range(NT + 4):
                if s < NT:
                    i, r = s, rows_of(s)
                    bk = wait_full(dve, "up", i)
                    wait_evac(dve, "gate", i)
                    if i >= 3:
                        dve.wait_ge(sq_done, i - 2)
                        dve.wait_ge(yg_done, i - 2)
                    frees(v.scalar_tensor_tensor(out=y[0:r, i % 3, :], in0=bk[0:r, :], scalar=c1[0:r, i:i + 1],
                                                 in1=sg[0:r, i % 4, :], op0=ALU.mult, op1=ALU.mult), "up", i)
                if 0 <= s - 2 < NT:
                    i, r = s - 2, rows_of(s - 2)
                    dve.wait_ge(pow2, i + 1)
                    st_.settle()
                    rr = rs[0:r, NT + i:NT + i + 1]
                    st_.then(v.tensor_scalar(am2[0:r, i:i + 1], am2[0:r, i:i + 1], rr, 1e-5, ALU.mult, ALU.max))
                    st_.do(v.tensor_scalar(c2[0:r, i:i + 1], am2[0:r, i:i + 1], mwd[0:r, 1:2], None, ALU.mult))
                    st_.then(v.reciprocal(qs[0:r, i:i + 1], am2[0:r, i:i + 1]))
                    st_.then(v.tensor_scalar(qs[0:r, i:i + 1], qs[0:r, i:i + 1], 127.0, rr, ALU.mult, ALU.mult))
                    v.tensor_scalar(sg[0:r, i % 4, :], sg[0:r, i % 4, :], qs[0:r, i:i + 1], MAGIC, ALU.mult, ALU.add).then_inc(y_round, 1)
                if 0 <= s - 1 < NT:
                    i, r = s - 1, rows_of(s - 1)
                    dve.wait_ge(sq_done, i + 1)
                    v.tensor_scalar(arg[0:r, NT + i:NT + i + 1], ssq[0:r, i:i + 1], 1.0 / FH, 1e-6, ALU.mult, ALU.add).then_inc(arg2, 1)
                    dve.wait_ge(yg_done, i + 1)
                    st_.do(v.tensor_reduce(am2[0:r, i:i + 1], sg[0:r, i % 4, :], AX.X, ALU.max, apply_absolute_value=True))
                if s == 3:
                    bk = wait_full(dve, "wz")
                    frees(v.tensor_copy(wb[:, :, D:2 * D], bk[0:HF, 0:2 * D].rearrange("p (c n) -> p c n", c=2)), "wz")
                if s == 7:
                    dve.wait_ge(tw_hi, 4)
                    v.tensor_tensor(wb16[:, 1], wb[:, :, :], wb16[:, 0], ALU.subtract).then_inc(tw_lo, 1)
                if 0 <= s - 4:
                    i, r = s - 4, rows_of(s - 4)
                    bk = wait_full(dve, "down", i)
                    frees(v.scalar_tensor_tensor(out=h[0:r, i, :], in0=bk[0:r, 0:D], scalar=c2[0:r, i:i + 1], in1=h[0:r, i, :],
                                                 op0=ALU.mult, op1=ALU.add), "down", i)
                    wait_evac(dve, "down", i)
                    stats(i, 1.0, 1e-5)
                    if i >= 1:
                        normalise(2 * NT + i, i - 1)
            normalise(3 * NT, NT - 1)
            for i in range(NT):
                r = rows_of(i)
                bk = wait_full(dve, "x1T", i)
                dve.wait_ge(x1_hi, i + 1)
                frees(v.tensor_tensor(xnp[:, 1, :, 128 * i:128 * i + r], bk[0:HF, 0:256].rearrange("p (j n) -> p j n", j=2)[:, :, 0:r],
                                      xnp[:, 0, :, 128 * i:128 * i + r], ALU.subtract), "x1T", i)
            NH3 = 3 * TH
            def heads(ap, n):
                return ap[:, n * NH3:(n + 1) * NH3]

            def flat(x, n):
                return x[:, 3 * n:3 * n + 3, :].rearrange("p t (h c) -> p (t h) c", c=TD)

            def bc(ap):
                return ap.unsqueeze(2).broadcast_to([TR, NH3, TD])

            def rstd(n, k):
                a, b_, c_ = heads(hv[0], n), heads(hv[1], n), heads(hv[2], n)
                if k <= 2:
                    dve.wait_ge(tt_sq, k)
                    st_.then(v.tensor_reduce(a, flat(SQ, n), AX.X, ALU.add))
                    v.tensor_scalar(a, a, 1.0 / TD, 1e-6, ALU.mult, ALU.add).then_inc(tt_var, 1)
                if k == 2:
                    q_low()
                    w_step(0)
                    w_step(1)
                dve.wait_ge(tt_sqrt, k)
                st_.then(v.reciprocal(b_, b_))
                st_.then(v.tensor_tensor(c_, b_, b_, ALU.mult))
                st_.then(v.tensor_tensor(c_, c_, a, ALU.mult))
                st_.then(v.tensor_scalar(c_, c_, -0.5, 1.5, ALU.mult, ALU.add))
                st_.then(v.tensor_tensor(b_, b_, c_, ALU.mult))
                return b_

            def linear(n):
                for t in range(3 * n, 3 * n + 3):
                    bk = wait_full(dve, "B", t)
                    frees(v.tensor_tensor(CZ[:, t, :], bk[0:TR, 0:2 * D + TH], rowb[:, :], ALU.add), "B", t)
                for t in range(3 * n, 3 * n + 3):
                    bk = wait_full(dve, "A", t)
                    dve.wait_ge(k1_hi, t + 1)
                    if t >= 3:
                        dve.wait_ge(km_lo, t - 2)
                    frees(v.tensor_tensor(K16[:, t % 3, 1, :], bk[0:TR, 0:D], K16[:, t % 3, 0, :], ALU.subtract), "A", t)

            def w_step(t):
                for j in range(2):
                    bk = wait_full(dve, "gW", t, j)
                    if t >= 2 and j == 0:
                        dve.wait_ge(w_lo, t - 1)
                    frees(v.tensor_tensor(Wt[:, t % 2, j, :].rearrange("p (g n) -> p g n", g=G3),
                                          bk[0:HF + 1, 0:G3 * HF].rearrange("p (g n) -> p g n", g=G3),
                                          bd[:, :].unsqueeze(1).broadcast_to([HF + 1, G3, HF]), ALU.mult), "gW", t, j)

            def q_low():
                for jo in range(2):
                    for m in range(2):
                        bk = wait_full(dve, "Q", jo, m)
                        dve.wait_ge(q1_hi, 2 * jo + m + 1)
                        o = slice(288 * m, 288 * m + 288)
                        frees(v.scalar_tensor_tensor(out=q16[0:HF, 1, jo, o], in0=bk[0:HF, 0:288], scalar=cols[:, 8 + jo:9 + jo],
                                                     in1=q16[0:HF, 0, jo, o], op0=ALU.add, op1=ALU.subtract), "Q", jo, m)

            def rstd_spread(n):
                wait_evac(dve, "var", 3 * n + 2)
                r_ = rstd(n, 2 + n + 1)
                e_ = E16[:, 3 * n:3 * n + 3]
                rb = r_.rearrange("p (t h) -> p t h", h=TH).unsqueeze(3).broadcast_to([TR, 3, TH, TD])
                st_.then(v.tensor_copy(e_[:, :, 0, :].rearrange("p t (h c) -> p t h c", c=TD), rb))
                v.tensor_tensor(e_[:, :, 1, :].rearrange("p t (h c) -> p t h c", c=TD), rb,
                                e_[:, :, 0, :].rearrange("p t (h c) -> p t h c", c=TD), ALU.subtract).then_inc(e_done, 1)

            for n in range(2):
                linear(n)
                r_ = rstd(n, n + 1)
                z = CZ[:, 3 * n:3 * n + 3, D:2 * D]
                xh, gg, sq = flat(XH, n), flat(GG, n), flat(SQ, n)
                st_.then(v.tensor_tensor(XH[:, 3 * n:3 * n + 3, :].rearrange("p t (h c) -> p t h c", c=TD),
                                         z.rearrange("p t (h c) -> p t h c", c=TD),
                                         r_.rearrange("p (t h) -> p t h", h=TH).unsqueeze(3).broadcast_to([TR, 3, TH, TD]), ALU.mult))
                st_.then(v.tensor_tensor(GG[:, 3 * n:3 * n + 3, :], XH[:, 3 * n:3 * n + 3, :],
                                         gam2[:, :].unsqueeze(1).broadcast_to([TR, 3, D]), ALU.mult))
                st_.then(v.tensor_tensor(GG[:, 3 * n:3 * n + 3, :], GG[:, 3 * n:3 * n + 3, :], CZ[:, 3 * n:3 * n + 3, 0:D], ALU.add))
                st_.do(v.tensor_tensor(sq, gg, xh, ALU.mult))
                st_.do(v.tensor_reduce(heads(hv[3], n), gg, AX.X, ALU.add))
                st_.settle()
                st_.then(v.tensor_reduce(heads(hv[4], n), sq, AX.X, ALU.add))
                st_.do(v.tensor_scalar(heads(hv[4], n), heads(hv[4], n), 1.0 / TD, None, ALU.mult))
                st_.do(v.tensor_scalar(heads(hv[3], n), heads(hv[3], n), 1.0 / TD, None, ALU.mult))
                st_.settle()
                dve.wait_ge(tt_sig, n + 1)
                st_.do(v.scalar_tensor_tensor(out=heads(hv[5], n), in0=r_, scalar=-1.0 / (TD * NP),
                                              in1=sig[:, 3 * n:3 * n + 3, :].rearrange("p t h -> p (t h)"), op0=ALU.mult, op1=ALU.mult))
                st_.then(v.tensor_tensor(sq, xh, bc(heads(hv[4], n)), ALU.mult))
                st_.then(v.tensor_tensor(gg, gg, sq, ALU.subtract))
                st_.then(v.tensor_tensor(gg, gg, bc(heads(hv[3], n)), ALU.subtract))
                v.tensor_tensor(gg, gg, bc(heads(hv[5], n)), ALU.mult).then_inc(tt_g, 1)
                dve.wait_ge(tt_ghi, n + 1)
                v.tensor_tensor(G16[:, 3 * n:3 * n + 3, 1, :], GG[:, 3 * n:3 * n + 3, :], G16[:, 3 * n:3 * n + 3, 0, :],
                                ALU.subtract).then_inc(tt_glo, 1)
            for t in range(TT + 3):
                if 2 <= t < TT:
                    w_step(t)
                u = t - 3
                if u >= 0:
                    bk = wait_full(dve, "var", u)
                    frees(v.tensor_scalar(hv[0][:, TH * u:TH * u + TH], bk[0:TR, 0:TH], 1.0 / TD, 1e-6, ALU.mult, ALU.add), "var", u)
                u = t - 2
                if 0 <= u < TT:
                    dve.wait_ge(z_copied, u + 1)
                    z = zT[:, u]
                    f = sqf[:, u % 2, :].rearrange("p (j n) -> p j n", j=2)
                    st_.then(v.tensor_tensor(f, z, z, ALU.mult))
                    wait_evac(dve, "Z", u)
                    v.tensor_tensor(sq16[:, u % 2, 1, :], sqf[:, u % 2, :], sq16[:, u % 2, 0, :], ALU.subtract).then_inc(sq_lo, 1)
                if t == 7:
                    rstd_spread(0)
            rstd_spread(1)
            for n in range(2):
                for t in range(3 * n, 3 * n + 3):
                    bk = wait_full(dve, "R", t)
                    for j in range(2):
                        ins = v.scalar_tensor_tensor(out=zT[:, t, j, :], in0=bk[0:HF, TR * j:TR * j + TR], scalar=cols[:, 4 + j:5 + j],
                                                     in1=zT[:, t, j, :], op0=ALU.mult, op1=ALU.mult)
                        if j == 0:
                            st_.do(ins)
                    frees(ins, "R", t)
                wait_evac(dve, "R", 3 * n + 2)
                st_.settle()
                g_ = slice(3 * n, 3 * n + 3)
                for j in range(2):
                    q_ = qtb[:, j, 3 * TR * n:3 * TR * (n + 1)].rearrange("p (t n) -> p t n", t=3)
                    ins = v.tensor_tensor(zT[:, g_, j, :], zT[:, g_, j, :], q_, ALU.add)
                    if j == 0:
                        st_.do(ins)
                ins.then_inc(o_done, 1)
                dve.wait_ge(o_done, n + 1)
                dve.wait_ge(o_hi, n + 1)
                for j in range(2):
                    c = slice(3 * TR * n, 3 * TR * (n + 1))
                    ins = v.tensor_tensor(xnp[:, 1, j, c].rearrange("p (t n) -> p t n", t=3), zT[:, g_, j, :],
                                          xnp[:, 0, j, c].rearrange("p (t n) -> p t n", t=3), ALU.subtract)
                    if j == 0:
                        st_.do(ins)
                ins.then_inc(o_lo, 1)
            dve.wait_ge(hbias, 2)
            for i in range(NT):
                r = rows_of(i)
                bk = wait_full(dve, "proj", i)
                frees(v.tensor_tensor(h[0:r, i, :], bk[0:r, 0:D], h[0:r, i, :], ALU.add), "proj", i)
                wait_evac(dve, "proj", i)
                stats(i, 1.0, 1e-5, (1.0 + 0.25e-6, 0.25e-11))
                if i >= 1:
                    normalise(3 * NT + i, i - 1)
            normalise(4 * NT, NT - 1)
            for i in range(NT):
                r = rows_of(i)
                v.tensor_scalar(xs[0:r, i, :], h[0:r, i, :], mv[0:r, i, 0:1], rs[0:r, NT + i:NT + i + 1],
                                ALU.subtract, ALU.mult).then_inc(xs_f, 1)
            bk = wait_full(dve, "logits")
            dve.wait_ge(zeroed, 6)
            st_.do(v.tensor_copy(lg[:, 0:NT - 1, :], bk[:, 0:E * (NT - 1)].rearrange("p (i e) -> p i e", e=E)))
            frees(v.tensor_copy(lg[0:64, NT - 1, :], bk[0:64, E * (NT - 1):E * NT]), "logits")
            st_.settle()
            wait_evac(dve, "logits")
            for i in range(NT):
                st_.do(v.max(top[:, i, :], lg[:, i, :]))
            st_.settle()
            for i in range(NT):
                st_.do(v.max_index(topi[:, i, :], top[:, i, :], lg[:, i, :]))
            v.tensor_tensor(wts[:, :, 0], top[:, :, 1], top[:, :, 0], ALU.subtract).then_inc(lam, 1)
            st_.settle()
            st_.then(v.tensor_copy(topf[:], topi[:]))
            dve.wait_ge(loaded("iota8"), 16)
            i8 = iota8[:, :].unsqueeze(1).broadcast_to([128, NT, E])
            st_.do(v.tensor_tensor(m1[:], i8, topf[:, :, 0:1].broadcast_to([128, NT, E]), ALU.is_equal))
            st_.do(v.tensor_tensor(m2[:], i8, topf[:, :, 1:2].broadcast_to([128, NT, E]), ALU.is_equal))
            st_.settle()
            st_.do(v.tensor_tensor(mk[:], m1[:], m2[:], ALU.add))
            v.tensor_tensor(mk16[:], m1[:], m2[:], ALU.add).then_inc(mk_done, 1)
            for i in range(NT):
                r = rows_of(i)
                dve.wait_ge(xs_hi, i + 1)
                ins = v.tensor_tensor(xsp[0:r, 1, i, :], xs[0:r, i, :], xsp[0:r, 0, i, :], ALU.subtract)
                if i < NT - 1:
                    st_.do(ins)
            ins.then_inc(xs_done, 1)
            dve.wait_ge(ex1, 1)
            st_.then(v.tensor_scalar(wts[:, :, 2], wts[:, :, 1], 1.0, None, ALU.add))
            st_.then(v.reciprocal(wts[:, :, 2], wts[:, :, 2]))
            st_.then(v.tensor_tensor(wts[:, :, 3], wts[:, :, 1], wts[:, :, 2], ALU.mult))
            st_.do(v.tensor_tensor(m1[:], m1[:], wts[:, :, 2:3].broadcast_to([128, NT, E]), ALU.mult))
            st_.do(v.tensor_tensor(m2[:], m2[:], wts[:, :, 3:4].broadcast_to([128, NT, E]), ALU.mult))
            st_.settle()
            st_.then(v.tensor_tensor(cw[:], m1[:], m2[:], ALU.add))
            st_.then(v.tensor_copy(cwp[:, :, :, 0], cw[:]))
            v.tensor_tensor(cwp[:, :, :, 1], cw[:], cwp[:, :, :, 0], ALU.subtract).then_inc(cw_done, 1)
            bk = wait_full(dve, "pos")
            st_.do(v.tensor_scalar(posf[:, 0:NT - 1, :], bk[:, 0:E * (NT - 1)].rearrange("p (i e) -> p i e", e=E), 1.0, None, ALU.add))
            frees(v.tensor_scalar(posf[0:64, NT - 1, :], bk[0:64, E * (NT - 1):E * NT], 1.0, None, ALU.add), "pos")
            st_.settle()
            wait_evac(dve, "pos")
            st_.then(v.tensor_tensor(posf[:], posf[:], mk[:], ALU.mult))
            st_.do(v.tensor_scalar(kp[:], posf[:], float(CAP), None, ALU.is_le))
            st_.do(v.tensor_scalar(posf[:], posf[:], -1.0, None, ALU.add))
            st_.settle()
            st_.do(v.tensor_tensor(kp[:], kp[:], cw[:], ALU.mult))
            v.tensor_copy(pos16[:], posf[:]).then_inc(pos_done, 1)
            st_.settle()
            st_.then(v.tensor_reduce(kw[:], kp[:], AX.X, ALU.add))
            dve.wait_ge(loaded("iota"), 16)
            dve.wait_ge(loaded("slot"), 16)

            def onehots(e):
                if e >= 2:
                    wait_full(dve, "z", e - 2)
                for i in range(NT):
                    r = rows_of(i)
                    ins = v.tensor_scalar(oh[0:r, e % 2, i, :], iota[0:r, :], posf[0:r, i, e:e + 1], None, ALU.is_equal)
                    if i < NT - 1:
                        st_.do(ins)
                ins.then_inc(oh_done, 1)

            def onehots_t(e):
                wait_evac(dve, "posb", e, 0)
                wait_evac(dve, "posb", e, 1)
                if e >= 2:
                    dve.wait_ge(moe_combined, e - 1)
                st_.do(v.tensor_scalar(ohT[:, e % 2, 0, :], posb[:, :], slot[:, 0:1], None, ALU.is_equal))
                v.tensor_scalar(ohT[:, e % 2, 1, :], posb[:, :], slot[:, 1:2], None, ALU.is_equal).then_inc(oht_done, 1)

            def z_split(e):
                wait_evac(dve, "z", e)
                if e >= 1:
                    wait_full(dve, "u", e - 1, 1)
                st_.then(v.tensor_copy(zp[:, 0], zf[:, :, :]))
                v.tensor_tensor(zp[:, 1], zf[:, :, :], zp[:, 0], ALU.subtract).then_inc(z_done, 1)
                st_.then(v.tensor_tensor(cws[:, e % 2, :], cwx[:, e % 2, :, 0], cwx[:, e % 2, :, 1], ALU.add))

            onehots(0)
            for s in range(E + 1):
                if s == 2:
                    for i in range(NT):
                        r = rows_of(i)
                        st_.do(v.scalar_tensor_tensor(out=h[0:r, i, :], in0=xc[0:r, i, :], scalar=kw[0:r, i:i + 1],
                                                      in1=h[0:r, i, :], op0=ALU.mult, op1=ALU.add))
                if s < E:
                    z_split(s)
                if s >= 1:
                    e = s - 1
                    bk = wait_full(dve, "y", e)
                    if e >= 1:
                        dve.wait_ge(moe_combined, e)
                    for k in range(2):
                        ins = v.tensor_scalar(yf[:, k, :], bk[0:SH, D * k:D * k + D], cws[:, e % 2, k:k + 1], None, ALU.mult)
                        if k == 0:
                            st_.do(ins)
                    frees(ins, "y", e)
                    wait_evac(dve, "y", e)
                    st_.then(v.tensor_copy(yp[:, 0], yf[:, :, :]))
                    v.tensor_tensor(yp[:, 1], yf[:, :, :], yp[:, 0], ALU.subtract).then_inc(yp_done, 1)
                if s < E:
                    onehots_t(s)
                    if s + 1 < E:
                        onehots(s + 1)
                    for rnd in range(2):
                        bk = wait_full(dve, "u", s, rnd)
                        wait_evac(dve, "g", s, rnd)
                        if s >= 1 and rnd == 0:
                            dve.wait_ge(acth, s)
                            dve.wait_ge(act_done, s)
                        frees(v.tensor_tensor(actf[:, 2 * rnd:2 * rnd + 2, :], bk[:, 0:2 * CAP].rearrange("p (m n) -> p m n", m=2),
                                              sgm[:, rnd, :].rearrange("p (m n) -> p m n", m=2), ALU.mult), "u", s, rnd)
                    wait_evac(dve, "u", s, 1)
                    dve.wait_ge(acth, s + 1)
                    v.tensor_tensor(actp[:, 1], actf[:, :, :], actp[:, 0], ALU.subtract).then_inc(act_done, 1)
            st_.settle()
            for i in range(NT):
                r = rows_of(i)
                bk = wait_full(dve, "acc", i // 2)
                v.tensor_tensor(h[0:r, i, :], bk[0:r, D * (i % 2):D * (i % 2) + D], h[0:r, i, :], ALU.add).then_inc(fin, 1)

        @block.scalar
        def _(act):
            st_ = Steps(act, act_s)
            a = nc.scalar.activation

            def table(function):
                act.wait_ge(pool_s, 1)
                st_.then(a(warm[:, :], half_[:, 0:1], function, scale=-1.0))

            for k in range(KC):
                act.wait_ge(loaded(f"x{k}"), 32)
                a(xpT[:, 0, k, :], xraw[:, k, :], ACT.Copy).then_inc(x_hi, 1)
                a(wp16[:, 0, k, :], wpraw[:, k, :], ACT.Copy).then_inc(x_hi, 1)
            act.wait_ge(loaded("cols"), 16)
            act.wait_ge(loaded("wv"), 16)
            a(wqkv[:, 0, :, 1536:], wqkvraw[:, :, 1536:], ACT.Copy).then_inc(wv_hi, 1)
            act.wait_ge(loaded("wk"), 16)
            a(wqkv[:, 0, :, 768:1536], wqkvraw[:, :, 768:1536], ACT.Copy).then_inc(wqk_hi, 1)
            for i in range(NT):
                r = rows_of(i)
                bk = wait_full(act, "xnT", i)
                for j in range(2):
                    ins = a(xnT[:, j, 128 * i:128 * i + r], bk[0:HF, 128 * j:128 * j + r], ACT.Identity,
                            scale=cols[:, j:j + 1], bias=cols[:, 2 + j:3 + j])
                frees(ins, "xnT", i)
                wait_evac(act, "xnT", i)
                a(x16[:, 0, :, 128 * i:128 * i + r], xnT[:, :, 128 * i:128 * i + r], ACT.Copy).then_inc(xn_hi, 1)
            act.wait_ge(loaded("wq"), 16)
            a(wqkv[:, 0, :, 0:768], wqkvraw[:, :, 0:768], ACT.Copy).then_inc(wqk_hi, 1)
            for i in range(NT):
                r = rows_of(i)
                for c in range(2):
                    bk = wait_full(act, "v", i, c)
                    a(v_sb[0:r, i, 6 * c:6 * c + 6, :, 0], bk[0:r, 0:384].rearrange("p (h c) -> p h c", h=6),
                      ACT.Copy).then_inc(v_hi, 1)
            act.wait_ge(zeroed, 1)
            for hp in range(HP):
                if hp == 4:
                    act.wait_ge(wq_sum, 1)
                    a(w2q[:], stage2[:], ACT.Identity, bias=nmagic[:, 0:1]).then_inc(wq_done, 1)
                for n in range(2):
                    bk = wait_full(act, "k", hp, n)
                    for x in range(2):
                        o = slice(64 * x, 64 * x + 64)
                        ins = a(Kbd[o, 0, hp, 8 * n:8 * n + 8, NP * x:NP * x + NP],
                                bk[o, 0:288].rearrange("p (b k) -> p b k", k=NP), ACT.Copy)
                    ins.then_inc(k_hi, 1)
                for n in range(2):
                    bk = wait_full(act, "q", hp, n)
                    a(qT[:, 0, hp, 288 * n:288 * n + 288], bk[:, 0:288], ACT.Copy, scale=AD ** -0.5).then_inc(q_hi, 1)
            act.wait_ge(wq_sum, 2)
            a(wiq[:], stage13[:], ACT.Identity, bias=nmagic[0:HF, 0:1]).then_inc(wq_done, 1)
            for s in range(PAIRS + 3):
                if s < PAIRS:
                    wait_evac(act, "S", s)
                    a(P[:, s % 3, :], P[:, s % 3, :], ACT.Exp).then_inc(exped, 1)
                p = s - 2
                if 0 <= p < PAIRS:
                    if p >= 2:
                        wait_full(act, "PV", p - 2)
                    bk = wait_full(act, "PT", p, 0)
                    frees(a(PT[:, p % 2, 0, :], bk[0:72, :].bitcast(F16)[:, 0:768], ACT.Copy), "PT", p, 0)
                p = s - 1
                if 0 <= p < PAIRS:
                    act.wait_ge(normed, p + 1)
                    if p >= 2:
                        wait_full(act, "PT", p - 2, 0)
                    a(P16[:, p % 2, 0, :], P[:, p % 3, :], ACT.Copy).then_inc(p_hi, 1)
                p = s - 3
                if 0 <= p < PAIRS:
                    bk = wait_full(act, "PV", p)
                    a(aoT[:, 0, :, 72 * p:72 * p + 72], bk[:, 0:432].rearrange("p (h q) -> p h q", h=HP),
                      ACT.Copy).then_inc(ao_hi, 1)
                if s == 4:
                    act.wait_ge(loaded("woT"), 16)
                    a(woT[:, 0], woraw, ACT.Copy).then_inc(wo_hi, 1)
            split_high(act, 0)
            table(ACT.Silu)
            for name in ("wa", "wpj"):
                act.wait_ge(loaded(name), 16)
            a(wa16[:, 0], wa[:, :, :], ACT.Copy).then_inc(tw_hi, 1)
            a(wpj16[:, 0], wpj[:, :, :], ACT.Copy).then_inc(tw_hi, 1)
            def xi_quantised(tiles):
                for i in tiles:
                    r = rows_of(i)
                    act.wait_ge(x_round, i + 1)
                    a(xi[0:r, i, :], xc[0:r, i, :], ACT.Identity, bias=nmagic[0:r, 0:1]).then_inc(q_ready, 1)
                for i in tiles:
                    r = rows_of(i)
                    bk = wait_full(act, "xiT", i)
                    frees(a(xiT[:, :, 128 * i:128 * i + r],
                            bk[0:HF, :].bitcast(BF16)[:, 0:256].rearrange("p (j n) -> p j n", j=2)[:, :, 0:r], ACT.Copy), "xiT", i)

            xi_quantised(range(3))
            for s in range(NT + 3):
                if s < NT:
                    i, r = s, rows_of(s)
                    bk = wait_full(act, "gate", i)
                    frees(a(sg[0:r, i % 4, :], bk[0:r, :], ACT.Silu, scale=c1[0:r, i:i + 1]), "gate", i)
                if s == 0:
                    xi_quantised(range(3, NT))
                if 0 <= s - 1 < NT:
                    i, r = s - 1, rows_of(s - 1)
                    wait_evac(act, "up", i)
                    if i >= 1:
                        act.wait_ge(sq_done, i)
                    a(junk[0:r, :], y[0:r, i % 3, :], ACT.Square, accum_out=ssq[0:r, i:i + 1]).then_inc(sq_done, 1)
                if 0 <= s - 3:
                    i, r = s - 3, rows_of(s - 3)
                    bk = wait_full(act, "yiT", i)
                    if i >= 2:
                        wait_full(act, "down", i - 2)
                    frees(a(yiT[:, i % 2, :, 0:r], bk[:, :].bitcast(BF16)[:, 0:512].rearrange("p (m n) -> p m n", m=4)[:, :, 0:r],
                            ACT.Copy), "yiT", i)
                if 0 <= s - 2 < NT:
                    i, r = s - 2, rows_of(s - 2)
                    act.wait_ge(y_round, i + 1)
                    if i >= 2:
                        wait_full(act, "yiT", i - 2)
                    a(yi[0:r, i % 2, :], sg[0:r, i % 4, :], ACT.Identity, bias=nmagic[0:r, 0:1]).then_inc(yi_done, 1)
                if s == 0:
                    act.wait_ge(bdw1_done, 2)
                    a(base16[:, 0], bdw1[:, :, :], ACT.Copy).then_inc(tw_hi, 1)
                if s == 6:
                    wait_evac(act, "wz")
                    act.wait_ge(loaded("lrT"), 16)
                    a(wb16[:, 0], wb[:, :, :], ACT.Copy).then_inc(tw_hi, 1)
            for i in range(NT):
                r = rows_of(i)
                bk = wait_full(act, "x1T", i)
                a(xnp[:, 0, :, 128 * i:128 * i + r], bk[0:HF, 0:256].rearrange("p (j n) -> p j n", j=2)[:, :, 0:r],
                  ACT.Copy).then_inc(x1_hi, 1)
            def k_high(t):
                bk = wait_full(act, "A", t)
                if t >= 3:
                    act.wait_ge(km_hi, t - 2)
                a(K16[:, t % 3, 0, :], bk[0:TR, 0:D], ACT.Copy).then_inc(k1_hi, 1)

            def z_square(n):
                wait_evac(act, "B", 3 * n + 2)
                a(SQ[:, 3 * n:3 * n + 3, :], CZ[:, 3 * n:3 * n + 3, D:2 * D], ACT.Square).then_inc(tt_sq, 1)

            def rates(n):
                a(sig[:, 3 * n:3 * n + 3, :], CZ[:, 3 * n:3 * n + 3, 2 * D:], ACT.Sigmoid).then_inc(tt_sig, 1)

            def roots(k):
                n = k % 2
                if k < 2:
                    act.wait_ge(tt_var, k + 1)
                else:
                    for t in range(3 * n, 3 * n + 3):
                        wait_evac(act, "var", t)
                a(hv[1][:, n * 36:n * 36 + 36], hv[0][:, n * 36:n * 36 + 36], ACT.Sqrt).then_inc(tt_sqrt, 1)

            def gradient_high(n):
                act.wait_ge(tt_g, n + 1)
                a(G16[:, 3 * n:3 * n + 3, 0, :], GG[:, 3 * n:3 * n + 3, :], ACT.Copy).then_inc(tt_ghi, 1)

            table(ACT.Sqrt)
            z_square(0)
            for t in range(3):
                k_high(t)
            roots(0)
            rates(0)
            table(ACT.Sqrt)
            split_high(act, 1)
            for t in range(3, 6):
                k_high(t)
            gradient_high(0)
            z_square(1)
            act.wait_ge(zeroed, 5)
            for j in range(2):
                for n in range(2):
                    bk = wait_full(act, "Q", j, n)
                    a(q16[0:HF, 0, j, 288 * n:288 * n + 288], bk[0:HF, 0:288], ACT.Identity, bias=cols[:, 8 + j:9 + j])
                    a(qtb[:, j, 288 * n:288 * n + 288], bk[0:HF, 0:288], ACT.Identity, bias=qbt[:, j:j + 1]).then_inc(q1_hi, 1)
                if j == 0:
                    roots(1)
            rates(1)
            table(ACT.Sqrt)

            def w_high(t):
                wait_evac(act, "gW", t, 0)
                wait_evac(act, "gW", t, 1)
                if t >= 2:
                    wait_full(act, "Z", t - 2)
                a(W16[t % 2][:, 0], Wt[:, t % 2], ACT.Copy).then_inc(w_hi, 1)

            def z_high(u):
                bk = wait_full(act, "Z", u)
                z = bk[0:HF, 0:2 * TR]
                a(zT[:, u], z.rearrange("p (j n) -> p j n", j=2), ACT.Copy).then_inc(z_copied, 1)
                if u >= 2:
                    wait_full(act, "var", u - 2)
                frees(a(sq16[:, u % 2, 0, :], z, ACT.Square), "Z", u)

            w_high(0)
            w_high(1)
            split_high(act, 2)
            gradient_high(1)
            for t in range(2, TT + 2):
                if t < TT:
                    w_high(t)
                z_high(t - 2)
                if t == 6:
                    roots(2)
            roots(3)
            table(ACT.Exp)
            split_high(act, 3)
            for n in range(2):
                act.wait_ge(o_done, n + 1)
                for j in range(2):
                    c = slice(3 * TR * n, 3 * TR * (n + 1))
                    ins = a(xnp[:, 0, j, c].rearrange("p (t n) -> p t n", t=3), zT[:, 3 * n:3 * n + 3, j, :], ACT.Copy)
                    if j == 0:
                        st_.do(ins)
                ins.then_inc(o_hi, 1)
            for i in range(NT):
                r = rows_of(i)
                bk = wait_full(act, "x2T", i)
                if i == 0:
                    wait_full(act, "proj", NT - 1)
                frees(a(xnT[:, :, 128 * i:128 * i + r], bk[0:HF, 0:256].rearrange("p (j n) -> p j n", j=2)[:, :, 0:r],
                        ACT.Copy), "x2T", i)
            for i in range(NT):
                r = rows_of(i)
                act.wait_ge(xs_f, i + 1)
                a(xsp[0:r, 0, i, :], xs[0:r, i, :], ACT.Copy).then_inc(xs_hi, 1)
            act.wait_ge(lam, 1)
            a(wts[:, :, 1], wts[:, :, 0], ACT.Exp).then_inc(ex1, 1)
            table(ACT.Silu)
            split_high(act, 4)
            for s in range(E):
                if s >= 1:
                    act.wait_ge(oht_done, s)
                for c in range(2):
                    bk = wait_full(act, "posb", s, c)
                    n = (384, T - 384)[c]
                    frees(a(posb[:, 384 * c:384 * c + n], bk[0:SH, 0:n], ACT.Copy), "posb", s, c)
                bk = wait_full(act, "z", s)
                if s >= 1:
                    act.wait_ge(z_done, s)
                if s >= 2:
                    act.wait_ge(yp_done, s - 1)
                for j in range(2):
                    st_.do(a(zf[:, j, :], bk[0:HF, CAP * j:CAP * j + CAP], ACT.Copy, scale=nw[:, j, s:s + 1]))
                frees(a(cwx[:, s % 2], bk[0:SH, 2 * CAP:2 * CAP + 4].rearrange("p (s x) -> p s x", s=2), ACT.Copy), "z", s)
                if s in (1, 3, 5):
                    split_high(act, 5 + s // 2)
                for rnd in range(2):
                    bk = wait_full(act, "g", s, rnd)
                    if s >= 1:
                        wait_evac(act, "u", s - 1, rnd)
                    frees(a(sgm[:, rnd, :], bk[:, 0:2 * CAP], ACT.Silu), "g", s, rnd)
                wait_evac(act, "u", s, 0)
                wait_evac(act, "u", s, 1)
                if s >= 1:
                    wait_full(act, "y", s - 1)
                a(actp[:, 0], actf[:, :, :], ACT.Copy).then_inc(acth, 1)

        @block.gpsimd
        def _(pool):
            st_ = Steps(pool, pool_s)
            g = nc.gpsimd
            g.memset(half_[:], -0.5).then_inc(pool_s, 1)
            st_.n += 1
            st_.do(g.memset(ones16[:], 1.0))
            st_.do(g.memset(ones[:], 1.0))
            st_.do(g.memset(nmagic[:], -MAGIC))
            st_.do(g.memset(am[:], 0.0))
            st_.do(g.memset(qT[:, :, :, T:], 0.0))
            st_.settle()
            g.memset(arenaK[:, 0:K_W], 0.0).then_inc(zeroed, 1)

            def power(sem_in, n, i, o, sem_out):
                r = rows_of(i)
                pool.wait_ge(sem_in, n)
                g.tensor_tensor(rs[0:r, o + i:o + i + 1], arg[0:r, o + i:o + i + 1], half_[0:r, 0:1], ALU.pow).then_inc(sem_out, 1)

            def weight_low(n, w, w16):
                pool.wait_ge(tw_hi, n + 1)
                g.tensor_tensor(w16[:, 1], w[:, :, :], w16[:, 0], ALU.subtract).then_inc(tw_lo, 1)

            for i in range(NT):
                power(ln_arg, i + 1, i, 0, ln_pow)
            for n in range(2):
                pool.wait_ge(wqk_hi, n + 1)
                o = slice(768 - 768 * n, 1536 - 768 * n)
                g.tensor_tensor(wqkv[:, 1, :, o], wqkvraw[:, :, o], wqkv[:, 0, :, o], ALU.subtract).then_inc(wqk_lo, 1)
            pool.wait_ge(wqk_lo, 2)
            pool.wait_ge(wv_lo, 1)
            wait_full(pool, "embed", NT - 1)
            g.memset(arenaV[0:72, :], 0.0).then_inc(zeroed, 1)
            pool.wait_ge(ln_x, NT)
            pool.wait_ge(loaded("rows"), 16)
            for i in range(NT):
                r = rows_of(i)
                ins = g.tensor_tensor(h[0:r, i, :], h[0:r, i, :], row("b_out", r), ALU.add)
                if i < NT - 1:
                    st_.do(ins)
            ins.then_inc(hbias, 1)
            for p in range(PAIRS):
                pool.wait_ge(rinved, p + 1)
                pv = P[:, p % 3, :].rearrange("p (h k) -> p h k", k=NP)
                g.tensor_tensor(pv, pv, ri[:, p % 2, :].unsqueeze(2).broadcast_to([128, AH, NP]), ALU.mult).then_inc(normed, 1)
                if p == 4:
                    pool.wait_ge(wo_hi, 1)
                    g.tensor_tensor(woT[:, 1], woraw, woT[:, 0], ALU.subtract).then_inc(wo_lo, 1)
            for i in range(NT):
                power(ln_arg, NT + i + 1, i, 0, ln_pow)
            split_low(pool, 0)
            weight_low(0, wa, wa16)
            weight_low(1, wpj, wpj16)
            for s in range(NT + 1):
                if s < NT:
                    i, r = s, rows_of(s)
                    wait_evac(pool, "up", i)
                    g.tensor_tensor(sg[0:r, i % 4, :], y[0:r, i % 3, :], row("g_out", r), ALU.mult).then_inc(yg_done, 1)
                if s >= 1:
                    power(arg2, s, s - 1, NT, pow2)
            weight_low(2, bdw1, base16)
            for i in range(NT):
                power(ln_arg, 2 * NT + i + 1, i, 0, ln_pow)
            g.memset(xnp[:, :, :, T:], 0.0).then_inc(zeroed, 1)
            wait_full(pool, "down", NT - 1)
            st_.do(g.memset(W16f[:, :, W_N:], 0.0))
            st_.do(g.memset(base16f[:, 4 * HF:], 0.0))
            st_.settle()
            for t in range(TT):
                st_.do(g.memset(Kmf[t][:, KM_N:], 0.0))
                st_.do(g.memset(Km[t][:, 1, :, :, HF:HF + 1], 0.0))
                ins = g.tensor_copy(Km[t][:, 0, :, :, HF], bmask[:, :].unsqueeze(2).broadcast_to([TR, G3, 2]))
                if t < TT - 1:
                    st_.do(ins)
            ins.then_inc(zeroed, 1)
            for t in range(TT):
                wait_evac(pool, "A", t)
                for x, done in enumerate((km_hi, km_lo)):
                    g.tensor_tensor(Km[t][:, x, :, :, 0:HF],
                                    K16[:, t % 3, x, :].rearrange("p (j n) -> p j n", j=2).unsqueeze(1).broadcast_to([TR, G3, 2, HF]),
                                    bmask[:, :].unsqueeze(2).unsqueeze(3).broadcast_to([TR, G3, 2, HF]), ALU.mult).then_inc(done, 1)
                if t == 0:
                    st_.do(g.memset(qtb[:, :, T:], 0.0))
                    st_.do(g.memset(q16[:, 1, :, :], 0.0))
                    st_.then(g.memset(q16[0:HF, 0, :, T:], 0.0))
                    g.memset(q16[HF:HF + 1, 0, :, :], 1.0).then_inc(zeroed, 1)
                    pool.wait_ge(zeroed, 5)
                if t == 2:
                    split_low(pool, 1)
            for t in range(TT):
                if t == 2:
                    split_low(pool, 2)
                pool.wait_ge(w_hi, t + 1)
                g.tensor_tensor(W16[t % 2][:, 1], Wt[:, t % 2], W16[t % 2][:, 0], ALU.subtract).then_inc(w_lo, 1)
            pool.wait_ge(ln_x, 2 * NT)
            for i in range(NT):
                r = rows_of(i)
                ins = g.tensor_tensor(h[0:r, i, :], h[0:r, i, :], row("pb", r), ALU.add)
                if i < NT - 1:
                    st_.do(ins)
            ins.then_inc(hbias, 1)
            split_low(pool, 3)
            for i in range(NT):
                r = rows_of(i)
                pool.wait_ge(ln_arg, 3 * NT + i + 1)
                both = [x[0:r, :].rearrange("p (x n) -> p x n", x=2)[:, :, i] for x in (rs, arg, half_)]
                g.tensor_tensor(both[0], both[1], both[2], ALU.pow).then_inc(ln_pow, 1)
                if i == 1:
                    wait_full(pool, "proj", NT - 1)
                    st_.then(g.memset(lg[:], 0.0))
                    g.memset(posf[:], 0.0).then_inc(zeroed, 1)
            split_low(pool, 4)
            split_low(pool, 5)
            split_low(pool, 6)
            split_low(pool, 7)


def laid_out(x):
    c = np.ascontiguousarray

    def tiles(a, p):
        return c(a.reshape(a.shape[0] // p, p, *a.shape[1:]).swapaxes(0, 1))

    patches = x["x"].reshape(B, 3, 6, 16, 6, 16).transpose(1, 3, 5, 0, 2, 4).reshape(CPP, T)
    rows = [x["L1_attn_v_bias"], x["L0_tok_b_proj"], x["L1_attn_ttt_lr_bias"].reshape(-1), x["L0_attn_b_out"], x["L0_ffn_g_in"],
            x["L0_ffn_g_out"], x["L1_attn_proj_bias"], x["L1_attn_ttt_norm_weight"].reshape(-1),
            x["L1_attn_ttt_norm_bias"].reshape(-1), x["L1_attn_b1"].reshape(-1)]
    qkv = x["L1_attn_qkv_weight"]
    img = np.arange(TR) // NP
    head = np.arange(HF) // TD
    return {
        "xT": tiles(patches, 128),
        "wpT": tiles(x["L0_tok_W_proj"].T, 128),
        "rows": np.concatenate(rows),
        "cols": c(np.concatenate([x[n].reshape(2, HF) for n in (
            "L0_attn_gamma", "L0_attn_beta", "L1_attn_ttt_norm_weight", "L1_attn_ttt_norm_bias", "L1_attn_q_bias")]).T),
        "wqkv": tiles(x["L0_attn_w_qkv"], HF),
        "woT": tiles(x["L0_attn_w_out"], 128),
        "w_in": tiles(x["L0_ffn_w_in"].T, HF),
        "w_out2": tiles(x["L0_ffn_w_out"].T, 128),
        "wa": tiles(qkv[0:2 * D].T, HF),
        "wvT": tiles(qkv[2 * D:].T, HF),
        "wkn": tiles(qkv[D:2 * D], HF),
        "lrT": tiles(x["L1_attn_ttt_lr_weight"].reshape(TH, D).T, HF),
        "w1s": tiles(x["L1_attn_W1"].reshape(D, TD), HF),
        "wpj": tiles(x["L1_attn_proj_weight"].T, HF),
        "gateT": tiles(x["L1_ffn_gate_w"].T, HF),
        "nw": tiles(x["L1_ffn_norm_w"].T, HF),
        "w13": c(x["L1_ffn_w13"].transpose(2, 0, 1).reshape(2, HF, E, 2 * FH).transpose(1, 2, 0, 3)),
        "w2": c(x["L1_ffn_w2"].transpose(2, 0, 1).reshape(4, 128, E, D).transpose(1, 2, 0, 3)),
        "idf": np.eye(128, dtype=np.float32),
        "idh": np.eye(128, dtype=np.float16),
        "tri": np.triu(np.ones((128, 128)), 1).astype(np.float16),
        "iota": c(np.broadcast_to(np.arange(CAP), (128, CAP)).astype(np.float16)),
        "iota8": c(np.broadcast_to(np.arange(E), (128, E)).astype(np.float32)),
        "slot": np.arange(CAP).reshape(2, SH).T.astype(np.float32).copy(),
        "bmask": (img[:, None] == np.arange(G3)).astype(np.float32),
        "hsel": c((np.arange(D)[:, None] // TD == np.arange(TH)).astype(np.float16).reshape(2, HF, TH).swapaxes(0, 1)),
        "bd": np.concatenate([head[:, None] == head[None, :], np.ones((1, HF), bool)]).astype(np.float32),
    }


def kernel(**inputs):
    import concourse.bacc as _bacc
    from concourse.bass_utils import run_bass_kernel_spmd as _run

    nc = _bacc.Bacc("TRN2", target_bir_lowering=False, num_devices=1)
    arrays = laid_out({k: np.asarray(v) for k, v in inputs.items()})
    d = {}
    for name, a in arrays.items():
        d[name] = nc.dram_tensor(f"in_{name}", a.shape, mybir.dt.from_np(a.dtype), kind="ExternalInput").ap()
    out = nc.dram_tensor("out_0", (T, D), F32, kind="ExternalOutput").ap()
    tower(nc, d, out)
    r = _run(nc, [{f"in_{k}": a for k, a in arrays.items()}], core_ids=[0])
    return r.results[0]["out_0"].reshape(B, NP, D)
```
